# Optimizing a Trainium2 kernel written in Bass

```python
import numpy as np
import jax
import jax.numpy as jnp

def _softmax(x, axis=-1):
    return jax.nn.softmax(x, axis=axis)

def _gelu(x):
    return jax.nn.gelu(x, approximate=True)

def _silu(x):
    return jax.nn.silu(x)

def _sigmoid(x):
    return jax.nn.sigmoid(x)

def _layernorm(x, axis=-1, eps=1e-05):
    m = jnp.mean(x, axis=axis, keepdims=True)
    v = jnp.var(x, axis=axis, keepdims=True)
    return (x - m) / jnp.sqrt(v + eps)

def _scatter_add(tgt, idx, src, axis=0):
    return tgt.at[idx].add(src)

def _segment_sum(src, seg, n):
    return jax.ops.segment_sum(src, seg, n)
kernel_name = 'mk_decoder_postln_d2_seqx_r8_32191b'

def setup_inputs(seed: int=0):
    np.random.seed(seed)
    _w = jnp.asarray

    def _rec_inputs():
        import jax
        import jax.numpy as jnp
        _rk = jax.random.key(seed)
        x = 7.22e-05 + 1 * jax.random.normal(jax.random.fold_in(_rk, 1), (32, 128, 128), jnp.float32)
        _lenS = 128 - jax.random.randint(jax.random.fold_in(_rk, 7), (32,), 0, max(1, 128 // 4) + 1, jnp.int32)
        _lenS2 = 128 - jax.random.randint(jax.random.fold_in(_rk, 8), (32,), 0, max(1, 128 // 4) + 1, jnp.int32)
        _ctx_1024P = jax.random.normal(jax.random.fold_in(_rk, 11), (32, 16, 128), jnp.float32)
        _ctx_1024c = jax.random.dirichlet(jax.random.fold_in(_rk, 511), 0.3 * jnp.ones((16,), jnp.float32), (32, 128))
        _ctx_1024t = jnp.einsum('bsk,bkd->bsd', _ctx_1024c, _ctx_1024P)
        _ctx_1024t = _ctx_1024t * jax.lax.rsqrt(jnp.mean(jnp.square(_ctx_1024t)) + 1e-12) * 0.953939
        ctx_1024 = 4.13588e-05 + 0.999923 * (_ctx_1024t + 0.3 * jax.random.normal(jax.random.fold_in(_rk, 611), (32, 128, 128), jnp.float32))
        return (x, ctx_1024)
    x, ctx_1024 = _rec_inputs()

    def _L0_attn_setup():
        import jax, jax.numpy as jnp
        import numpy as np
        D_MODEL = 128
        NUM_HEADS = 16
        OMEGA_0 = 30.0
        D_K = D_MODEL // NUM_HEADS

        def _siren_uniform(key, shape, fan_in, omega_0=OMEGA_0):
            bound = np.sqrt(6.0 / fan_in) / omega_0
            return jax.random.uniform(key, shape, minval=-bound, maxval=bound, dtype=jnp.float32)
        key = jax.random.key(seed)
        ks = jax.random.split(key, 9)
        B, S = (2, 256)
        x = jax.random.normal(ks[0], (B, S, D_MODEL), dtype=jnp.float32)
        Wq = _siren_uniform(ks[1], (D_MODEL, D_MODEL), D_MODEL)
        bq = _siren_uniform(ks[2], (D_MODEL,), D_MODEL)
        Wk = _siren_uniform(ks[3], (D_MODEL, D_MODEL), D_MODEL)
        bk = _siren_uniform(ks[4], (D_MODEL,), D_MODEL)
        Wv = _siren_uniform(ks[5], (D_MODEL, D_MODEL), D_MODEL)
        bv = _siren_uniform(ks[6], (D_MODEL,), D_MODEL)
        Wo = _siren_uniform(ks[7], (D_MODEL, D_MODEL), D_MODEL)
        bo = _siren_uniform(ks[8], (D_MODEL,), D_MODEL)
        return {'x': x, 'Wq': Wq, 'bq': bq, 'Wk': Wk, 'bk': bk, 'Wv': Wv, 'bv': bv, 'Wo': Wo, 'bo': bo}
    _L0_attn_all = _L0_attn_setup()
    _L0_attn_in = {k: v for k, v in _L0_attn_all.items() if k in ('Wq', 'bq', 'Wk', 'bk', 'Wv', 'bv', 'Wo', 'bo')}
    del _L0_attn_all

    def _L0_xattn_setup():
        import jax, jax.numpy as jnp
        import numpy as np
        D_MODEL = 128
        NUM_HEADS = 16
        HEAD_DIM = D_MODEL // NUM_HEADS
        MAX_SEQ = 64

        def rope_tables(seq_len, dim):
            inv_freq = 1.0 / 10000.0 ** (jnp.arange(0, dim, 2, dtype=jnp.float32) / dim)
            t = jnp.arange(seq_len, dtype=jnp.float32)
            freqs = jnp.einsum('i,j->ij', t, inv_freq)
            emb = jnp.concatenate([freqs, freqs], axis=-1)
            return (jnp.cos(emb), jnp.sin(emb))

        def rotate_half(x):
            x1, x2 = jnp.split(x, 2, axis=-1)
            return jnp.concatenate([-x2, x1], axis=-1)
        key = jax.random.key(seed)
        ks = jax.random.split(key, 12)
        B, S, D = (16, 64, D_MODEL)
        s = 1.0 / np.sqrt(D)
        inp = {'query': jax.random.normal(ks[0], (B, S, D), jnp.float32), 'key': jax.random.normal(ks[1], (B, S, D), jnp.float32), 'value': jax.random.normal(ks[2], (B, S, D), jnp.float32), 'Wq': jax.random.normal(ks[3], (D, D), jnp.float32) * s, 'bq': jnp.zeros((D,), jnp.float32), 'Wk': jax.random.normal(ks[4], (D, D), jnp.float32) * s, 'bk': jnp.zeros((D,), jnp.float32), 'Wv': jax.random.normal(ks[5], (D, D), jnp.float32) * s, 'bv': jnp.zeros((D,), jnp.float32), 'Wo': jax.random.normal(ks[6], (D, D), jnp.float32) * s, 'bo': jnp.zeros((D,), jnp.float32)}
        return inp
    _L0_xattn_all = _L0_xattn_setup()
    _L0_xattn_in = {k: v for k, v in _L0_xattn_all.items() if k in ('Wq', 'bq', 'Wk', 'bk', 'Wv', 'bv', 'Wo', 'bo')}
    del _L0_xattn_all

    def _L0_ffn_setup():
        import jax, jax.numpy as jnp
        import numpy as np
        H, I, E_ROUTED, TOP_K = (128, 352, 7, 2)
        B, S = (4, 256)

        def _expert(h, g, u, d):
            return jnp.einsum('...i,hi->...h', jax.nn.silu(h @ g.T) * (h @ u.T), d)
        key = jax.random.key(seed)
        ks = jax.random.split(key, 10)
        sc = 0.02
        return {'x': jax.random.normal(ks[0], (B, S, H), dtype=jnp.float32), 'sg': jax.random.normal(ks[1], (I, H), dtype=jnp.float32) * sc, 'su': jax.random.normal(ks[2], (I, H), dtype=jnp.float32) * sc, 'sd': jax.random.normal(ks[3], (H, I), dtype=jnp.float32) * sc, 'rg': jax.random.normal(ks[4], (E_ROUTED, I, H), dtype=jnp.float32) * sc, 'ru': jax.random.normal(ks[5], (E_ROUTED, I, H), dtype=jnp.float32) * sc, 'rd': jax.random.normal(ks[6], (E_ROUTED, H, I), dtype=jnp.float32) * sc, 'wr': jax.random.normal(ks[7], (E_ROUTED, H), dtype=jnp.float32) * sc, 'rb': jnp.zeros((E_ROUTED,), dtype=jnp.float32)}
    _L0_ffn_all = _L0_ffn_setup()
    _L0_ffn_in = {k: v for k, v in _L0_ffn_all.items() if k in ('sg', 'su', 'sd', 'rg', 'ru', 'rd', 'wr', 'rb')}
    del _L0_ffn_all

    def _L1_attn_setup():
        import jax, jax.numpy as jnp
        import numpy as np
        B, T, C = (2, 256, 128)
        LAT = 32
        N_HEAD = 16
        HEAD_DIM = C // N_HEAD
        SCALE = 1.0 / np.sqrt(HEAD_DIM).astype(np.float32)
        key = jax.random.key(seed)
        ks = jax.random.split(key, 9)
        s_in = 0.02
        return {'x': jax.random.normal(ks[0], (B, T, C), dtype=jnp.float32), 'wq_lat': jax.random.normal(ks[1], (C, LAT), dtype=jnp.float32) * s_in, 'wk_lat': jax.random.normal(ks[2], (C, LAT), dtype=jnp.float32) * s_in, 'wv_lat': jax.random.normal(ks[3], (C, LAT), dtype=jnp.float32) * s_in, 'wq_heads': jax.random.normal(ks[4], (LAT, C), dtype=jnp.float32) * s_in, 'wk_heads': jax.random.normal(ks[5], (LAT, C), dtype=jnp.float32) * s_in, 'wv_heads': jax.random.normal(ks[6], (LAT, C), dtype=jnp.float32) * s_in, 'w_proj': jax.random.normal(ks[7], (C, C), dtype=jnp.float32) * s_in, 'b_proj': jnp.zeros((C,), dtype=jnp.float32)}
    _L1_attn_all = _L1_attn_setup()
    _L1_attn_in = {k: v for k, v in _L1_attn_all.items() if k in ('wq_lat', 'wk_lat', 'wv_lat', 'wq_heads', 'wk_heads', 'wv_heads', 'w_proj', 'b_proj')}
    del _L1_attn_all

    def _L1_xattn_setup():
        import jax, jax.numpy as jnp
        import numpy as np
        N_HEADS = 4
        IN_FEATURES = 128

        def _channel_attention(qm, km, vm, scale):
            b, n, c = qm.shape
            d = c // N_HEADS
            qh = qm.reshape(b, n, N_HEADS, d).transpose(0, 2, 3, 1)
            kh = km.reshape(b, n, N_HEADS, d).transpose(0, 2, 3, 1)
            vh = vm.reshape(b, n, N_HEADS, d).transpose(0, 2, 3, 1)
            scores = jnp.einsum('bhdn,bhen->bhde', qh, kh) * scale
            attn = jax.nn.softmax(scores, axis=-1)
            out = jnp.einsum('bhde,bhen->bhdn', attn, vh)
            return out.transpose(0, 3, 1, 2).reshape(b, n, c)
        key = jax.random.key(seed)
        ks = jax.random.split(key, 20)
        B, HW, C = (2, 2048, 128)
        inp = {'q': jax.random.normal(ks[0], (B, HW, C), dtype=jnp.float32), 'k': jax.random.normal(ks[1], (B, HW, C), dtype=jnp.float32), 'v': jax.random.normal(ks[2], (B, HW, C), dtype=jnp.float32)}
        names = ['wqg', 'bqg', 'wkg', 'bkg', 'wvg', 'bvg', 'wql', 'bql', 'wkl', 'bkl', 'wvl', 'bvl', 'wp', 'bp']
        for i, n in enumerate(names):
            inp[n] = jax.random.normal(ks[3 + i], (C,), dtype=jnp.float32)
        return inp
    _L1_xattn_all = _L1_xattn_setup()
    _L1_xattn_in = {k: v for k, v in _L1_xattn_all.items() if k in ('wqg', 'bqg', 'wkg', 'bkg', 'wvg', 'bvg', 'wql', 'bql', 'wkl', 'bkl', 'wvl', 'bvl', 'wp', 'bp')}
    del _L1_xattn_all

    def _L1_ffn_setup():
        import jax, jax.numpy as jnp
        import numpy as np
        HIDDEN = 128
        FFN = 512
        NUM_EXPERTS = 8
        TOP_K = 2
        BATCH, SEQ = (2, 256)
        key = jax.random.key(seed)
        ks = jax.random.split(key, 6)
        s_h = 1.0 / np.sqrt(HIDDEN)
        s_f = 1.0 / np.sqrt(FFN)
        return {'hidden_states': jax.random.normal(ks[0], (BATCH, SEQ, HIDDEN), jnp.float32), 'gate_w': jax.random.uniform(ks[1], (HIDDEN, NUM_EXPERTS), jnp.float32, -s_h, s_h), 'gate_b': jax.random.uniform(ks[2], (NUM_EXPERTS,), jnp.float32, -s_h, s_h), 'w1': jax.random.uniform(ks[3], (NUM_EXPERTS, HIDDEN, FFN), jnp.float32, -s_h, s_h), 'w3': jax.random.uniform(ks[4], (NUM_EXPERTS, HIDDEN, FFN), jnp.float32, -s_h, s_h), 'w2': jax.random.uniform(ks[5], (NUM_EXPERTS, FFN, HIDDEN), jnp.float32, -s_f, s_f)}
    _L1_ffn_all = _L1_ffn_setup()
    _L1_ffn_in = {k: v for k, v in _L1_ffn_all.items() if k in ('gate_w', 'gate_b', 'w1', 'w3', 'w2')}
    del _L1_ffn_all
    return {'x': x, 'ctx_1024': ctx_1024, 'L0_attn_Wq': _L0_attn_in['Wq'], 'L0_attn_bq': _L0_attn_in['bq'], 'L0_attn_Wk': _L0_attn_in['Wk'], 'L0_attn_bk': _L0_attn_in['bk'], 'L0_attn_Wv': _L0_attn_in['Wv'], 'L0_attn_bv': _L0_attn_in['bv'], 'L0_attn_Wo': _L0_attn_in['Wo'], 'L0_attn_bo': _L0_attn_in['bo'], 'L0_xattn_Wq': _L0_xattn_in['Wq'], 'L0_xattn_bq': _L0_xattn_in['bq'], 'L0_xattn_Wk': _L0_xattn_in['Wk'], 'L0_xattn_bk': _L0_xattn_in['bk'], 'L0_xattn_Wv': _L0_xattn_in['Wv'], 'L0_xattn_bv': _L0_xattn_in['bv'], 'L0_xattn_Wo': _L0_xattn_in['Wo'], 'L0_xattn_bo': _L0_xattn_in['bo'], 'L0_ffn_sg': _L0_ffn_in['sg'], 'L0_ffn_su': _L0_ffn_in['su'], 'L0_ffn_sd': _L0_ffn_in['sd'], 'L0_ffn_rg': _L0_ffn_in['rg'], 'L0_ffn_ru': _L0_ffn_in['ru'], 'L0_ffn_rd': _L0_ffn_in['rd'], 'L0_ffn_wr': _L0_ffn_in['wr'], 'L0_ffn_rb': _L0_ffn_in['rb'], 'L1_attn_wq_lat': _L1_attn_in['wq_lat'], 'L1_attn_wk_lat': _L1_attn_in['wk_lat'], 'L1_attn_wv_lat': _L1_attn_in['wv_lat'], 'L1_attn_wq_heads': _L1_attn_in['wq_heads'], 'L1_attn_wk_heads': _L1_attn_in['wk_heads'], 'L1_attn_wv_heads': _L1_attn_in['wv_heads'], 'L1_attn_w_proj': _L1_attn_in['w_proj'], 'L1_attn_b_proj': _L1_attn_in['b_proj'], 'L1_xattn_wqg': _L1_xattn_in['wqg'], 'L1_xattn_bqg': _L1_xattn_in['bqg'], 'L1_xattn_wkg': _L1_xattn_in['wkg'], 'L1_xattn_bkg': _L1_xattn_in['bkg'], 'L1_xattn_wvg': _L1_xattn_in['wvg'], 'L1_xattn_bvg': _L1_xattn_in['bvg'], 'L1_xattn_wql': _L1_xattn_in['wql'], 'L1_xattn_bql': _L1_xattn_in['bql'], 'L1_xattn_wkl': _L1_xattn_in['wkl'], 'L1_xattn_bkl': _L1_xattn_in['bkl'], 'L1_xattn_wvl': _L1_xattn_in['wvl'], 'L1_xattn_bvl': _L1_xattn_in['bvl'], 'L1_xattn_wp': _L1_xattn_in['wp'], 'L1_xattn_bp': _L1_xattn_in['bp'], 'L1_ffn_gate_w': _L1_ffn_in['gate_w'], 'L1_ffn_gate_b': _L1_ffn_in['gate_b'], 'L1_ffn_w1': _L1_ffn_in['w1'], 'L1_ffn_w3': _L1_ffn_in['w3'], 'L1_ffn_w2': _L1_ffn_in['w2']}

def reference(x, ctx_1024, L0_attn_Wq, L0_attn_bq, L0_attn_Wk, L0_attn_bk, L0_attn_Wv, L0_attn_bv, L0_attn_Wo, L0_attn_bo, L0_xattn_Wq, L0_xattn_bq, L0_xattn_Wk, L0_xattn_bk, L0_xattn_Wv, L0_xattn_bv, L0_xattn_Wo, L0_xattn_bo, L0_ffn_sg, L0_ffn_su, L0_ffn_sd, L0_ffn_rg, L0_ffn_ru, L0_ffn_rd, L0_ffn_wr, L0_ffn_rb, L1_attn_wq_lat, L1_attn_wk_lat, L1_attn_wv_lat, L1_attn_wq_heads, L1_attn_wk_heads, L1_attn_wv_heads, L1_attn_w_proj, L1_attn_b_proj, L1_xattn_wqg, L1_xattn_bqg, L1_xattn_wkg, L1_xattn_bkg, L1_xattn_wvg, L1_xattn_bvg, L1_xattn_wql, L1_xattn_bql, L1_xattn_wkl, L1_xattn_bkl, L1_xattn_wvl, L1_xattn_bvl, L1_xattn_wp, L1_xattn_bp, L1_ffn_gate_w, L1_ffn_gate_b, L1_ffn_w1, L1_ffn_w3, L1_ffn_w2):
    import jax
    import jax.numpy as jnp

    def _L0_attn_ref(x, Wq, bq, Wk, bk, Wv, bv, Wo, bo):
        import jax, jax.numpy as jnp
        import numpy as np
        D_MODEL = 128
        NUM_HEADS = 16
        OMEGA_0 = 30.0
        D_K = D_MODEL // NUM_HEADS

        def _siren_uniform(key, shape, fan_in, omega_0=OMEGA_0):
            bound = np.sqrt(6.0 / fan_in) / omega_0
            return jax.random.uniform(key, shape, minval=-bound, maxval=bound, dtype=jnp.float32)
        B, S, _ = x.shape
        scale = np.sqrt(D_K).astype(np.float32)

        def proj(W, b):
            y = jnp.einsum('bsd,ed->bse', x, W) + b
            return y.reshape(B, S, NUM_HEADS, D_K).transpose(0, 2, 1, 3)
        Q = proj(Wq, bq)
        K = proj(Wk, bk)
        V = proj(Wv, bv)
        logits = jnp.einsum('bhqd,bhkd->bhqk', Q, K) / scale
        attn = jnp.sin(OMEGA_0 * logits)
        out = jnp.einsum('bhqk,bhkd->bhqd', attn, V)
        out = out.transpose(0, 2, 1, 3).reshape(B, S, D_MODEL)
        return jnp.einsum('bsd,ed->bse', out, Wo) + bo

    def _L0_xattn_ref(query, key, value, Wq, bq, Wk, bk, Wv, bv, Wo, bo):
        import jax, jax.numpy as jnp
        import numpy as np
        D_MODEL = 128
        NUM_HEADS = 16
        HEAD_DIM = D_MODEL // NUM_HEADS
        MAX_SEQ = 64

        def rope_tables(seq_len, dim):
            inv_freq = 1.0 / 10000.0 ** (jnp.arange(0, dim, 2, dtype=jnp.float32) / dim)
            t = jnp.arange(seq_len, dtype=jnp.float32)
            freqs = jnp.einsum('i,j->ij', t, inv_freq)
            emb = jnp.concatenate([freqs, freqs], axis=-1)
            return (jnp.cos(emb), jnp.sin(emb))

        def rotate_half(x):
            x1, x2 = jnp.split(x, 2, axis=-1)
            return jnp.concatenate([-x2, x1], axis=-1)
        B, S, D = query.shape
        H, Hd = (NUM_HEADS, HEAD_DIM)
        scale = Hd ** (-0.5)

        def proj(x, W, b):
            y = jnp.einsum('bsd,ed->bse', x, W) + b
            return y.reshape(B, S, H, Hd).transpose(0, 2, 1, 3)
        q = proj(query, Wq, bq)
        k = proj(key, Wk, bk)
        v = proj(value, Wv, bv)
        cos, sin = rope_tables(S, Hd)
        cos = cos[None, None]
        sin = sin[None, None]
        q = q * cos + rotate_half(q) * sin
        k = k * cos + rotate_half(k) * sin
        attn = jnp.einsum('bhqd,bhkd->bhqk', q, k) * scale
        attn_w = jax.nn.softmax(attn, axis=-1)
        out = jnp.einsum('bhqk,bhkd->bhqd', attn_w, v)
        out = out.transpose(0, 2, 1, 3).reshape(B, S, D)
        out = jnp.einsum('bsd,ed->bse', out, Wo) + bo
        return out

    def _L0_ffn_ref(x, sg, su, sd, rg, ru, rd, wr, rb):
        import jax, jax.numpy as jnp
        import numpy as np
        H, I, E_ROUTED, TOP_K = (128, 352, 7, 2)
        B, S = (4, 256)

        def _expert(h, g, u, d):
            return jnp.einsum('...i,hi->...h', jax.nn.silu(h @ g.T) * (h @ u.T), d)
        shared_out = _expert(x, sg, su, sd)
        logits = x @ wr.T + rb
        probs = jax.nn.softmax(logits, axis=-1)
        scores, idx = jax.lax.top_k(probs, TOP_K)
        scores = scores / scores.sum(axis=-1, keepdims=True)
        w = jnp.sum(scores[..., None] * jax.nn.one_hot(idx, E_ROUTED, dtype=x.dtype), axis=-2)
        out = shared_out
        for e in range(E_ROUTED):
            out = out + w[..., e:e + 1] * _expert(x, rg[e], ru[e], rd[e])
        return out

    def _L1_attn_ref(x, wq_lat, wk_lat, wv_lat, wq_heads, wk_heads, wv_heads, w_proj, b_proj):
        import jax, jax.numpy as jnp
        import numpy as np
        B, T, C = (2, 256, 128)
        LAT = 32
        N_HEAD = 16
        HEAD_DIM = C // N_HEAD
        SCALE = 1.0 / np.sqrt(HEAD_DIM).astype(np.float32)
        Bx, Tx, Cx = x.shape
        q = x @ wq_lat @ wq_heads
        k = x @ wk_lat @ wk_heads
        v = x @ wv_lat @ wv_heads
        q = q.reshape(Bx, Tx, N_HEAD, HEAD_DIM).transpose(0, 2, 1, 3)
        k = k.reshape(Bx, Tx, N_HEAD, HEAD_DIM).transpose(0, 2, 1, 3)
        v = v.reshape(Bx, Tx, N_HEAD, HEAD_DIM).transpose(0, 2, 1, 3)
        att = jnp.einsum('bhqd,bhkd->bhqk', q, k) * SCALE
        causal = jnp.tril(jnp.ones((Tx, Tx), dtype=bool))
        att = jnp.where(causal[None, None], att, -jnp.inf)
        att = jax.nn.softmax(att, axis=-1)
        y = jnp.einsum('bhqk,bhkd->bhqd', att, v)
        y = y.transpose(0, 2, 1, 3).reshape(Bx, Tx, Cx)
        return y @ w_proj + b_proj

    def _L1_xattn_ref(q, k, v, wqg, bqg, wkg, bkg, wvg, bvg, wql, bql, wkl, bkl, wvl, bvl, wp, bp):
        import jax, jax.numpy as jnp
        import numpy as np
        N_HEADS = 4
        IN_FEATURES = 128

        def _channel_attention(qm, km, vm, scale):
            b, n, c = qm.shape
            d = c // N_HEADS
            qh = qm.reshape(b, n, N_HEADS, d).transpose(0, 2, 3, 1)
            kh = km.reshape(b, n, N_HEADS, d).transpose(0, 2, 3, 1)
            vh = vm.reshape(b, n, N_HEADS, d).transpose(0, 2, 3, 1)
            scores = jnp.einsum('bhdn,bhen->bhde', qh, kh) * scale
            attn = jax.nn.softmax(scores, axis=-1)
            out = jnp.einsum('bhde,bhen->bhdn', attn, vh)
            return out.transpose(0, 3, 1, 2).reshape(b, n, c)
        scale = IN_FEATURES ** (-0.5)
        att_global = _channel_attention(q * wqg + bqg, k * wkg + bkg, v * wvg + bvg, scale)
        att_local = _channel_attention(q * wql + bql, k * wkl + bkl, v * wvl + bvl, scale)
        att = att_global + att_local
        return 2.0 * att * wp + bp

    def _L1_ffn_ref(hidden_states, gate_w, gate_b, w1, w3, w2):
        import jax, jax.numpy as jnp
        import numpy as np
        HIDDEN = 128
        FFN = 512
        NUM_EXPERTS = 8
        TOP_K = 2
        BATCH, SEQ = (2, 256)
        B, S, D = hidden_states.shape
        T = B * S
        x = hidden_states.reshape(T, D)
        logits = x @ gate_w + gate_b
        probs = jax.nn.softmax(logits.astype(jnp.float32), axis=-1)
        top_w, top_idx = jax.lax.top_k(probs, TOP_K)
        top_w = top_w / jnp.sum(top_w, axis=-1, keepdims=True)
        combine = jnp.zeros((T, NUM_EXPERTS), jnp.float32)
        combine = combine.at[jnp.arange(T)[:, None], top_idx].set(top_w)
        combine = combine.astype(x.dtype)
        h = jax.nn.silu(jnp.einsum('td,edf->tef', x, w1)) * jnp.einsum('td,edf->tef', x, w3)
        out_e = jnp.einsum('tef,efd->ted', h, w2)
        out = jnp.einsum('ted,te->td', out_e, combine)
        return out.reshape(B, S, D)
    x = _layernorm(x + _L0_attn_ref(x, L0_attn_Wq, L0_attn_bq, L0_attn_Wk, L0_attn_bk, L0_attn_Wv, L0_attn_bv, L0_attn_Wo, L0_attn_bo), axis=-1)
    x = _layernorm(x + _L0_xattn_ref(x, ctx_1024, ctx_1024, L0_xattn_Wq, L0_xattn_bq, L0_xattn_Wk, L0_xattn_bk, L0_xattn_Wv, L0_xattn_bv, L0_xattn_Wo, L0_xattn_bo), axis=-1)
    x = _layernorm(x + _L0_ffn_ref(x, L0_ffn_sg, L0_ffn_su, L0_ffn_sd, L0_ffn_rg, L0_ffn_ru, L0_ffn_rd, L0_ffn_wr, L0_ffn_rb), axis=-1)
    x = _layernorm(x + _L1_attn_ref(x, L1_attn_wq_lat, L1_attn_wk_lat, L1_attn_wv_lat, L1_attn_wq_heads, L1_attn_wk_heads, L1_attn_wv_heads, L1_attn_w_proj, L1_attn_b_proj), axis=-1)
    x = _layernorm(x + _L1_xattn_ref(x, ctx_1024, ctx_1024, L1_xattn_wqg, L1_xattn_bqg, L1_xattn_wkg, L1_xattn_bkg, L1_xattn_wvg, L1_xattn_bvg, L1_xattn_wql, L1_xattn_bql, L1_xattn_wkl, L1_xattn_bkl, L1_xattn_wvl, L1_xattn_bvl, L1_xattn_wp, L1_xattn_bp), axis=-1)
    x = _layernorm(x + _L1_ffn_ref(x, L1_ffn_gate_w, L1_ffn_gate_b, L1_ffn_w1, L1_ffn_w3, L1_ffn_w2), axis=-1)
    return x

_drawn_inputs = setup_inputs


def setup_inputs(seed=0):
    import zlib

    import numpy as np

    out = dict(_drawn_inputs(seed))
    spreads = {'L0_xattn_bq': (0.0, 0.305),
     'L0_xattn_bk': (0.0, 0.8),
     'L0_xattn_bv': (0.0, 0.1),
     'L0_xattn_bo': (0.0, 0.1),
     'L0_ffn_rb': (0.0, 0.8),
     'L1_attn_b_proj': (0.0, 0.1)}
    factors = {'L0_attn_Wq': 8.0,
     'L0_attn_bq': 8.0,
     'L0_attn_Wk': 8.0,
     'L0_attn_bk': 8.0,
     'L0_attn_Wv': 8.0,
     'L0_attn_bv': 8.0,
     'L0_attn_Wo': 8.0,
     'L0_attn_bo': 6.219,
     'L0_ffn_sg': 7.54,
     'L0_ffn_su': 7.819,
     'L0_ffn_sd': 6.885,
     'L0_ffn_rg': 8.0,
     'L0_ffn_ru': 8.0,
     'L0_ffn_rd': 8.0,
     'L0_ffn_wr': 8.0,
     'L1_attn_wq_lat': 8.0,
     'L1_attn_wk_lat': 8.0,
     'L1_attn_wv_lat': 8.0,
     'L1_attn_wq_heads': 8.0,
     'L1_attn_wk_heads': 8.0,
     'L1_attn_wv_heads': 7.439,
     'L1_attn_w_proj': 6.748,
     'L1_ffn_gate_b': 2.909}
    for name, (base, spread) in spreads.items():
        noise = np.random.default_rng([zlib.crc32(name.encode()), seed]).standard_normal(out[name].shape)
        drawn = base * np.exp(spread * noise) if base else spread * noise
        out[name] = jnp.asarray(drawn.astype(out[name].dtype))
    for name, factor in factors.items():
        out[name] = (out[name] * factor).astype(out[name].dtype)
    return out
```

```python
from contextlib import ExitStack

import numpy as np

import concourse.bass as bass
from concourse import mybir

F32 = mybir.dt.float32
F32R = mybir.dt.float32r
BF16 = mybir.dt.bfloat16
I32 = mybir.dt.int32
ALU = mybir.AluOpType
ACT = mybir.ActivationFunctionType
AX = mybir.AxisListType

P = 128
NB = 32
NPAIR = NB // 2
H, HD = 16, 8
G, J = 4, 4
VW = 64
EPS = 1e-5
NEG = -1e30
MAGIC = 12582912.0
E0, I0 = 7, 352
E1, I1 = 8, 512
CH0 = [(0, 128), (128, 128), (256, 96)]
W0 = 384
LAT = 32
CONST = {}
_at = 0
for _n, _w in (("ident", 128), ("rot", 128), ("cos", 256), ("sin", 256), ("sumrep", 128),
               ("before", 128), ("ones", 128), ("causal_qk", 128), ("causal_kq", 128),
               ("blocks", 128), ("mask", 4), ("maskc", 4), ("tile0", 80), ("eidx", 8)):
    CONST[_n] = (_at, _w)
    _at += _w
NCONST = _at


def constants():
    c = {n: np.zeros((P, w), np.float32) for n, (_, w) in CONST.items()}
    p = np.arange(P)
    c["ident"][p, p] = 1
    for e in range(P):
        lo = e % HD < HD // 2
        c["rot"][e + 4 if lo else e - 4, e] = -1 if lo else 1
    inv = (1.0 / np.float32(10000.0) ** (np.arange(0, HD, 2, dtype=np.float32) / HD)).astype(np.float32)
    ang = np.arange(P, dtype=np.float32)[None, :] * inv[p % (HD // 2)][:, None]
    c["cos"][:] = np.tile(np.cos(ang), (1, 2))
    c["sin"][:] = np.tile(np.sin(ang), (1, 2))
    for a in range(2):
        for j in range(J):
            c["sumrep"][64 * a + 32 + j, 64 * a + 8 * j:64 * a + 8 * j + 8] = 1
        c["sumrep"][64 * a + 32, 64 * a + 32:64 * a + 64] = 1
    c["before"][:] = p[:, None] < p[None, :]
    c["ones"][:] = 1
    c["causal_qk"][:] = np.where(p[None, :] > p[:, None], NEG, 0)
    c["causal_kq"][:] = c["causal_qk"].T
    c["blocks"][:] = np.where(p[None, :] // 32 != p[:, None] // 32, NEG, 0)
    c["mask"][:] = (p[:, None] % 32) // HD == np.arange(J)
    c["maskc"][:] = c["mask"] * np.float32(30.0 / (np.sqrt(8.0) * 2 * np.pi))
    c["tile0"][:] = 128 * np.arange(80)
    c["eidx"][:] = np.arange(8)
    return np.concatenate([c[n] for n in CONST], axis=1)


class Core:

    def __init__(self, nc, ctx, dram):
        self.nc, self.ctx, self.dram = nc, ctx, dram
        sb = self.sb
        self.const = sb("const", [P, NCONST])
        self.ident_bf = sb("ident_bf", [P, P], BF16)
        self.ones_bf = sb("ones_bf", [P, P], BF16)
        self.before_bf = sb("before_bf", [P, P], BF16)
        self.causal_qk_bf = sb("causal_qk_bf", [P, P], BF16)
        self.causal_kq_bf = sb("causal_kq_bf", [P, P], BF16)
        self.blocks_bf = sb("blocks_bf", [P, P], BF16)
        self.ones_r = sb("ones_r", [P, P], F32R)
        self.x = sb("x_state", [P, NB, P])
        self.w_sin = sb("w_sin", [P, 5, P])
        self.w_rope = sb("w_rope", [P, 7, P])
        self.w_lat = sb("w_lat", [P, 3 * LAT])
        self.w_heads = sb("w_heads", [P, 3, P])
        self.w_proj = sb("w_proj", [P, 2, P])
        self.bias_col = sb("bias_col", [P, 8])
        self.bias_row = sb("bias_row", [P, 5, P])
        self.wr0 = sb("wr0", [P, E0])
        self.rb0 = sb("rb0", [P, E0])
        self.gate_w = sb("gate_w", [P, E1])
        self.gate_b = sb("gate_b", [P, E1])
        self.gu0 = sb("gu0", [P, E0 + 1, 2 * W0])
        self.dn0 = sb("dn0", [P, E0 + 1, 3, P])
        self.gu1 = sb("gu1", [P, E1, 2 * I1])
        self.dn1 = sb("dn1", [P, E1, 4, P])
        self.ch_row = sb("ch_row", [P, 9, P])
        self.ch_col = sb("ch_col", [P, 5])
        self.loaded_channel = self.sem("loaded_channel")
        self.loaded_ffn1 = self.sem("loaded_ffn1")

    def sb(self, name, shape, dt=F32):
        return self.ctx.enter_context(self.nc.sbuf_tensor(name, shape, dt))

    def sem(self, name):
        return self.nc.alloc_semaphore(name)

    def c(self, name, a=0, b=None):
        at, w = CONST[name]
        return self.const[:, at + a:at + (w if b is None else b)]


BQ0, BK0, BQ1, BK1, BQ1R, BK1R = range(6)
BV0, BO0, BV1, BO1, BPROJ = range(5)
CH_ROWS = ["wqg", "wql", "bqg", "bql", "wkg", "wkl", "bkg", "bkl", "bp"]
WQ, BQ, WK, BK, BP = 0, 2, 4, 6, 8
CH_COLS = ["wvg", "wvl", "bvg", "bvl", "wp"]
WV, BV, WP = 0, 2, 4
N_CHANNEL = 16 * (len(CH_ROWS) + len(CH_COLS))
N_FFN1 = 16 * 3 * E1


def setup(k, d):
    nc = k.nc
    with ExitStack() as ctx:
        sb = lambda n, s, dt=F32: ctx.enter_context(nc.sbuf_tensor(n, s, dt))
        raw = sb("raw_attn", [P, 8, P])
        raw_gu = sb("raw_gu", [P, 2 * (E0 + 1), 3, P])
        raw_dn = sb("raw_dn", [P, E0 + 1, I0])
        raw_wr = sb("raw_wr", [E0, P])
        bank = [ctx.enter_context(nc.psum_tensor(f"turn{i}", [P, 512], F32)) for i in range(4)]
        loaded_attn = k.sem("loaded_attn")
        loaded_ffn = k.sem("loaded_ffn")
        cleared = k.sem("cleared")
        cast = k.sem("cast")
        turned = [k.sem(f"turned{i}") for i in range(4)]
        taken = [k.sem(f"taken{i}") for i in range(4)]
        attn_names = ["L0_attn_Wq", "L0_attn_Wk", "L0_attn_Wv", "L0_attn_Wo",
                      "L0_xattn_Wq", "L0_xattn_Wk", "L0_xattn_Wv", "L0_xattn_Wo"]
        cols = ["L0_attn_bq", "L0_attn_bk", "L0_xattn_bq", "L0_xattn_bk"]
        rows = ["L0_attn_bv", "L0_attn_bo", "L0_xattn_bv", "L0_xattn_bo", "L1_attn_b_proj"]
        n_attn, n_ffn = [0], [0]

        ident, rot = k.c("ident"), k.c("rot")

        def jobs():
            for base, dst, plan in ((0, k.w_sin, ((0, ident), (1, ident), (2, ident))),
                                    (4, k.w_rope, ((0, ident), (0, rot), (1, ident), (1, rot), (2, ident)))):
                for n0 in range(0, len(plan), 4):
                    part = plan[n0:n0 + 4]
                    yield ([(raw[:, base + m, :], by, (slice(0, P), slice(i * P, i * P + P)))
                            for i, (m, by) in enumerate(part)],
                           [((slice(0, P), slice(0, len(part) * P)),
                             dst[:, n0:n0 + len(part), :].rearrange("p a b -> p (a b)"))])
            for m, dst in ((3, k.w_sin[:, 3:5, :]), (7, k.w_rope[:, 5:7, :])):
                yield ([(raw[:, m, :], ident, (slice(0, P), slice(0, P)))],
                       [((slice(32 * g, 32 * g + 32), slice(0, P)), dst[64 * (g % 2):64 * (g % 2) + 32, g // 2, :])
                        for g in range(G)])
            yield ([(rot, k.bias_col[:, BQ1:BQ1 + 2], (slice(0, P), slice(0, 2))),
                    (raw_wr[:, :], ident[0:E0, 0:E0], (slice(0, P), slice(128, 128 + E0)))],
                   [((slice(0, P), slice(0, 2)), k.bias_col[:, BQ1R:BQ1R + 2]),
                    ((slice(0, P), slice(128, 128 + E0)), k.wr0[:, :])])
            for e in range(E0 + 1):
                for m in range(2):
                    yield ([(raw_gu[0:n, 2 * e + m, c, :], ident[0:n, 0:n], (slice(0, P), slice(a, a + n)))
                            for c, (a, n) in enumerate(CH0)],
                           [((slice(0, P), slice(0, I0)), k.gu0[:, e, m * W0:m * W0 + I0])])
                yield ([(raw_dn[:, e, a:a + n], ident, (slice(0, n), slice(c * P, c * P + P)))
                        for c, (a, n) in enumerate(CH0)],
                       [((slice(0, P), slice(0, 2 * P)), k.dn0[:, e, 0:2, :].rearrange("p a b -> p (a b)")),
                        ((slice(0, 96), slice(2 * P, 3 * P)), k.dn0[0:96, e, 2, :])])

        work = list(jobs())
        first_ffn = len(work) - 3 * (E0 + 1)
        block = ctx.enter_context(nc.Block())

        @block.sync
        def _(sp):
            sp.dma_start(k.const[:, :], d["const"]).then_inc(loaded_attn, 16)
            for m, n in enumerate(attn_names):
                sp.dma_start(raw[:, m, :], d[n]).then_inc(loaded_attn, 16)
            sp.dma_start(raw_wr[:, :], d["L0_ffn_wr"]).then_inc(loaded_attn, 16)
            n_attn[0] += 2 + len(attn_names)
            for m, n in enumerate(cols):
                sp.dma_start(k.bias_col[:, m:m + 1], d[n].rearrange("(p o) -> p o", o=1)).then_inc(loaded_attn, 16)
                n_attn[0] += 1
            for m, n in enumerate(rows):
                sp.dma_start(k.bias_row[:, m, :], d[n].rearrange("(o n) -> o n", o=1).partition_broadcast(P)
                             ).then_inc(loaded_attn, 16)
                n_attn[0] += 1
            for dst, n in ((k.rb0, "L0_ffn_rb"), (k.gate_b, "L1_ffn_gate_b")):
                sp.dma_start(dst[:, :], d[n].rearrange("(o n) -> o n", o=1).partition_broadcast(P)
                             ).then_inc(loaded_attn, 16)
                n_attn[0] += 1
            sp.dma_start(k.gate_w[:, :], d["L1_ffn_gate_w"]).then_inc(loaded_attn, 16)
            n_attn[0] += 1
            for m, n in enumerate(("L1_attn_wq_lat", "L1_attn_wk_lat", "L1_attn_wv_lat")):
                sp.dma_start(k.w_lat[:, m * LAT:(m + 1) * LAT], d[n]).then_inc(loaded_attn, 16)
                n_attn[0] += 1
            sp.wait_ge(cleared, 2)
            for m, n in enumerate(("L1_attn_wq_heads", "L1_attn_wk_heads", "L1_attn_wv_heads")):
                sp.dma_start(k.w_heads[m * LAT:(m + 1) * LAT, m, :], d[n]).then_inc(loaded_attn, 16)
                n_attn[0] += 1
            for g in range(G):
                sp.dma_start(k.w_proj[64 * (g % 2):64 * (g % 2) + 32, g // 2, :],
                             d["L1_attn_w_proj"][32 * g:32 * g + 32, :]).then_inc(loaded_attn, 16)
                n_attn[0] += 1
            for m, n in enumerate(CH_ROWS):
                sp.dma_start(k.ch_row[:, m, :], d["L1_xattn_" + n].rearrange("(o n) -> o n", o=1).partition_broadcast(P)
                             ).then_inc(k.loaded_channel, 16)
            for m, n in enumerate(CH_COLS):
                sp.dma_start(k.ch_col[:, m:m + 1], d["L1_xattn_" + n].rearrange("(p o) -> p o", o=1)
                             ).then_inc(k.loaded_channel, 16)
            for e in range(E1):
                sp.dma_start(k.gu1[:, e, 0:I1], d["L1_ffn_w1"][e, :, :]).then_inc(k.loaded_ffn1, 16)
                sp.dma_start(k.gu1[:, e, I1:], d["L1_ffn_w3"][e, :, :]).then_inc(k.loaded_ffn1, 16)
                sp.dma_start(k.dn1[:, e, :, :], d["L1_ffn_w2"][e, :, :].rearrange("(c p) h -> p c h", p=P)
                             ).then_inc(k.loaded_ffn1, 16)

        @block.scalar
        def _(act):
            for s, n in enumerate(("g", "u")):
                for e in range(E0):
                    act.dma_start(raw_gu[:, 2 * e + s, 0:2, :],
                                  d["L0_ffn_r" + n][e, 0:256, :].rearrange("(c p) h -> p c h", p=P)
                                  ).then_inc(loaded_ffn, 16)
                    act.dma_start(raw_gu[0:96, 2 * e + s, 2, :], d["L0_ffn_r" + n][e, 256:I0, :]).then_inc(loaded_ffn, 16)
                act.dma_start(raw_gu[:, 2 * E0 + s, 0:2, :],
                              d["L0_ffn_s" + n][0:256, :].rearrange("(c p) h -> p c h", p=P)).then_inc(loaded_ffn, 16)
                act.dma_start(raw_gu[0:96, 2 * E0 + s, 2, :], d["L0_ffn_s" + n][256:I0, :]).then_inc(loaded_ffn, 16)
                n_ffn[0] += 2 * (E0 + 1)
            act.dma_start(raw_dn[:, 0:E0, :], d["L0_ffn_rd"].rearrange("e h i -> h e i")).then_inc(loaded_ffn, 16)
            act.dma_start(raw_dn[:, E0, :], d["L0_ffn_sd"]).then_inc(loaded_ffn, 16)
            n_ffn[0] += 2
            act.wait_ge(cleared, 4)
            for n in range(1, len(work), 2):
                b = n % 4
                act.wait_ge(turned[b], n // 4 + 1)
                for i, (s, dst) in enumerate(work[n][1]):
                    ins = nc.scalar.copy(dst, bank[b][s[0], s[1]])
                ins.then_inc(taken[b], 1)

        @block.gpsimd
        def _(pool):
            nc.gpsimd.memset(k.w_heads[:, :, :], 0.0).then_inc(cleared, 1)
            nc.gpsimd.memset(k.w_proj[:, :, :], 0.0).then_inc(cleared, 1)
            nc.gpsimd.memset(k.w_sin[:, :, :], 0.0).then_inc(cleared, 1)
            nc.gpsimd.memset(k.w_rope[:, :, :], 0.0).then_inc(cleared, 1)
            nc.gpsimd.memset(k.gu0[:, :, I0:W0], 0.0).then_inc(cleared, 1)
            nc.gpsimd.memset(k.gu0[:, :, W0 + I0:], 0.0).then_inc(cleared, 1)
            pool.wait_ge(cleared, 6)
            nc.gpsimd.memset(k.dn0[96:P, :, 2, :], 0.0).then_inc(cleared, 1)

        @block.tensor
        def _(pe):
            pe.wait_ge(loaded_attn, 16 * n_attn[0])
            for n, (turns, _) in enumerate(work):
                b = n % 4
                if n == first_ffn:
                    pe.wait_ge(loaded_ffn, 16 * n_ffn[0])
                if n >= 4:
                    pe.wait_ge(taken[b], n // 4)
                for w, by, (r, c) in turns:
                    ins = nc.tensor.matmul(bank[b][r, c], w, by, start=True, stop=True)
                ins.then_inc(turned[b], 1)

        @block.vector
        def _(dve):
            dve.wait_ge(loaded_attn, 16 * n_attn[0])
            for dst, n in ((k.ident_bf, "ident"), (k.ones_bf, "ones"), (k.before_bf, "before"),
                           (k.causal_qk_bf, "causal_qk"), (k.causal_kq_bf, "causal_kq"),
                           (k.blocks_bf, "blocks"), (k.ones_r, "ones")):
                nc.vector.tensor_copy(dst[:, :], k.c(n)).then_inc(cast, 1)
            dve.wait_ge(cleared, 4)
            for n in range(0, len(work), 2):
                b = n % 4
                dve.wait_ge(turned[b], n // 4 + 1)
                for s, dst in work[n][1]:
                    ins = nc.vector.tensor_copy(dst, bank[b][s[0], s[1]])
                ins.then_inc(taken[b], 1)


def head_attention(k, kind, x_in, ctx_in):
    nc = k.nc
    softmax = kind != "sine"
    with ExitStack() as ctx:
        sb = lambda n, s, dt=F32: ctx.enter_context(nc.sbuf_tensor(f"{kind}_{n}", s, dt))
        ps = lambda n, s: ctx.enter_context(nc.psum_tensor(f"{kind}_{n}", s, F32))
        sem = lambda n: k.sem(f"{kind}_{n}")
        scores = [ps("scores0", [P, 1024]), ps("scores1", [P, 1024])]
        bank = {n: ps("bank" + n, [P, 512]) for n in "ABCD"}
        xin = sb("xin", [P, 2, P])
        cin = sb("cin", [P, 2, P]) if ctx_in is not None else None
        xres = sb("xres", [P, 2, P])
        xT = sb("xT", [P, 512])
        latT = sb("latT", [P, 256]) if kind == "causal" else None
        turn = [sb(f"turn{i}", [P, 256]) for i in range(6)] if kind == "rope" else None
        rnd = [sb(f"rnd{i}", [P, 1024]) for i in range(2)] if kind == "sine" else None
        q4 = sb("q4", [P, J, 256])
        kg = sb("kg", [P, G, 256])
        vb = [sb(f"vb{i}", [P, G, J, VW]) for i in range(2)]
        probs = [sb(f"probs{i}", [P, H * P]) for i in range(2)]
        if softmax:
            negmax = [sb(f"negmax{i}", [P, H]) for i in range(2)]
            negmaxT = [sb(f"negmaxT{i}", [H, P], F32R) for i in range(2)]
            shift = [sb(f"shift{i}", [P, H * P], F32R) for i in range(2)]
            osum = [sb(f"osum{i}", [P, 256]) for i in range(2)]
            recip = [sb(f"recip{i}", [P, 256]) for i in range(2)]
        onorm = [sb(f"onorm{i}", [P, 256]) for i in range(2)]
        z = sb("z", [P, 2, P])
        stats = sb("stats", [P, 2, 6])
        mv = sb("mv", [P, 2, 2])
        vare = sb("vare", [P, 2])
        rstd = sb("rstd", [P, 2])
        mhalf = sb("mhalf", [P, 2])
        warm = sb("warm", [P, 5])
        one = sb("one", [P, 3])


        before_loop = {"A": ["lat"] * (kind == "causal") + ["q"], "B": ["k"], "C": ["xT", "v"], "D": []}
        in_loop = {"A": (["m00", "m02", "m10", "m12"] if softmax else []) + before_loop["A"],
                   "B": (["m01", "m03", "m11", "m13"] if softmax else []) + ["k"],
                   "C": ["xT"] + (["nm0", "nm1"] if softmax else []) + ["v", "y0", "y1"],
                   "D": ["pv0", "sum0", "pv1", "sum1"] if softmax else ["pv0", "pv1"]}
        full = {n: sem("full" + n) for n in "ABCD"}
        empty = {n: sem("empty" + n) for n in "ABCD"}

        def nth(b, use, i):
            if i is None:
                return before_loop[b].index(use)
            return i * len(in_loop[b]) + (len(before_loop[b]) + in_loop[b].index(use))

        def ready(b, i):
            return i * len(in_loop[b]) + len(before_loop[b])

        x_loaded = sem("x_loaded")
        xres_ready = sem("xres_ready")
        turned = sem("turned")
        q_ready = sem("q_ready")
        k_ready = sem("k_ready")
        shift_loaded = sem("shift_loaded")
        scores_full = [sem(f"scores_full{i}") for i in range(2)]
        rounded = [sem(f"rounded{i}") for i in range(2)]
        frac_ready = [sem(f"frac_ready{i}") for i in range(2)]
        probs_ready = [sem(f"probs_ready{i}") for i in range(2)]
        onorm_ready = sem("onorm_ready")
        stats_ready = sem("stats_ready")
        var_ready = sem("var_ready")
        vare_ready = sem("vare_ready")
        rstd_ready = sem("rstd_ready")
        x_ready = sem("x_ready")
        warmed = sem("warmed")
        init = sem("init")
        n_init = 7 if softmax else 5
        scores_empty = probs_ready if softmax else frac_ready

        def value_blocks(s):
            return bass.AP(vb[s], 0, [[G * J * VW, P], [J * VW, G], [VW + HD, J], [1, HD]])

        def sum_columns(s):
            return bass.AP(vb[s], 32, [[G * J * VW, P], [J * VW, G], [VW + 1, J]])

        n_in = 2 if ctx_in is not None else 1
        w, cst = (k.w_sin if kind == "sine" else k.w_rope), k.c
        w_out = {"sine": k.w_sin[:, 3:5, :], "rope": k.w_rope[:, 5:7, :], "causal": k.w_proj[:, :, :]}[kind]
        b_out = {"sine": BO0, "rope": BO1, "causal": BPROJ}[kind]
        block = ctx.enter_context(nc.Block())

        def pair(i):
            return 0 if i is None else i + 1

        @block.sync
        def _(sp):
            def load(n):
                if x_in is None:
                    src = k.x[:, bass.ds(n * 2, 2), :]
                else:
                    src = x_in[bass.ds(n * 2, 2), :, :].rearrange("b t d -> t b d")
                sp.dma_start(xin[:, :, :], src).then_inc(x_loaded, 16)
                if ctx_in is not None:
                    sp.dma_start(cin[:, :, :], ctx_in[bass.ds(n * 2, 2), :, :].rearrange("b t d -> t b d")
                                 ).then_inc(x_loaded, 16)

            load(0)
            sp.wait_ge(xres_ready, 1)
            load(1)
            with sp.Fori(0, NPAIR - 2) as i:
                sp.wait_ge(xres_ready, i + 2)
                load(i + 2)
            sp.wait_ge(xres_ready, NPAIR)
            load(0)
            sp.wait_ge(x_loaded, 16 * n_in * (NPAIR + 1))

        @block.tensor
        def _(pe):
            def transposes(i):
                pe.wait_ge(x_loaded, (pair(i) + 1) * (16 * n_in))
                pe.wait_ge(empty["C"], nth("C", "xT", i))
                for m, src in enumerate((xin, cin)[:n_in]):
                    for s in range(2):
                        ins = nc.tensor.transpose(bank["C"][:, (2 * m + s) * P:(2 * m + s + 1) * P],
                                                  src[:, s, :], cst("ident"))
                ins.then_inc(full["C"], 1)

            def project_qk(i):
                pe.wait_ge(empty["C"], nth("C", "xT", i) + 1)
                src_q, src_k = xT[:, 0:256], xT[:, 256:512] if n_in == 2 else xT[:, 0:256]
                if kind == "causal":
                    pe.wait_ge(empty["A"], nth("A", "lat", i))
                    nc.tensor.matmul(bank["A"][0:3 * LAT, 0:256], k.w_lat[:, :], src_q, start=True, stop=True
                                     ).then_inc(full["A"], 1)
                pe.wait_ge(empty["A"], nth("A", "q", i))
                if kind == "causal":
                    nc.tensor.matmul(bank["A"][:, 0:256], k.w_heads[0:3 * LAT, 0, :], latT[0:3 * LAT, :],
                                     start=True, stop=True).then_inc(full["A"], 1)
                    pe.wait_ge(empty["B"], nth("B", "k", i))
                    nc.tensor.matmul(bank["B"][:, 0:256], k.w_heads[0:3 * LAT, 1, :], latT[0:3 * LAT, :],
                                     start=True, stop=True).then_inc(full["B"], 1)
                elif kind == "rope":
                    nc.tensor.matmul(bank["A"][:, 0:256], w[:, 0, :], src_q, start=True, stop=True)
                    nc.tensor.matmul(bank["A"][:, 256:512], w[:, 1, :], src_q, start=True, stop=True
                                     ).then_inc(full["A"], 1)
                    pe.wait_ge(empty["B"], nth("B", "k", i))
                    nc.tensor.matmul(bank["B"][:, 0:256], w[:, 2, :], src_k, start=True, stop=True)
                    nc.tensor.matmul(bank["B"][:, 256:512], w[:, 3, :], src_k, start=True, stop=True
                                     ).then_inc(full["B"], 1)
                else:
                    nc.tensor.matmul(bank["A"][:, 0:256], w[:, 0, :], src_q, start=True, stop=True
                                     ).then_inc(full["A"], 1)
                    pe.wait_ge(empty["B"], nth("B", "k", i))
                    nc.tensor.matmul(bank["B"][:, 0:256], w[:, 1, :], src_k, start=True, stop=True
                                     ).then_inc(full["B"], 1)

            def project_v(i):
                pe.wait_ge(empty["C"], nth("C", "v", i))
                for s in range(2):
                    if kind == "causal":
                        src, wv = latT[0:3 * LAT, s * P:(s + 1) * P], k.w_heads[0:3 * LAT, 2, :]
                    elif kind == "rope":
                        src, wv = xT[:, 256 + s * P:256 + (s + 1) * P], w[:, 4, :]
                    else:
                        src, wv = xT[:, s * P:(s + 1) * P], w[:, 2, :]
                    ins = nc.tensor.matmul(bank["C"][:, s * P:(s + 1) * P], src, wv, start=True, stop=True)
                ins.then_inc(full["C"], 1)

            def row_scores(i, s):
                for j in range(J):
                    b = "AB"[j % 2]
                    pe.wait_ge(empty[b], nth(b, f"m{s}{j}", i))
                    ins = nc.tensor.matmul(bank[b][:, :], q4[:, j, s * P:(s + 1) * P], kg[:, :, s * P:(s + 1) * P],
                                           start=True, stop=kind != "causal")
                    if kind == "causal":
                        ins = nc.tensor.matmul(bank[b][:, :], k.ident_bf[:, :],
                                               k.causal_qk_bf[:, :].unsqueeze(1).to_broadcast([P, 4, P]),
                                               start=False, stop=True)
                    ins.then_inc(full[b], 1)

            def turn_maxima(i, s):
                pe.wait_ge(empty["B"], nth("B", f"m{s}3", i) + 1)
                pe.wait_ge(empty["C"], nth("C", f"nm{s}", i))
                nc.tensor.transpose(bank["C"][0:H, 0:P], negmax[s][:, :], cst("ident")).then_inc(full["C"], 1)

            def key_scores(i, s):
                if softmax:
                    pe.wait_ge(shift_loaded, i * 32 + 16 * (s + 1))
                for half in range(2):
                    pe.wait_ge(scores_empty[half], i * 2 + (s + 1))
                    for g in (2 * half, 2 * half + 1):
                        out = scores[half][:, (g % 2) * 512:(g % 2 + 1) * 512]
                        ins = nc.tensor.matmul(out, kg[:, g, s * P:(s + 1) * P], q4[:, :, s * P:(s + 1) * P],
                                               start=True, stop=not softmax)
                        if kind == "causal":
                            nc.tensor.matmul(out, k.ident_bf[:, :],
                                             k.causal_kq_bf[:, :].unsqueeze(1).to_broadcast([P, 4, P]),
                                             start=False, stop=False)
                        if softmax:
                            ins = nc.tensor.matmul(out, k.ones_r[:, :], shift[s][:, g * 512:(g + 1) * 512],
                                                   start=False, stop=True)
                    ins.then_inc(scores_full[half], 1)

            def values(i, s):
                pe.wait_ge(empty["D"], nth("D", f"pv{s}", i) + 1)
                for r in range(2):
                    pe.wait_ge(probs_ready[r], i * 2 + (s + 2))
                    for j in range(J):
                        for a in range(2):
                            h = 4 * (2 * r + a) + j
                            ins = nc.tensor.matmul(bank["D"][64 * a:64 * a + 64, r * P:(r + 1) * P],
                                                   vb[s][:, 2 * r + a, j, :], probs[s][:, h * P:(h + 1) * P],
                                                   start=(j == 0), stop=(j == J - 1))
                ins.then_inc(full["D"], 1)

            def repeat_sums(i, s):
                pe.wait_ge(empty["D"], nth("D", f"sum{s}", i) + 1)
                nc.tensor.matmul(bank["D"][:, 256:512], cst("sumrep"), osum[s][:, :], start=True, stop=True
                                 ).then_inc(full["D"], 1)

            def project_out(i, s):
                if softmax:
                    pe.wait_ge(onorm_ready, i * 2 + (s + 1))
                else:
                    pe.wait_ge(empty["D"], nth("D", f"pv{s}", i) + 2)
                pe.wait_ge(empty["C"], nth("C", f"y{s}", i))
                for r in range(2):
                    ins = nc.tensor.matmul(bank["C"][:, 0:P], onorm[s][:, r * P:(r + 1) * P], w_out[:, r, :],
                                           start=(r == 0), stop=(r == 1))
                ins.then_inc(full["C"], 1)

            transposes(None)
            project_qk(None)
            project_v(None)
            with pe.Fori(0, NPAIR) as i:
                if kind == "rope":
                    pe.wait_ge(q_ready, i + 1)
                    pe.wait_ge(k_ready, i + 1)
                else:
                    pe.wait_ge(empty["A"], ready("A", i))
                    pe.wait_ge(empty["B"], ready("B", i))
                if softmax:
                    row_scores(i, 0)
                    transposes(i)
                    turn_maxima(i, 0)
                    row_scores(i, 1)
                    key_scores(i, 0)
                    turn_maxima(i, 1)
                    key_scores(i, 1)
                else:
                    key_scores(i, 0)
                    transposes(i)
                    key_scores(i, 1)
                project_qk(i)
                values(i, 0)
                if softmax:
                    repeat_sums(i, 0)
                values(i, 1)
                project_v(i)
                project_out(i, 0)
                if softmax:
                    repeat_sums(i, 1)
                project_out(i, 1)

        @block.scalar
        def _(act):
            def take_xT(i):
                act.wait_ge(full["C"], nth("C", "xT", i) + 1)
                nc.scalar.copy(xT[:, 0:256 * n_in], bank["C"][:, 0:256 * n_in]).then_inc(empty["C"], 1)

            def take_k(i):
                if kind == "rope":
                    act.wait_ge(turned, pair(i) * 2 + 2)
                else:
                    act.wait_ge(full["B"], nth("B", "k", i) + 1)
                for g in range(G):
                    rows = slice(32 * g, 32 * g + 32)
                    if kind == "rope":
                        ins = nc.scalar.copy(kg[rows, g, :], turn[5][rows, :])
                    elif kind == "sine":
                        ins = nc.scalar.activation(kg[rows, g, :], bank["B"][rows, 0:256], ACT.Identity,
                                                   bias=k.bias_col[rows, BK0:BK0 + 1])
                    else:
                        ins = nc.scalar.copy(kg[rows, g, :], bank["B"][rows, 0:256])
                ins.then_inc(k_ready if kind == "rope" else empty["B"], 1)

            def take_v(i):
                act.wait_ge(full["C"], nth("C", "v", i) + 1)
                for s in range(2):
                    ins = nc.scalar.copy(value_blocks(s), bank["C"][:, s * P:(s + 1) * P]
                                         .rearrange("p (g j d) -> p g j d", g=G, j=J))
                ins.then_inc(empty["C"], 1)

            def take_maxima(i, s):
                act.wait_ge(full["C"], nth("C", f"nm{s}", i) + 1)
                nc.scalar.copy(negmaxT[s][:, :], bank["C"][0:H, 0:P]).then_inc(empty["C"], 1)
                act.wait_ge(empty["C"], nth("C", f"nm{s}", i) + 1)
                act.dma_start(shift[s][0:1, :].bitcast(F32).rearrange("o (h q) -> o h q", q=P),
                              negmaxT[s][:, :].bitcast(F32)).then_inc(shift_loaded, 16)

            def exps(i, s, half):
                act.wait_ge(scores_full[half], i * 2 + (s + 1))
                nc.scalar.activation(probs[s][:, half * 1024:(half + 1) * 1024], scores[half][:, :], ACT.Exp,
                                     scale=HD ** -0.5).then_inc(probs_ready[half], 1)

            def take_out(i, s):
                act.wait_ge(full["D"], nth("D", f"pv{s}", i) + 1)
                nc.scalar.copy((osum if softmax else onorm)[s][:, :], bank["D"][:, 0:256]
                               ).then_inc(empty["D"], 1)

            def rounds(i, s, half):
                act.wait_ge(probs_ready[half], i * 2 + (s + 1))
                act.wait_ge(scores_full[half], i * 2 + (s + 1))
                nc.scalar.activation(rnd[half][:, :], scores[half][:, :], ACT.Copy, bias=MAGIC
                                     ).then_inc(rounded[half], 1)

            def sines(i, s, half):
                act.wait_ge(frac_ready[half], i * 2 + (s + 2))
                nc.scalar.activation(probs[s][:, half * 1024:(half + 1) * 1024], rnd[half][:, :], ACT.Sin,
                                     scale=float(-2 * np.pi)).then_inc(probs_ready[half], 1)

            act.wait_ge(init, n_init)
            for n, sem_one in enumerate((*probs_ready, empty["D"], warmed)):
                nc.scalar.copy(warm[:, n:n + 1], cst("ident", 0, 1)).then_inc(sem_one, 1)
            take_xT(None)
            take_k(None)
            if kind == "causal":
                take_v(None)
            with act.Fori(0, NPAIR) as i:
                act.wait_ge(warmed, i + 1)
                nc.scalar.activation(warm[:, 4:5], cst("ident", 0, 1), ACT.Exp if softmax else ACT.Sin).then_inc(warmed, 1)
                if softmax:
                    take_xT(i)
                    take_maxima(i, 0)
                    exps(i, 0, 0)
                    take_maxima(i, 1)
                    exps(i, 0, 1)
                    exps(i, 1, 0)
                    exps(i, 1, 1)
                else:
                    rounds(i, 0, 0)
                    rounds(i, 0, 1)
                    take_xT(i)
                    sines(i, 0, 0)
                    rounds(i, 1, 0)
                    sines(i, 0, 1)
                    rounds(i, 1, 1)
                    sines(i, 1, 0)
                    sines(i, 1, 1)
                take_k(i)
                take_out(i, 0)
                take_out(i, 1)
                if kind == "causal":
                    take_v(i)

        @block.gpsimd
        def _(pool):
            for s in range(2):
                nc.gpsimd.memset(vb[s][:, :, :, :], 0.0).then_inc(init, 1)
            nc.gpsimd.memset(kg[:, :, :], 0.0).then_inc(init, 1)
            if softmax:
                for s in range(2):
                    nc.gpsimd.memset(shift[s][:, :].bitcast(F32), 0.0).then_inc(init, 1)
            pool.wait_ge(init, 2)
            for s in range(2):
                ins = nc.gpsimd.memset(sum_columns(s), 1.0)
            ins.then_inc(init, 1)
            nc.gpsimd.memset(mhalf[:, :], -0.5).then_inc(init, 1)

            def residual(i):
                pool.wait_ge(empty["C"], nth("C", "xT", None) + 1 if i is None else nth("C", "y1", i) + 1)
                pool.wait_ge(x_loaded, (pair(i) + 1) * (16 * n_in))
                for s in range(2):
                    ins = nc.gpsimd.tensor_tensor(xres[:, s, :], xin[:, s, :], k.bias_row[:, b_out, :], ALU.add)
                ins.then_inc(xres_ready, 1)

            def inverse_deviation(i, s):
                pool.wait_ge(vare_ready, i * 2 + (s + 1))
                nc.gpsimd.tensor_tensor(rstd[:, s:s + 1], vare[:, s:s + 1], mhalf[:, s:s + 1], ALU.pow
                                        ).then_inc(rstd_ready, 1)

            residual(None)
            with pool.Fori(0, NPAIR) as i:
                inverse_deviation(i, 0)
                inverse_deviation(i, 1)
                residual(i)

        @block.vector
        def _(dve):
            dve.wait_ge(init, n_init)

            def maxima(i, s):
                for j in range(J):
                    b = "AB"[j % 2]
                    dve.wait_ge(full[b], nth(b, f"m{s}{j}", i) + 1)
                    nc.vector.tensor_reduce(negmax[s][:, j::4], bank[b][:, :].rearrange("p (g t) -> p g t", g=G),
                                            AX.X, ALU.max, negate=True).then_inc(empty[b], 1)

            def take_qk(i):
                if kind == "causal":
                    dve.wait_ge(full["A"], nth("A", "lat", i) + 1)
                    nc.vector.tensor_copy(latT[0:3 * LAT, :], bank["A"][0:3 * LAT, 0:256]
                                          ).then_inc(empty["A"], 1)
                dve.wait_ge(full["A"], nth("A", "q", i) + 1)
                if kind == "rope":
                    nc.vector.scalar_tensor_tensor(turn[0][:, :], bank["A"][:, 0:256], k.bias_col[:, BQ1:BQ1 + 1],
                                                   cst("cos"), ALU.add, ALU.mult)
                    nc.vector.scalar_tensor_tensor(turn[1][:, :], bank["A"][:, 256:512], k.bias_col[:, BQ1R:BQ1R + 1],
                                                   cst("sin"), ALU.add, ALU.mult).then_inc(empty["A"], 1)
                    dve.wait_ge(full["B"], nth("B", "k", i) + 1)
                    nc.vector.scalar_tensor_tensor(turn[3][:, :], bank["B"][:, 0:256], k.bias_col[:, BK1:BK1 + 1],
                                                   cst("cos"), ALU.add, ALU.mult)
                    nc.vector.scalar_tensor_tensor(turn[4][:, :], bank["B"][:, 256:512], k.bias_col[:, BK1R:BK1R + 1],
                                                   cst("sin"), ALU.add, ALU.mult).then_inc(empty["B"], 1)
                    dve.wait_ge(empty["B"], nth("B", "k", i) + 1)
                    nc.vector.tensor_tensor(turn[2][:, :], turn[0][:, :], turn[1][:, :], ALU.add).then_inc(turned, 1)
                    nc.vector.tensor_tensor(turn[5][:, :], turn[3][:, :], turn[4][:, :], ALU.add).then_inc(turned, 1)
                    dve.wait_ge(turned, pair(i) * 2 + 2)
                for j in range(J):
                    if kind == "sine":
                        ins = nc.vector.tensor_scalar(q4[:, j, :], bank["A"][:, 0:256], k.bias_col[:, BQ0:BQ0 + 1],
                                                      cst("maskc", j, j + 1), ALU.add, ALU.mult)
                    else:
                        ins = nc.vector.tensor_scalar(q4[:, j, :], turn[2][:, :] if kind == "rope" else bank["A"][:, 0:256],
                                                      cst("mask", j, j + 1), None, ALU.mult)
                ins.then_inc(q_ready if kind == "rope" else empty["A"], 1)

            def take_v(i):
                dve.wait_ge(full["C"], nth("C", "v", i) + 1)
                bias = k.bias_row[:, BV0 if kind == "sine" else BV1, :].rearrange("p (g j d) -> p g j d", g=G, j=J)
                for s in range(2):
                    ins = nc.vector.tensor_tensor(value_blocks(s), bank["C"][:, s * P:(s + 1) * P]
                                                  .rearrange("p (g j d) -> p g j d", g=G, j=J), bias, ALU.add)
                ins.then_inc(empty["C"], 1)

            def fractions(i, s, half):
                dve.wait_ge(rounded[half], i * 2 + (s + 1))
                nc.vector.scalar_tensor_tensor(rnd[half][:, :], rnd[half][:, :], -MAGIC, scores[half][:, :],
                                               ALU.add, ALU.subtract).then_inc(frac_ready[half], 1)

            def normalise(i, s):
                dve.wait_ge(full["D"], nth("D", f"sum{s}", i) + 1)
                nc.vector.reciprocal(recip[s][:, :], bank["D"][:, 256:512]).then_inc(empty["D"], 1)
                dve.wait_ge(empty["D"], nth("D", f"sum{s}", i) + 2)
                nc.vector.tensor_tensor(onorm[s][:, :], osum[s][:, :], recip[s][:, :], ALU.mult).then_inc(onorm_ready, 1)

            def add_residual(i, s):
                dve.wait_ge(full["C"], nth("C", f"y{s}", i) + 1)
                dve.wait_ge(xres_ready, i + 1)
                nc.vector.tensor_tensor(z[:, s, :], bank["C"][:, 0:P], xres[:, s, :], ALU.add
                                        ).then_inc(empty["C"], 1)

            def statistics(i, s):
                dve.wait_ge(empty["C"], nth("C", f"y{s}", i) + 1)
                nc.vector.bn_stats(stats[:, s, :], z[:, s, :]).then_inc(stats_ready, 1)

            def variance(i, s):
                nc.vector.bn_aggr(mv[:, s, :], stats[:, s, :]).then_inc(var_ready, 1)
                dve.wait_ge(var_ready, i * 2 + (s + 1))
                nc.vector.tensor_scalar(vare[:, s:s + 1], mv[:, s, 1:2], EPS, None, ALU.add).then_inc(vare_ready, 1)

            def layer_norm(i, s):
                dve.wait_ge(rstd_ready, i * 2 + (s + 1))
                nc.vector.tensor_scalar(k.x[:, bass.ds(i * 2 + s, 1), :].rearrange("p o d -> p (o d)"), z[:, s, :],
                                        mv[:, s, 0:1], rstd[:, s:s + 1], ALU.subtract, ALU.mult).then_inc(x_ready, 1)

            for n, sem_one in enumerate((x_ready,) if softmax else (x_ready, *frac_ready)):
                nc.vector.tensor_copy(one[:, n:n + 1], cst("ident", 0, 1)).then_inc(sem_one, 1)
            take_qk(None)
            if kind != "causal":
                take_v(None)
            with dve.Fori(0, NPAIR) as i:
                dve.wait_ge(x_ready, i * 2 + 1)
                if softmax:
                    maxima(i, 0)
                    maxima(i, 1)
                else:
                    for s in range(2):
                        for half in range(2):
                            fractions(i, s, half)
                take_qk(i)
                if softmax:
                    normalise(i, 0)
                if kind != "causal":
                    take_v(i)
                add_residual(i, 0)
                statistics(i, 0)
                if softmax:
                    normalise(i, 1)
                dve.wait_ge(stats_ready, i * 2 + 1)
                add_residual(i, 1)
                variance(i, 0)
                statistics(i, 1)
                dve.wait_ge(stats_ready, i * 2 + 2)
                layer_norm(i, 0)
                variance(i, 1)
                layer_norm(i, 1)


def channel_attention(k, ctx_in):
    nc = k.nc
    with ExitStack() as ctx:
        sb = lambda n, s, dt=F32: ctx.enter_context(nc.sbuf_tensor(f"channel_{n}", s, dt))
        ps = lambda n: ctx.enter_context(nc.psum_tensor(f"channel_{n}", [P, 512], F32))
        sem = lambda n: k.sem(f"channel_{n}")
        scores, turned_ctx, turned_attn, attended = ps("scores"), ps("turned_ctx"), ps("turned_attn"), ps("attended")
        cin = sb("cin", [P, 2, P])
        qp = sb("qp", [P, 2, 2, P])
        q = sb("q", [P, 2, 2, P])
        kp = sb("kp", [P, 2, 2, P])
        key = sb("key", [P, 2, 2, P])
        vT = sb("vT", [P, 2, 2, P])
        xres = sb("xres", [P, 2, P])
        negmax = sb("negmax", [P, 4])
        shift = sb("shift", [P, 4])
        ex = sb("ex", [P, 4, P])
        sums = sb("sums", [P, 4])
        recip = sb("recip", [P, 4])
        factor = sb("factor", [P, 4])
        attn = sb("attn", [P, 4, P])
        attnT = sb("attnT", [P, 4, P])
        z = sb("z", [P, 2, P])
        stats = sb("stats", [P, 2, 6])
        mv = sb("mv", [P, 2, 2])
        vare = sb("vare", [P, 2])
        rstd = sb("rstd", [P, 2])
        mhalf = sb("mhalf", [P, 2])

        c_loaded = sem("c_loaded")
        qp_ready = sem("qp_ready")
        q_ready = sem("q_ready")
        kp_ready = sem("kp_ready")
        key_ready = sem("key_ready")
        v_ready = sem("v_ready")
        xres_ready = sem("xres_ready")
        ctx_turned = sem("ctx_turned")
        scores_full = sem("scores_full")
        attn_turned = sem("attn_turned")
        out_full = sem("out_full")
        max_ready = sem("max_ready")
        shift_ready = sem("shift_ready")
        ex_ready = sem("ex_ready")
        sums_ready = sem("sums_ready")
        recip_ready = sem("recip_ready")
        factor_ready = sem("factor_ready")
        attn_ready = sem("attn_ready")
        attnT_ready = sem("attnT_ready")
        z_ready = sem("z_ready")
        stats_ready = sem("stats_ready")
        var_ready = sem("var_ready")
        vare_ready = sem("vare_ready")
        rstd_ready = sem("rstd_ready")
        x_ready = sem("x_ready")
        init = sem("init")
        LAST = NPAIR - 1
        scale = P ** -0.5
        rows = lambda m: k.ch_row[:, m:m + 2, :].unsqueeze(1).to_broadcast([P, 2, 2, P])
        block = ctx.enter_context(nc.Block())


        @block.sync
        def _(sp):
            def load(n):
                sp.dma_start(cin[:, :, :], ctx_in[bass.ds(n * 2, 2), :, :].rearrange("b t d -> t b d")
                             ).then_inc(c_loaded, 16)

            load(0)
            with sp.Fori(0, LAST) as i:
                sp.wait_ge(key_ready, i + 1)
                load(i + 1)

        @block.tensor
        def _(pe):
            def turn_ctx(n):
                pe.wait_ge(c_loaded, n * 16 + 16)
                for s in range(2):
                    ins = nc.tensor.transpose(turned_ctx[:, s * P:(s + 1) * P], cin[:, s, :], k.c("ident"))
                ins.then_inc(ctx_turned, 1)

            def turn(i, last):
                pe.wait_ge(q_ready, i + 1)
                pe.wait_ge(key_ready, i + 1)
                nc.tensor.matmul(scores[:, :], k.ident_bf[:, :],
                                 k.blocks_bf[:, :].unsqueeze(1).to_broadcast([P, 4, P]), start=True, stop=False)
                for s in range(2):
                    for m in range(2):
                        ins = nc.tensor.matmul(scores[:, (2 * s + m) * P:(2 * s + m + 1) * P], q[:, s, m, :],
                                               key[:, s, m, :], start=False, stop=s + m == 2)
                ins.then_inc(scores_full, 1)
                pe.wait_ge(v_ready, i + 1)
                if not last:
                    turn_ctx(i + 1)
                pe.wait_ge(attn_ready, i + 1)
                for n in range(4):
                    ins = nc.tensor.transpose(turned_attn[:, n * P:(n + 1) * P], attn[:, n, :], k.c("ident"))
                ins.then_inc(attn_turned, 1)
                pe.wait_ge(attnT_ready, i + 1)
                for s in range(2):
                    for m in range(2):
                        ins = nc.tensor.matmul(attended[:, s * P:(s + 1) * P], vT[:, m, s, :], attnT[:, 2 * s + m, :],
                                               start=(m == 0), stop=(m == 1))
                ins.then_inc(out_full, 1)

            turn_ctx(0)
            with pe.Fori(0, LAST) as i:
                turn(i, False)
            turn(LAST, True)

        @block.scalar
        def _(act):
            def take_values(n):
                act.wait_ge(ctx_turned, n + 1)
                for m in range(2):
                    ins = nc.scalar.activation(vT[:, m, :, :].rearrange("p s t -> p (s t)"), turned_ctx[:, 0:256],
                                               ACT.Identity, bias=k.ch_col[:, BV + m:BV + m + 1],
                                               scale=k.ch_col[:, WV + m:WV + m + 1])
                ins.then_inc(v_ready, 1)

            def turn(i, last):
                act.wait_ge(shift_ready, i + 1)
                for n in range(4):
                    ins = nc.scalar.activation(ex[:, n, :], scores[:, n * P:(n + 1) * P], ACT.Exp,
                                               bias=shift[:, n:n + 1], scale=scale)
                ins.then_inc(ex_ready, 1)
                act.wait_ge(attn_turned, i + 1)
                nc.scalar.copy(attnT[:, :, :].rearrange("p n d -> p (n d)"), turned_attn[:, :]).then_inc(attnT_ready, 1)
                if not last:
                    act.wait_ge(out_full, i + 1)
                    take_values(i + 1)

            act.wait_ge(k.loaded_channel, N_CHANNEL)
            take_values(0)
            with act.Fori(0, LAST) as i:
                turn(i, False)
            turn(LAST, True)

        @block.gpsimd
        def _(pool):
            def take_keys(n):
                pool.wait_ge(c_loaded, n * 16 + 16)
                pool.wait_ge(ctx_turned, n + 1)
                nc.gpsimd.tensor_tensor(kp[:, :, :, :], cin[:, :, :].unsqueeze(2).to_broadcast([P, 2, 2, P]), rows(WK),
                                        ALU.mult).then_inc(kp_ready, 1)
                pool.wait_ge(kp_ready, n + 1)
                nc.gpsimd.tensor_tensor(key[:, :, :, :], kp[:, :, :, :], rows(BK), ALU.add).then_inc(key_ready, 1)

            def turn(i, last):
                pool.wait_ge(max_ready, i + 1)
                nc.gpsimd.tensor_tensor(xres[:, :, :], k.x[:, bass.ds(i * 2, 2), :],
                                        k.ch_row[:, BP:BP + 1, :].to_broadcast([P, 2, P]), ALU.add
                                        ).then_inc(xres_ready, 1)
                if not last:
                    take_keys(i + 1)
                pool.wait_ge(vare_ready, i + 1)
                nc.gpsimd.tensor_tensor(rstd[:, :], vare[:, :], mhalf[:, :], ALU.pow).then_inc(rstd_ready, 1)

            nc.gpsimd.memset(mhalf[:, :], -0.5).then_inc(init, 1)
            pool.wait_ge(k.loaded_channel, N_CHANNEL)
            take_keys(0)
            pool.wait_ge(init, 1)
            with pool.Fori(0, LAST) as i:
                turn(i, False)
            turn(LAST, True)

        @block.vector
        def _(dve):
            def scale_queries(n):
                nc.vector.tensor_tensor(qp[:, :, :, :], k.x[:, bass.ds(n * 2, 2), :].unsqueeze(2)
                                        .to_broadcast([P, 2, 2, P]), rows(WQ), ALU.mult).then_inc(qp_ready, 1)

            def finish_queries(n):
                dve.wait_ge(qp_ready, n + 1)
                nc.vector.tensor_tensor(q[:, :, :, :], qp[:, :, :, :], rows(BQ), ALU.add).then_inc(q_ready, 1)

            def turn(i, last):
                dve.wait_ge(scores_full, i + 1)
                nc.vector.tensor_reduce(negmax[:, :], scores[:, :].rearrange("p (n e) -> p n e", n=4), AX.X, ALU.max,
                                        negate=True).then_inc(max_ready, 1)
                dve.wait_ge(max_ready, i + 1)
                nc.vector.tensor_scalar(shift[:, :], negmax[:, :], scale, None, ALU.mult).then_inc(shift_ready, 1)
                if not last:
                    dve.wait_ge(q_ready, i + 1)
                    scale_queries(i + 1)
                dve.wait_ge(ex_ready, i + 1)
                nc.vector.tensor_reduce(sums[:, :], ex[:, :, :], AX.X, ALU.add).then_inc(sums_ready, 1)
                dve.wait_ge(sums_ready, i + 1)
                nc.vector.reciprocal(recip[:, :], sums[:, :]).then_inc(recip_ready, 1)
                dve.wait_ge(recip_ready, i + 1)
                nc.vector.scalar_tensor_tensor(factor[:, :], recip[:, :], 2.0, k.ch_col[:, WP:WP + 1].to_broadcast([P, 4]),
                                               ALU.mult, ALU.mult).then_inc(factor_ready, 1)
                dve.wait_ge(factor_ready, i + 1)
                nc.vector.tensor_tensor(attn[:, :, :], ex[:, :, :], factor[:, :].unsqueeze(2).to_broadcast([P, 4, P]),
                                        ALU.mult).then_inc(attn_ready, 1)
                dve.wait_ge(out_full, i + 1)
                dve.wait_ge(xres_ready, i + 1)
                nc.vector.tensor_tensor(z[:, :, :], attended[:, 0:256].rearrange("p (s d) -> p s d", s=2), xres[:, :, :],
                                        ALU.add).then_inc(z_ready, 1)
                dve.wait_ge(z_ready, i + 1)
                for s in range(2):
                    ins = nc.vector.bn_stats(stats[:, s, :], z[:, s, :])
                ins.then_inc(stats_ready, 1)
                dve.wait_ge(stats_ready, i + 1)
                if not last:
                    finish_queries(i + 1)
                for s in range(2):
                    ins = nc.vector.bn_aggr(mv[:, s, :], stats[:, s, :])
                ins.then_inc(var_ready, 1)
                dve.wait_ge(var_ready, i + 1)
                nc.vector.tensor_scalar(vare[:, :], mv[:, :, 1], EPS, None, ALU.add).then_inc(vare_ready, 1)
                dve.wait_ge(rstd_ready, i + 1)
                for s in range(2):
                    ins = nc.vector.tensor_scalar(k.x[:, bass.ds(i * 2 + s, 1), :].rearrange("p o d -> p (o d)"),
                                                  z[:, s, :], mv[:, s, 0:1], rstd[:, s:s + 1], ALU.subtract, ALU.mult)
                ins.then_inc(x_ready, 1)

            dve.wait_ge(k.loaded_channel, N_CHANNEL)
            scale_queries(0)
            finish_queries(0)
            with dve.Fori(0, LAST) as i:
                turn(i, False)
            turn(LAST, True)


def experts(k, layer):
    nc = k.nc
    tag = f"moe{layer}"
    NE, NX = (E0, E0 + 1) if layer == 0 else (E1, E1)
    router, bias = (k.wr0, k.rb0) if layer == 0 else (k.gate_w, k.gate_b)
    gu, dn, W = (k.gu0, k.dn0, W0) if layer == 0 else (k.gu1, k.dn1, I1)
    NC = W // P
    NG = NB // 4
    with ExitStack() as outer:
        sb = lambda n, s, dt=F32: outer.enter_context(nc.sbuf_tensor(f"{tag}_{n}", s, dt))
        sem = lambda n: k.sem(f"{tag}_{n}")
        xT = sb("xT", [P, NB * P])
        weight = sb("weight", [P, NB, NX])
        credit = sb("credit", [P, 4])

        with ExitStack() as ctx:
            rows = ctx.enter_context(nc.sbuf_tensor(f"{tag}_rows", [P, 2, 4, P], F32))
            part = lambda n: ctx.enter_context(nc.sbuf_tensor(f"{tag}_{n}", [P, NB, NE], F32))
            line = lambda n: ctx.enter_context(nc.sbuf_tensor(f"{tag}_{n}", [P, NB], F32))
            logits, equal1, place1, first, rest, equal2, place2, second, w_first, w_second = (
                part(n) for n in ("logits", "equal1", "place1", "first", "rest", "equal2", "place2", "second",
                                  "w_first", "w_second"))
            max1, at1, max2, at2, gap, ratio, total, w1, w2 = (
                line(n) for n in ("max1", "at1", "max2", "at2", "gap", "ratio", "total", "w1", "w2"))
            turned = [ctx.enter_context(nc.psum_tensor(f"{tag}_turned{b}", [P, 512], F32)) for b in range(2)]
            scored = [ctx.enter_context(nc.psum_tensor(f"{tag}_scored{b}", [P, 4, NE], F32)) for b in range(2)]
            rows_loaded = [sem(f"rows_loaded{b}") for b in range(2)]
            turned_full = [sem(f"turned_full{b}") for b in range(2)]
            xT_ready = [sem(f"xT_ready{b}") for b in range(2)]
            scored_full = [sem(f"scored_full{b}") for b in range(2)]
            logits_ready = sem("logits_ready")
            gap_ready = sem("gap_ready")
            ratio_ready = sem("ratio_ready")
            step = sem("step")
            block = ctx.enter_context(nc.Block())

            @block.sync
            def _(sp):
                for g in range(NG):
                    if g >= 2:
                        sp.wait_ge(turned_full[g % 2], g // 2)
                    sp.dma_start(rows[:, g % 2, :, :], k.x[:, 4 * g:4 * g + 4, :]).then_inc(rows_loaded[g % 2], 16)

            @block.tensor
            def _(pe):
                for g in range(NG):
                    b = g % 2
                    pe.wait_ge(rows_loaded[b], 16 * (g // 2 + 1))
                    if g >= 2:
                        pe.wait_ge(xT_ready[b], g // 2)
                    for t in range(4):
                        ins = nc.tensor.transpose(turned[b][:, t * P:(t + 1) * P], rows[:, b, t, :], k.c("ident"))
                    ins.then_inc(turned_full[b], 1)
                    pe.wait_ge(xT_ready[b], g // 2 + 1)
                    if g >= 2:
                        pe.wait_ge(logits_ready, g - 1)
                    for t in range(4):
                        at = (4 * g + t) * P
                        ins = nc.tensor.matmul(scored[b][:, t, :], xT[:, at:at + P], router[:, :], start=True, stop=True)
                    ins.then_inc(scored_full[b], 1)

            @block.scalar
            def _(act):
                for g in range(NG):
                    act.wait_ge(turned_full[g % 2], g // 2 + 1)
                    nc.scalar.copy(xT[:, g * 512:(g + 1) * 512], turned[g % 2][:, :]).then_inc(xT_ready[g % 2], 1)
                act.wait_ge(gap_ready, 1)
                nc.scalar.activation(ratio[:, :], gap[:, :], ACT.Exp).then_inc(ratio_ready, 1)

            @block.vector
            def _(dve):
                for g in range(NG):
                    dve.wait_ge(scored_full[g % 2], g // 2 + 1)
                    nc.vector.tensor_tensor(logits[:, 4 * g:4 * g + 4, :], scored[g % 2][:, :, :],
                                            bias[:, :].unsqueeze(1).to_broadcast([P, 4, NE]), ALU.add
                                            ).then_inc(logits_ready, 1)
                over = lambda a: a[:, :].unsqueeze(2).to_broadcast([P, NB, NE])
                index = k.c("eidx", 0, NE).unsqueeze(1).to_broadcast([P, NB, NE])
                dve.wait_ge(logits_ready, NG)
                nc.vector.tensor_reduce(max1[:, :], logits[:, :, :], AX.X, ALU.max).then_inc(step, 1)
                dve.wait_ge(step, 1)
                nc.vector.tensor_tensor(equal1[:, :, :], logits[:, :, :], over(max1), ALU.is_equal).then_inc(step, 1)
                dve.wait_ge(step, 2)
                nc.vector.scalar_tensor_tensor(place1[:, :, :], equal1[:, :, :], -64.0, index, ALU.mult, ALU.add
                                               ).then_inc(step, 1)
                dve.wait_ge(step, 3)
                nc.vector.tensor_reduce(at1[:, :], place1[:, :, :], AX.X, ALU.min).then_inc(step, 1)
                dve.wait_ge(step, 4)
                nc.vector.tensor_tensor(first[:, :, :], place1[:, :, :], over(at1), ALU.is_equal).then_inc(step, 1)
                dve.wait_ge(step, 5)
                nc.vector.scalar_tensor_tensor(rest[:, :, :], first[:, :, :], NEG, logits[:, :, :], ALU.mult, ALU.add
                                               ).then_inc(step, 1)
                dve.wait_ge(step, 6)
                nc.vector.tensor_reduce(max2[:, :], rest[:, :, :], AX.X, ALU.max).then_inc(step, 1)
                dve.wait_ge(step, 7)
                nc.vector.tensor_tensor(gap[:, :], max2[:, :], max1[:, :], ALU.subtract).then_inc(gap_ready, 1)
                nc.vector.tensor_tensor(equal2[:, :, :], rest[:, :, :], over(max2), ALU.is_equal).then_inc(step, 1)
                dve.wait_ge(step, 8)
                nc.vector.scalar_tensor_tensor(place2[:, :, :], equal2[:, :, :], -64.0, index, ALU.mult, ALU.add
                                               ).then_inc(step, 1)
                dve.wait_ge(step, 9)
                nc.vector.tensor_reduce(at2[:, :], place2[:, :, :], AX.X, ALU.min).then_inc(step, 1)
                dve.wait_ge(step, 10)
                nc.vector.tensor_tensor(second[:, :, :], place2[:, :, :], over(at2), ALU.is_equal).then_inc(step, 1)
                dve.wait_ge(ratio_ready, 1)
                nc.vector.tensor_scalar(total[:, :], ratio[:, :], 1.0, None, ALU.add).then_inc(step, 1)
                dve.wait_ge(step, 12)
                nc.vector.reciprocal(w1[:, :], total[:, :]).then_inc(step, 1)
                dve.wait_ge(step, 13)
                nc.vector.tensor_tensor(w2[:, :], ratio[:, :], w1[:, :], ALU.mult).then_inc(step, 1)
                nc.vector.tensor_tensor(w_first[:, :, :], first[:, :, :], over(w1), ALU.mult).then_inc(step, 1)
                dve.wait_ge(step, 14)
                nc.vector.tensor_tensor(w_second[:, :, :], second[:, :, :], over(w2), ALU.mult).then_inc(step, 1)
                dve.wait_ge(step, 16)
                if NX > NE:
                    nc.vector.memset(weight[:, :, NE:], 1.0)
                nc.vector.tensor_tensor(weight[:, :, 0:NE], w_first[:, :, :], w_second[:, :, :], ALU.add
                                        ).then_inc(step, 1)

        with ExitStack() as ctx:
            buf = lambda n, s: ctx.enter_context(nc.sbuf_tensor(f"{tag}_{n}", s, F32))
            ps = lambda n: ctx.enter_context(nc.psum_tensor(f"{tag}_{n}", [P, 512], F32))
            gate, up, down = ([ps(f"{n}{b}") for b in range(2)] for n in ("gate", "up", "down"))
            silu = [buf(f"silu{b}", [P, 512]) for b in range(2)]
            hidden = [buf(f"hidden{b}", [P, NC, 512]) for b in range(2)]
            w_group = buf("w_group", [P, 4, NX])
            acc = buf("acc", [P, 4, P])
            stats = buf("stats", [P, 4, 6])
            mv = buf("mv", [P, 4, 2])
            vare = buf("vare", [P, 4])
            rstd = buf("rstd", [P, 4])
            mhalf = buf("mhalf", [P, 4])
            up_full = [sem(f"up_full{b}") for b in range(2)]
            silu_ready = [sem(f"silu_ready{b}") for b in range(2)]
            hidden_ready = sem("hidden_ready")
            down_full = sem("down_full")
            acc_ready = sem("acc_ready")
            w_ready = sem("w_ready")
            stats_ready = sem("stats_ready")
            wait_done = sem("wait_done")
            var_ready = sem("var_ready")
            vare_ready = sem("vare_ready")
            rstd_ready = sem("rstd_ready")
            x_ready = sem("x_ready")
            init = sem("init")
            N = NX * NC
            block = ctx.enter_context(nc.Block())


            @block.tensor
            def _(pe):
                def go_up(g, e):
                    for c in range(NC):
                        n = e * NC + c
                        b = n % 2
                        pe.wait_ge(hidden_ready, g * N + (n + 1))
                        x = xT[:, bass.ds(g * 512, 512)]
                        nc.tensor.matmul(gate[b][:, :], gu[:, e, c * P:(c + 1) * P], x, start=True, stop=True)
                        nc.tensor.matmul(up[b][:, :], gu[:, e, W + c * P:W + (c + 1) * P], x, start=True, stop=True
                                         ).then_inc(up_full[b], 1)

                def go_down(g, e):
                    pe.wait_ge(hidden_ready, g * N + ((e + 1) * NC + 2))
                    for t in range(4):
                        for c in range(NC):
                            ins = nc.tensor.matmul(down[e % 2][:, t * P:(t + 1) * P],
                                                   hidden[e % 2][:, c, t * P:(t + 1) * P], dn[:, e, c, :],
                                                   start=(c == 0), stop=(c == NC - 1))
                    ins.then_inc(down_full, 1)

                if layer == 1:
                    pe.wait_ge(k.loaded_ffn1, N_FFN1)
                with pe.Fori(0, NG) as g:
                    go_up(g, 0)
                    for e in range(1, NX):
                        go_up(g, e)
                        go_down(g, e - 1)
                    go_down(g, NX - 1)

            @block.scalar
            def _(act):
                with act.Fori(0, NG) as g:
                    for n in range(N):
                        b = n % 2
                        act.wait_ge(up_full[b], g * (N // 2) + (n // 2 + 1))
                        nc.scalar.activation(silu[b][:, :], gate[b][:, :], ACT.Silu).then_inc(silu_ready[b], 1)

            @block.gpsimd
            def _(pool):
                nc.gpsimd.memset(mhalf[:, :], -0.5).then_inc(init, 1)
                pool.wait_ge(init, 1)
                with pool.Fori(0, NG) as g:
                    pool.wait_ge(vare_ready, g + 1)
                    nc.gpsimd.tensor_tensor(rstd[:, :], vare[:, :], mhalf[:, :], ALU.pow).then_inc(rstd_ready, 1)

            @block.vector
            def _(dve):
                def join(g, e):
                    for c in range(NC):
                        n = e * NC + c
                        dve.wait_ge(silu_ready[n % 2], g * (N // 2) + (n // 2 + 1))
                        nc.vector.tensor_tensor(hidden[e % 2][:, c, :], silu[n % 2][:, :], up[n % 2][:, :], ALU.mult
                                                ).then_inc(hidden_ready, 1)

                def add_up(g, e):
                    dve.wait_ge(down_full, g * NX + (e + 1))
                    dve.wait_ge(w_ready, g + 1) if e == 0 else dve.wait_ge(acc_ready, g * NX + e)
                    for t in range(4):
                        below = (k.x[:, bass.ds(g * 4 + t, 1), :].rearrange("p o d -> p (o d)") if e == 0
                                 else acc[:, t, :])
                        ins = nc.vector.scalar_tensor_tensor(acc[:, t, :], down[e % 2][:, t * P:(t + 1) * P],
                                                             w_group[:, t, e:e + 1], below, ALU.mult, ALU.add)
                    ins.then_inc(acc_ready, 1)

                for n, (sem_one, by) in enumerate(((hidden_ready, 2), (x_ready, 1), (wait_done, 1))):
                    nc.vector.tensor_copy(credit[:, n:n + 1], k.c("ident", 0, 1)).then_inc(sem_one, by)
                with dve.Fori(0, NG) as g:
                    join(g, 0)
                    dve.wait_ge(x_ready, g + 1)
                    nc.vector.tensor_copy(w_group[:, :, :], weight[:, bass.ds(g * 4, 4), :]).then_inc(w_ready, 1)
                    for e in range(1, NX):
                        join(g, e)
                        add_up(g, e - 1)
                    add_up(g, NX - 1)
                    dve.wait_ge(acc_ready, g * NX + NX)
                    for t in range(4):
                        ins = nc.vector.bn_stats(stats[:, t, :], acc[:, t, :])
                    ins.then_inc(stats_ready, 1)
                    dve.wait_ge(wait_done, g + 1)
                    dve.wait_ge(stats_ready, g + 1)
                    nc.vector.tensor_copy(credit[:, 3:4], k.c("ident", 0, 1)).then_inc(wait_done, 1)
                    for t in range(4):
                        ins = nc.vector.bn_aggr(mv[:, t, :], stats[:, t, :])
                    ins.then_inc(var_ready, 1)
                    dve.wait_ge(var_ready, g + 1)
                    nc.vector.tensor_scalar(vare[:, :], mv[:, :, 1], EPS, None, ALU.add).then_inc(vare_ready, 1)
                    dve.wait_ge(rstd_ready, g + 1)
                    for t in range(4):
                        ins = nc.vector.tensor_scalar(k.x[:, bass.ds(g * 4 + t, 1), :].rearrange("p o d -> p (o d)"),
                                                      acc[:, t, :], mv[:, t, 0:1], rstd[:, t:t + 1],
                                                      ALU.subtract, ALU.mult)
                    ins.then_inc(x_ready, 1)


def write_state(k, out):
    nc = k.nc
    with ExitStack() as ctx:
        stored = k.sem("stored")
        block = ctx.enter_context(nc.Block())

        @block.sync
        def _(sp):
            for n in range(4):
                sp.dma_start(out[8 * n:8 * n + 8, :, :].rearrange("b t d -> t b d"), k.x[:, 8 * n:8 * n + 8, :]
                             ).then_inc(stored, 16)
            sp.wait_ge(stored, 64)


def program(nc, d, out):
    with ExitStack() as ctx:
        k = Core(nc, ctx, d)
        setup(k, d)
        with nc.cleanup_on_exit():
            head_attention(k, "sine", d["x"], None)
        with nc.cleanup_on_exit():
            head_attention(k, "rope", None, d["ctx_1024"])
        with nc.cleanup_on_exit():
            experts(k, 0)
        with nc.cleanup_on_exit():
            head_attention(k, "causal", None, None)
        with nc.cleanup_on_exit():
            channel_attention(k, d["ctx_1024"])
        with nc.cleanup_on_exit():
            experts(k, 1)
        write_state(k, out)


NAMES = ["x", "ctx_1024",
         "L0_attn_Wq", "L0_attn_bq", "L0_attn_Wk", "L0_attn_bk", "L0_attn_Wv", "L0_attn_bv", "L0_attn_Wo", "L0_attn_bo",
         "L0_xattn_Wq", "L0_xattn_bq", "L0_xattn_Wk", "L0_xattn_bk", "L0_xattn_Wv", "L0_xattn_bv", "L0_xattn_Wo",
         "L0_xattn_bo", "L0_ffn_sg", "L0_ffn_su", "L0_ffn_sd", "L0_ffn_rg", "L0_ffn_ru", "L0_ffn_rd", "L0_ffn_wr",
         "L0_ffn_rb", "L1_attn_wq_lat", "L1_attn_wk_lat", "L1_attn_wv_lat", "L1_attn_wq_heads", "L1_attn_wk_heads",
         "L1_attn_wv_heads", "L1_attn_w_proj", "L1_attn_b_proj",
         "L1_xattn_wqg", "L1_xattn_bqg", "L1_xattn_wkg", "L1_xattn_bkg", "L1_xattn_wvg", "L1_xattn_bvg",
         "L1_xattn_wql", "L1_xattn_bql", "L1_xattn_wkl", "L1_xattn_bkl", "L1_xattn_wvl", "L1_xattn_bvl",
         "L1_xattn_wp", "L1_xattn_bp", "L1_ffn_gate_w", "L1_ffn_gate_b", "L1_ffn_w1", "L1_ffn_w3", "L1_ffn_w2"]


def kernel(**inputs):
    import concourse.bacc as bacc
    from concourse.bass_utils import run_bass_kernel_spmd

    nc = bacc.Bacc("TRN2", target_bir_lowering=False, num_devices=1)
    arrays = {n: np.ascontiguousarray(inputs[n]) for n in NAMES}
    arrays["const"] = constants()
    drams = {n: nc.dram_tensor("in_" + n, a.shape, mybir.dt.from_np(a.dtype), kind="ExternalInput").ap()
             for n, a in arrays.items()}
    out = nc.dram_tensor("out", (NB, P, P), F32, kind="ExternalOutput").ap()
    program(nc, drams, out)
    r = run_bass_kernel_spmd(nc, [{"in_" + n: a for n, a in arrays.items()}], core_ids=[0])
    return r.results[0]["out"]
```

```python
from contextlib import ExitStack

import numpy as np

import concourse.bass as bass
from concourse import mybir

F32 = mybir.dt.float32
F32R = mybir.dt.float32r
BF16 = mybir.dt.bfloat16
I32 = mybir.dt.int32
ALU = mybir.AluOpType
ACT = mybir.ActivationFunctionType
AX = mybir.AxisListType

P = 128
NB = 32
NPAIR = NB // 2
H, HD = 16, 8
G, J = 4, 4
VW = 64
EPS = 1e-5
NEG = -1e30
MAGIC = 12582912.0
E0, I0 = 7, 352
E1, I1 = 8, 512
CH0 = [(0, 128), (128, 128), (256, 96)]
W0 = 384
LAT = 32
CONST = {}
_at = 0
for _n, _w in (("ident", 128), ("rot", 128), ("cos", 256), ("sin", 256), ("sumrep", 128),
               ("before", 128), ("ones", 128), ("causal_qk", 128), ("causal_kq", 128),
               ("blocks", 128), ("mask", 4), ("maskc", 4), ("tile0", 80), ("eidx", 8)):
    CONST[_n] = (_at, _w)
    _at += _w
NCONST = _at


def constants():
    c = {n: np.zeros((P, w), np.float32) for n, (_, w) in CONST.items()}
    p = np.arange(P)
    c["ident"][p, p] = 1
    for e in range(P):
        lo = e % HD < HD // 2
        c["rot"][e + 4 if lo else e - 4, e] = -1 if lo else 1
    inv = (1.0 / np.float32(10000.0) ** (np.arange(0, HD, 2, dtype=np.float32) / HD)).astype(np.float32)
    ang = np.arange(P, dtype=np.float32)[None, :] * inv[p % (HD // 2)][:, None]
    c["cos"][:] = np.tile(np.cos(ang), (1, 2))
    c["sin"][:] = np.tile(np.sin(ang), (1, 2))
    for a in range(2):
        for j in range(J):
            c["sumrep"][64 * a + 32 + j, 64 * a + 8 * j:64 * a + 8 * j + 8] = 1
        c["sumrep"][64 * a + 32, 64 * a + 32:64 * a + 64] = 1
    c["before"][:] = p[:, None] < p[None, :]
    c["ones"][:] = 1
    c["causal_qk"][:] = np.where(p[None, :] > p[:, None], NEG, 0)
    c["causal_kq"][:] = c["causal_qk"].T
    c["blocks"][:] = np.where(p[None, :] // 32 != p[:, None] // 32, NEG, 0)
    c["mask"][:] = (p[:, None] % 32) // HD == np.arange(J)
    c["maskc"][:] = c["mask"] * np.float32(30.0 / (np.sqrt(8.0) * 2 * np.pi))
    c["tile0"][:] = 128 * np.arange(80)
    c["eidx"][:] = np.arange(8)
    return np.concatenate([c[n] for n in CONST], axis=1)


class Core:

    def __init__(self, nc, ctx, dram):
        self.nc, self.ctx, self.dram = nc, ctx, dram
        sb = self.sb
        self.const = sb("const", [P, NCONST])
        self.ident_bf = sb("ident_bf", [P, P], BF16)
        self.ones_bf = sb("ones_bf", [P, P], BF16)
        self.before_bf = sb("before_bf", [P, P], BF16)
        self.causal_qk_bf = sb("causal_qk_bf", [P, P], BF16)
        self.causal_kq_bf = sb("causal_kq_bf", [P, P], BF16)
        self.blocks_bf = sb("blocks_bf", [P, P], BF16)
        self.ones_r = sb("ones_r", [P, P], F32R)
        self.x = sb("x_state", [P, NB, P])
        self.w_sin = sb("w_sin", [P, 5, P])
        self.w_rope = sb("w_rope", [P, 7, P])
        self.w_lat = sb("w_lat", [P, 3 * LAT])
        self.w_heads = sb("w_heads", [P, 3, P])
        self.w_proj = sb("w_proj", [P, 2, P])
        self.bias_col = sb("bias_col", [P, 8])
        self.bias_row = sb("bias_row", [P, 5, P])
        self.wr0 = sb("wr0", [P, E0])
        self.rb0 = sb("rb0", [P, E0])
        self.gate_w = sb("gate_w", [P, E1])
        self.gate_b = sb("gate_b", [P, E1])
        self.ch_row = sb("ch_row", [P, 9, P])
        self.ch_col = sb("ch_col", [P, 5])
        self.loaded_channel = self.sem("loaded_channel")
        self.loaded_ffn1 = self.sem("loaded_ffn1")

    def place_experts0(self, ctx):
        self.gu0 = ctx.enter_context(self.nc.sbuf_tensor("gu0", [P, E0 + 1, 2 * W0], F32))
        self.dn0 = ctx.enter_context(self.nc.sbuf_tensor("dn0", [P, E0 + 1, 3, P], F32))

    def place_experts1(self):
        self.dn1 = self.sb("dn1", [P, E1, 4, P])

    def sb(self, name, shape, dt=F32):
        return self.ctx.enter_context(self.nc.sbuf_tensor(name, shape, dt))

    def sem(self, name):
        return self.nc.alloc_semaphore(name)

    def c(self, name, a=0, b=None):
        at, w = CONST[name]
        return self.const[:, at + a:at + (w if b is None else b)]


BQ0, BK0, BQ1, BK1, BQ1R, BK1R = range(6)
BV0, BO0, BV1, BO1, BPROJ = range(5)
CH_ROWS = ["wqg", "wql", "bqg", "bql", "wkg", "wkl", "bkg", "bkl", "bp"]
WQ, BQ, WK, BK, BP = 0, 2, 4, 6, 8
CH_COLS = ["wvg", "wvl", "bvg", "bvl", "wp"]
WV, BV, WP = 0, 2, 4
N_CHANNEL = 16 * (len(CH_ROWS) + len(CH_COLS))
N_FFN1 = 16 * E1


def setup(k, d):
    nc = k.nc
    with ExitStack() as ctx:
        sb = lambda n, s, dt=F32: ctx.enter_context(nc.sbuf_tensor(n, s, dt))
        raw = sb("raw_attn", [P, 8, P])
        raw_gu = sb("raw_gu", [P, 2 * (E0 + 1), 3, P])
        raw_dn = sb("raw_dn", [P, E0 + 1, I0])
        raw_wr = sb("raw_wr", [E0, P])
        bank = [ctx.enter_context(nc.psum_tensor(f"turn{i}", [P, 512], F32)) for i in range(4)]
        loaded_x = k.sem("loaded_x")
        loaded_attn = k.sem("loaded_attn")
        loaded_ffn = k.sem("loaded_ffn")
        cleared = k.sem("cleared")
        cast = k.sem("cast")
        turned = [k.sem(f"turned{i}") for i in range(4)]
        taken = [k.sem(f"taken{i}") for i in range(4)]
        attn_names = ["L0_attn_Wq", "L0_attn_Wk", "L0_attn_Wv", "L0_attn_Wo",
                      "L0_xattn_Wq", "L0_xattn_Wk", "L0_xattn_Wv", "L0_xattn_Wo"]
        cols = ["L0_attn_bq", "L0_attn_bk", "L0_xattn_bq", "L0_xattn_bk"]
        rows = ["L0_attn_bv", "L0_attn_bo", "L0_xattn_bv", "L0_xattn_bo", "L1_attn_b_proj"]
        n_attn, n_ffn = [0], [0]

        ident, rot = k.c("ident"), k.c("rot")

        def jobs():
            for base, dst, plan in ((0, k.w_sin, ((0, ident), (1, ident), (2, ident))),
                                    (4, k.w_rope, ((0, ident), (0, rot), (1, ident), (1, rot), (2, ident)))):
                for n0 in range(0, len(plan), 4):
                    part = plan[n0:n0 + 4]
                    yield ([(raw[:, base + m, :], by, (slice(0, P), slice(i * P, i * P + P)))
                            for i, (m, by) in enumerate(part)],
                           [((slice(0, P), slice(0, len(part) * P)),
                             dst[:, n0:n0 + len(part), :].rearrange("p a b -> p (a b)"))])
            for m, dst in ((3, k.w_sin[:, 3:5, :]), (7, k.w_rope[:, 5:7, :])):
                yield ([(raw[:, m, :], ident, (slice(0, P), slice(0, P)))],
                       [((slice(32 * g, 32 * g + 32), slice(0, P)), dst[64 * (g % 2):64 * (g % 2) + 32, g // 2, :])
                        for g in range(G)])
            yield ([(rot, k.bias_col[:, BQ1:BQ1 + 2], (slice(0, P), slice(0, 2))),
                    (raw_wr[:, :], ident[0:E0, 0:E0], (slice(0, P), slice(128, 128 + E0)))],
                   [((slice(0, P), slice(0, 2)), k.bias_col[:, BQ1R:BQ1R + 2]),
                    ((slice(0, P), slice(128, 128 + E0)), k.wr0[:, :])])
            for e in range(E0 + 1):
                for m in range(2):
                    yield ([(raw_gu[0:n, 2 * e + m, c, :], ident[0:n, 0:n], (slice(0, P), slice(a, a + n)))
                            for c, (a, n) in enumerate(CH0)],
                           [((slice(0, P), slice(0, I0)), k.gu0[:, e, m * W0:m * W0 + I0])])
                yield ([(raw_dn[:, e, a:a + n], ident, (slice(0, n), slice(c * P, c * P + P)))
                        for c, (a, n) in enumerate(CH0)],
                       [((slice(0, P), slice(0, 2 * P)), k.dn0[:, e, 0:2, :].rearrange("p a b -> p (a b)")),
                        ((slice(0, 96), slice(2 * P, 3 * P)), k.dn0[0:96, e, 2, :])])

        work = list(jobs())
        first_ffn = len(work) - 3 * (E0 + 1)
        block = ctx.enter_context(nc.Block())

        @block.sync
        def _(sp):
            for n in range(4):
                sp.dma_start(k.x[:, 8 * n:8 * n + 8, :], d["x"][8 * n:8 * n + 8, :, :].rearrange("b t d -> t b d")
                             ).then_inc(loaded_x, 16)
            sp.dma_start(k.const[:, :], d["const"]).then_inc(loaded_attn, 16)
            for m, n in enumerate(attn_names):
                sp.dma_start(raw[:, m, :], d[n]).then_inc(loaded_attn, 16)
            sp.dma_start(raw_wr[:, :], d["L0_ffn_wr"]).then_inc(loaded_attn, 16)
            n_attn[0] += 2 + len(attn_names)
            for m, n in enumerate(cols):
                sp.dma_start(k.bias_col[:, m:m + 1], d[n].rearrange("(p o) -> p o", o=1)).then_inc(loaded_attn, 16)
                n_attn[0] += 1
            for m, n in enumerate(rows):
                sp.dma_start(k.bias_row[:, m, :], d[n].rearrange("(o n) -> o n", o=1).partition_broadcast(P)
                             ).then_inc(loaded_attn, 16)
                n_attn[0] += 1
            for dst, n in ((k.rb0, "L0_ffn_rb"), (k.gate_b, "L1_ffn_gate_b")):
                sp.dma_start(dst[:, :], d[n].rearrange("(o n) -> o n", o=1).partition_broadcast(P)
                             ).then_inc(loaded_attn, 16)
                n_attn[0] += 1
            sp.dma_start(k.gate_w[:, :], d["L1_ffn_gate_w"]).then_inc(loaded_attn, 16)
            n_attn[0] += 1
            for m, n in enumerate(("L1_attn_wq_lat", "L1_attn_wk_lat", "L1_attn_wv_lat")):
                sp.dma_start(k.w_lat[:, m * LAT:(m + 1) * LAT], d[n]).then_inc(loaded_attn, 16)
                n_attn[0] += 1
            sp.wait_ge(cleared, 2)
            for m, n in enumerate(("L1_attn_wq_heads", "L1_attn_wk_heads", "L1_attn_wv_heads")):
                sp.dma_start(k.w_heads[m * LAT:(m + 1) * LAT, m, :], d[n]).then_inc(loaded_attn, 16)
                n_attn[0] += 1
            for g in range(G):
                sp.dma_start(k.w_proj[64 * (g % 2):64 * (g % 2) + 32, g // 2, :],
                             d["L1_attn_w_proj"][32 * g:32 * g + 32, :]).then_inc(loaded_attn, 16)
                n_attn[0] += 1
            for m, n in enumerate(CH_ROWS):
                sp.dma_start(k.ch_row[:, m, :], d["L1_xattn_" + n].rearrange("(o n) -> o n", o=1).partition_broadcast(P)
                             ).then_inc(k.loaded_channel, 16)
            for m, n in enumerate(CH_COLS):
                sp.dma_start(k.ch_col[:, m:m + 1], d["L1_xattn_" + n].rearrange("(p o) -> p o", o=1)
                             ).then_inc(k.loaded_channel, 16)
            sp.wait_ge(loaded_x, 64)

        @block.scalar
        def _(act):
            for s, n in enumerate(("g", "u")):
                for e in range(E0):
                    act.dma_start(raw_gu[:, 2 * e + s, 0:2, :],
                                  d["L0_ffn_r" + n][e, 0:256, :].rearrange("(c p) h -> p c h", p=P)
                                  ).then_inc(loaded_ffn, 16)
                    act.dma_start(raw_gu[0:96, 2 * e + s, 2, :], d["L0_ffn_r" + n][e, 256:I0, :]).then_inc(loaded_ffn, 16)
                act.dma_start(raw_gu[:, 2 * E0 + s, 0:2, :],
                              d["L0_ffn_s" + n][0:256, :].rearrange("(c p) h -> p c h", p=P)).then_inc(loaded_ffn, 16)
                act.dma_start(raw_gu[0:96, 2 * E0 + s, 2, :], d["L0_ffn_s" + n][256:I0, :]).then_inc(loaded_ffn, 16)
                n_ffn[0] += 2 * (E0 + 1)
            act.dma_start(raw_dn[:, 0:E0, :], d["L0_ffn_rd"].rearrange("e h i -> h e i")).then_inc(loaded_ffn, 16)
            act.dma_start(raw_dn[:, E0, :], d["L0_ffn_sd"]).then_inc(loaded_ffn, 16)
            n_ffn[0] += 2
            act.wait_ge(cleared, 4)
            for n in range(1, len(work), 2):
                b = n % 4
                act.wait_ge(turned[b], n // 4 + 1)
                for i, (s, dst) in enumerate(work[n][1]):
                    ins = nc.scalar.copy(dst, bank[b][s[0], s[1]])
                ins.then_inc(taken[b], 1)

        @block.gpsimd
        def _(pool):
            nc.gpsimd.memset(k.w_heads[:, :, :], 0.0).then_inc(cleared, 1)
            nc.gpsimd.memset(k.w_proj[:, :, :], 0.0).then_inc(cleared, 1)
            nc.gpsimd.memset(k.w_sin[:, :, :], 0.0).then_inc(cleared, 1)
            nc.gpsimd.memset(k.w_rope[:, :, :], 0.0).then_inc(cleared, 1)
            nc.gpsimd.memset(k.gu0[:, :, I0:W0], 0.0).then_inc(cleared, 1)
            nc.gpsimd.memset(k.gu0[:, :, W0 + I0:], 0.0).then_inc(cleared, 1)
            pool.wait_ge(cleared, 6)
            nc.gpsimd.memset(k.dn0[96:P, :, 2, :], 0.0).then_inc(cleared, 1)

        @block.tensor
        def _(pe):
            pe.wait_ge(loaded_attn, 16 * n_attn[0])
            for n, (turns, _) in enumerate(work):
                b = n % 4
                if n == first_ffn:
                    pe.wait_ge(loaded_ffn, 16 * n_ffn[0])
                if n >= 4:
                    pe.wait_ge(taken[b], n // 4)
                for w, by, (r, c) in turns:
                    ins = nc.tensor.matmul(bank[b][r, c], w, by, start=True, stop=True)
                ins.then_inc(turned[b], 1)

        @block.vector
        def _(dve):
            dve.wait_ge(loaded_attn, 16 * n_attn[0])
            for dst, n in ((k.ident_bf, "ident"), (k.ones_bf, "ones"), (k.before_bf, "before"),
                           (k.causal_qk_bf, "causal_qk"), (k.causal_kq_bf, "causal_kq"),
                           (k.blocks_bf, "blocks"), (k.ones_r, "ones")):
                nc.vector.tensor_copy(dst[:, :], k.c(n)).then_inc(cast, 1)
            dve.wait_ge(cleared, 4)
            for n in range(0, len(work), 2):
                b = n % 4
                dve.wait_ge(turned[b], n // 4 + 1)
                for s, dst in work[n][1]:
                    ins = nc.vector.tensor_copy(dst, bank[b][s[0], s[1]])
                ins.then_inc(taken[b], 1)


class Turn:

    def __init__(self, n, loop=None):
        self.n, self.loop = n, loop

    def count(self, first, per):
        return first if self.loop is None else self.loop * (2 * per) + first

    def pairs(self, ahead, per=1, plus=0):
        return self.count((self.n + ahead) * per + plus, per)


def head_attention(k, kind, ctx_in):
    nc = k.nc
    softmax = kind != "sine"
    with ExitStack() as ctx:
        sb = lambda n, s, dt=F32: ctx.enter_context(nc.sbuf_tensor(f"{kind}_{n}", s, dt))
        ps = lambda n, s: ctx.enter_context(nc.psum_tensor(f"{kind}_{n}", s, F32))
        sem = lambda n: k.sem(f"{kind}_{n}")
        two = lambda n, s, dt=F32: [sb(f"{n}{i}", s, dt) for i in range(2)]
        scores = [ps("scores0", [P, 1024]), ps("scores1", [P, 1024])]
        bank = {n: ps("bank" + n, [P, 512]) for n in "ABCD"}
        xT = two("xT", [P, 512])
        latT = two("latT", [P, 256]) if kind == "causal" else None
        q4 = two("q4", [P, J, 256])
        kg = two("kg", [P, G, 256])
        vb = [[sb(f"vb{i}{s}", [P, G, J, VW]) for s in range(2)] for i in range(2)]
        xin = sb("xin", [P, 2, P])
        cin = sb("cin", [P, 2, P]) if ctx_in is not None else None
        rot = [sb(f"rot{i}", [P, 256]) for i in range(6)] if kind == "rope" else None
        rnd = two("rnd", [P, 1024]) if kind == "sine" else None
        probs = two("probs", [P, H * P])
        if softmax:
            q4_r = sb("q4_r", [P, J, 256], F32R)
            kg_r = sb("kg_r", [P, G, 256], F32R)
            negmax = two("negmax", [P, H])
            negmaxT = two("negmaxT", [H, P], F32R)
            shift = two("shift", [P, H * P], F32R)
            osum = two("osum", [P, 256])
            recip = two("recip", [P, 256])
        onorm = two("onorm", [P, 256])
        xres = two("xres", [P, P])
        z = two("z", [P, P])
        stats = two("stats", [P, 6])
        mv = two("mv", [P, 2])
        vare = two("vare", [P, 1])
        rstd = two("rstd", [P, 1])
        spare = two("spare", [P, 1])
        mhalf = sb("mhalf", [P, 1])
        warm = sb("warm", [P, 2])

        has = lambda pair: 0 <= pair < NPAIR

        def uses(b, n):
            p, m, v = has(n + 2), has(n + 1) and softmax, has(n + 1)
            o1, o0 = has(n - 1), has(n)
            return {"A": ["m00", "m02"] * m + ["lat"] * (p and kind == "causal") + ["m10", "m12"] * m + ["q"] * p,
                    "B": ["m01", "m03", "m11", "m13"] * m + ["k"] * p,
                    "C": ["y0"] * o1 + ["xT"] * p + ["nm0"] * m + ["y1"] * o1 + ["nm1"] * m + ["v"] * v,
                    "D": (["pv1"] + ["sum1"] * softmax) * o1 + (["pv0"] + ["sum0"] * softmax) * o0}[b]

        full = {n: sem("full" + n) for n in "ABCD"}
        empty = {n: sem("empty" + n) for n in "ABCD"}

        def nth(b, use, t):
            first = sum(len(uses(b, n)) for n in range(-2, t.n)) + uses(b, t.n).index(use)
            return t.count(first, len(uses(b, 2)))

        x_loaded = sem("x_loaded")
        rotated = sem("rotated")
        q_ready = sem("q_ready")
        k_ready = sem("k_ready")
        qr_ready = sem("qr_ready")
        kr_ready = sem("kr_ready")
        shift_loaded = [sem(f"shift_loaded{i}") for i in range(2)]
        scores_full = [sem(f"scores_full{i}") for i in range(2)]
        rounded = [sem(f"rounded{i}") for i in range(2)]
        frac_ready = [sem(f"frac_ready{i}") for i in range(2)]
        probs_ready = [sem(f"probs_ready{i}") for i in range(2)]
        onorm_ready = sem("onorm_ready")
        xres_ready = sem("xres_ready")
        z_ready = sem("z_ready")
        stats_ready = sem("stats_ready")
        var_ready = sem("var_ready")
        vare_ready = sem("vare_ready")
        rstd_ready = sem("rstd_ready")
        x_ready = sem("x_ready")
        warmed = sem("warmed")
        kg_zero = sem("kg_zero")
        shift_zero = sem("shift_zero")
        vb_zero = sem("vb_zero")
        vb_set = sem("vb_set")
        half_set = sem("half_set")
        scores_empty = probs_ready if softmax else frac_ready

        def wait(engine, semaphore, value):
            if not isinstance(value, int) or value > 0:
                engine.wait_ge(semaphore, value)

        def value_blocks(i, s):
            return bass.AP(vb[i][s], 0, [[G * J * VW, P], [J * VW, G], [VW + HD, J], [1, HD]])

        def sum_columns(i, s):
            return bass.AP(vb[i][s], 32, [[G * J * VW, P], [J * VW, G], [VW + 1, J]])

        def state(t, ahead, s):
            at = t.pairs(ahead, 2, s)
            rows = k.x[:, at:at + 1, :] if isinstance(at, int) else k.x[:, bass.ds(at, 1), :]
            return rows.rearrange("p o d -> p (o d)")

        n_in = 2 if ctx_in is not None else 1
        w, cst = (k.w_sin if kind == "sine" else k.w_rope), k.c
        w_out = {"sine": k.w_sin[:, 3:5, :], "rope": k.w_rope[:, 5:7, :], "causal": k.w_proj[:, :, :]}[kind]
        b_out = {"sine": BO0, "rope": BO1, "causal": BPROJ}[kind]
        LOOP0, LOOP1 = 2, NPAIR - 2
        block = ctx.enter_context(nc.Block())

        def all_turns(engine, turn, start_loop=None):
            for n in range(-2, LOOP0):
                turn(Turn(n))
            with engine.Fori(0, (LOOP1 - LOOP0) // 2) as i:
                if start_loop is not None:
                    start_loop(i)
                turn(Turn(LOOP0, i))
                turn(Turn(LOOP0 + 1, i))
            for n in range(LOOP1, NPAIR + 1):
                turn(Turn(n))

        @block.sync
        def _(sp):
            def turn(t):
                if not has(t.n + 2):
                    return
                if has(t.n + 1):
                    sp.wait_ge(full["C"], nth("C", "xT", Turn(t.n - 1, t.loop)) + 1)
                pair = bass.ds(t.pairs(2, 2), 2)
                sp.dma_start(xin[:, :, :], k.x[:, pair, :]).then_inc(x_loaded, 16)
                if ctx_in is not None:
                    sp.dma_start(cin[:, :, :], ctx_in[pair, :, :].rearrange("b t d -> t b d")).then_inc(x_loaded, 16)

            all_turns(sp, turn)
            sp.wait_ge(x_loaded, 16 * n_in * NPAIR)

        @block.tensor
        def _(pe):
            def transposes(t):
                pe.wait_ge(x_loaded, t.pairs(3, 16 * n_in))
                wait(pe, empty["C"], nth("C", "xT", t))
                for m, src in enumerate((xin, cin)[:n_in]):
                    for s in range(2):
                        ins = nc.tensor.transpose(bank["C"][:, (2 * m + s) * P:(2 * m + s + 1) * P],
                                                  src[:, s, :], cst("ident"))
                ins.then_inc(full["C"], 1)

            def project_lat(t):
                pe.wait_ge(empty["C"], nth("C", "xT", t) + 1)
                wait(pe, empty["A"], nth("A", "lat", t))
                nc.tensor.matmul(bank["A"][0:3 * LAT, 0:256], k.w_lat[:, :], xT[t.n % 2][:, 0:256],
                                 start=True, stop=True).then_inc(full["A"], 1)

            def project_qk(t):
                p = t.n % 2
                if kind != "causal":
                    pe.wait_ge(empty["C"], nth("C", "xT", t) + 1)
                wait(pe, empty["A"], nth("A", "q", t))
                src_q, src_k = xT[p][:, 0:256], xT[p][:, 256 * (n_in - 1):256 * n_in]
                if kind == "causal":
                    latent = latT[p][0:3 * LAT, :]
                    nc.tensor.matmul(bank["A"][:, 0:256], k.w_heads[0:3 * LAT, 0, :], latent, start=True, stop=True
                                     ).then_inc(full["A"], 1)
                    wait(pe, empty["B"], nth("B", "k", t))
                    nc.tensor.matmul(bank["B"][:, 0:256], k.w_heads[0:3 * LAT, 1, :], latent, start=True, stop=True
                                     ).then_inc(full["B"], 1)
                elif kind == "rope":
                    nc.tensor.matmul(bank["A"][:, 0:256], w[:, 0, :], src_q, start=True, stop=True)
                    nc.tensor.matmul(bank["A"][:, 256:512], w[:, 1, :], src_q, start=True, stop=True
                                     ).then_inc(full["A"], 1)
                    wait(pe, empty["B"], nth("B", "k", t))
                    nc.tensor.matmul(bank["B"][:, 0:256], w[:, 2, :], src_k, start=True, stop=True)
                    nc.tensor.matmul(bank["B"][:, 256:512], w[:, 3, :], src_k, start=True, stop=True
                                     ).then_inc(full["B"], 1)
                else:
                    nc.tensor.matmul(bank["A"][:, 0:256], w[:, 0, :], src_q, start=True, stop=True
                                     ).then_inc(full["A"], 1)
                    wait(pe, empty["B"], nth("B", "k", t))
                    nc.tensor.matmul(bank["B"][:, 0:256], w[:, 1, :], src_k, start=True, stop=True
                                     ).then_inc(full["B"], 1)

            def project_v(t):
                p = (t.n + 1) % 2
                pe.wait_ge(empty["C"], nth("C", "v", t))
                for s in range(2):
                    if kind == "causal":
                        src, wv = latT[p][0:3 * LAT, s * P:(s + 1) * P], k.w_heads[0:3 * LAT, 2, :]
                    else:
                        at = 256 * (n_in - 1) + s * P
                        src, wv = xT[p][:, at:at + P], w[:, 4 if kind == "rope" else 2, :]
                    ins = nc.tensor.matmul(bank["C"][:, s * P:(s + 1) * P], src, wv, start=True, stop=True)
                ins.then_inc(full["C"], 1)

            def row_scores(t, s, j0):
                if s == 0 and j0 == 0:
                    pe.wait_ge(qr_ready, t.pairs(2))
                    pe.wait_ge(kr_ready, t.pairs(2))
                for j in (j0, j0 + 1):
                    b = "AB"[j % 2]
                    pe.wait_ge(empty[b], nth(b, f"m{s}{j}", t))
                    ins = nc.tensor.matmul(bank[b][:, :], q4_r[:, j, s * P:(s + 1) * P], kg_r[:, :, s * P:(s + 1) * P],
                                           start=True, stop=kind != "causal")
                    if kind == "causal":
                        ins = nc.tensor.matmul(bank[b][:, :], k.ident_bf[:, :],
                                               k.causal_qk_bf[:, :].unsqueeze(1).to_broadcast([P, 4, P]),
                                               start=False, stop=True)
                    ins.then_inc(full[b], 1)

            def turn_maxima(t, s):
                pe.wait_ge(empty["B"], nth("B", f"m{s}3", t) + 1)
                pe.wait_ge(empty["C"], nth("C", f"nm{s}", t))
                nc.tensor.transpose(bank["C"][0:H, 0:P], negmax[s][:, :], cst("ident")).then_inc(full["C"], 1)

            def key_scores(t, s, half):
                p = t.n % 2
                if softmax and half == 0:
                    pe.wait_ge(shift_loaded[s], t.pairs(1, 16))
                elif s == 0 and half == 0:
                    pe.wait_ge(empty["A"], nth("A", "q", Turn(t.n - 2, t.loop)) + 1)
                    pe.wait_ge(empty["B"], nth("B", "k", Turn(t.n - 2, t.loop)) + 1)
                wait(pe, scores_empty[half], t.pairs(0, 2, s))
                for g in (2 * half, 2 * half + 1):
                    out = scores[half][:, (g % 2) * 512:(g % 2 + 1) * 512]
                    ins = nc.tensor.matmul(out, kg[p][:, g, s * P:(s + 1) * P], q4[p][:, :, s * P:(s + 1) * P],
                                           start=True, stop=not softmax)
                    if kind == "causal":
                        nc.tensor.matmul(out, k.ident_bf[:, :],
                                         k.causal_kq_bf[:, :].unsqueeze(1).to_broadcast([P, 4, P]),
                                         start=False, stop=False)
                    if softmax:
                        ins = nc.tensor.matmul(out, k.ones_r[:, :], shift[s][:, g * 512:(g + 1) * 512],
                                               start=False, stop=True)
                ins.then_inc(scores_full[half], 1)

            def values(t, ahead, s):
                p = (t.n + ahead) % 2
                wait(pe, empty["D"], nth("D", f"pv{s}", t))
                for r in range(2):
                    pe.wait_ge(probs_ready[r], t.pairs(ahead, 2, s + 1))
                    for j in range(J):
                        for a in range(2):
                            h = 4 * (2 * r + a) + j
                            ins = nc.tensor.matmul(bank["D"][64 * a:64 * a + 64, r * P:(r + 1) * P],
                                                   vb[p][s][:, 2 * r + a, j, :], probs[s][:, h * P:(h + 1) * P],
                                                   start=(j == 0), stop=(j == J - 1))
                ins.then_inc(full["D"], 1)

            def repeat_sums(t, s):
                pe.wait_ge(empty["D"], nth("D", f"sum{s}", t))
                nc.tensor.matmul(bank["D"][:, 256:512], cst("sumrep"), osum[s][:, :], start=True, stop=True
                                 ).then_inc(full["D"], 1)

            def project_out(t, ahead, s):
                if softmax:
                    pe.wait_ge(onorm_ready, t.pairs(ahead, 2, s + 1))
                else:
                    pe.wait_ge(empty["D"], nth("D", f"pv{s}", t if s == 1 else Turn(t.n - 1, t.loop)) + 1)
                wait(pe, empty["C"], nth("C", f"y{s}", t))
                for r in range(2):
                    ins = nc.tensor.matmul(bank["C"][:, 0:P], onorm[s][:, r * P:(r + 1) * P], w_out[:, r, :],
                                           start=(r == 0), stop=(r == 1))
                ins.then_inc(full["C"], 1)

            def turn(t):
                p, m, v, o1, o0 = has(t.n + 2), has(t.n + 1) and softmax, has(t.n + 1), has(t.n - 1), has(t.n)
                if o0:
                    key_scores(t, 0, 0)
                    key_scores(t, 0, 1)
                if o1:
                    project_out(t, -1, 0)
                if m:
                    row_scores(t, 0, 0)
                if o1:
                    values(t, -1, 1)
                if m:
                    row_scores(t, 0, 2)
                if p:
                    transposes(t)
                if o1 and softmax:
                    repeat_sums(t, 1)
                if o0:
                    key_scores(t, 1, 0)
                if p and kind == "causal":
                    project_lat(t)
                if m:
                    turn_maxima(t, 0)
                    row_scores(t, 1, 0)
                if o0:
                    key_scores(t, 1, 1)
                if m:
                    row_scores(t, 1, 2)
                if o1:
                    project_out(t, -1, 1)
                if p:
                    project_qk(t)
                if m:
                    turn_maxima(t, 1)
                if o0:
                    values(t, 0, 0)
                if v:
                    project_v(t)
                if o0 and softmax:
                    repeat_sums(t, 0)

            all_turns(pe, turn)

        @block.scalar
        def _(act):
            def take_xT(t):
                act.wait_ge(full["C"], nth("C", "xT", t) + 1)
                nc.scalar.copy(xT[t.n % 2][:, 0:256 * n_in], bank["C"][:, 0:256 * n_in]).then_inc(empty["C"], 1)

            def take_k(t):
                if kind == "rope":
                    act.wait_ge(rotated, t.pairs(3, 2))
                else:
                    act.wait_ge(full["B"], nth("B", "k", t) + 1)
                blocks = [(slice(32 * g, 32 * g + 32), g) for g in range(G)]
                src = rot[5] if kind == "rope" else bank["B"]
                if softmax:
                    for rows, g in blocks:
                        ins = nc.scalar.copy(kg_r[rows, g, :], src[rows, 0:256])
                    ins.then_inc(kr_ready, 1)
                for rows, g in blocks:
                    dst = kg[t.n % 2][rows, g, :]
                    if kind == "sine":
                        ins = nc.scalar.activation(dst, src[rows, 0:256], ACT.Identity,
                                                   bias=k.bias_col[rows, BK0:BK0 + 1])
                    else:
                        ins = nc.scalar.copy(dst, src[rows, 0:256])
                ins.then_inc(k_ready if kind == "rope" else empty["B"], 1)

            def take_v(t):
                act.wait_ge(full["C"], nth("C", "v", t) + 1)
                for s in range(2):
                    ins = nc.scalar.copy(value_blocks((t.n + 1) % 2, s), bank["C"][:, s * P:(s + 1) * P]
                                         .rearrange("p (g j d) -> p g j d", g=G, j=J))
                ins.then_inc(empty["C"], 1)

            def take_maxima(t, s):
                act.wait_ge(full["C"], nth("C", f"nm{s}", t) + 1)
                nc.scalar.copy(negmaxT[s][:, :], bank["C"][0:H, 0:P]).then_inc(empty["C"], 1)
                act.wait_ge(empty["C"], nth("C", f"nm{s}", t) + 1)
                act.dma_start(shift[s][0:1, :].bitcast(F32).rearrange("o (h q) -> o h q", q=P),
                              negmaxT[s][:, :].bitcast(F32)).then_inc(shift_loaded[s], 16)

            def exps(t, s, half):
                act.wait_ge(scores_full[half], t.pairs(0, 2, s + 1))
                nc.scalar.activation(probs[s][:, half * 1024:(half + 1) * 1024], scores[half][:, :], ACT.Exp,
                                     scale=HD ** -0.5).then_inc(probs_ready[half], 1)

            def take_out(t, s):
                act.wait_ge(full["D"], nth("D", f"pv{s}", t) + 1)
                nc.scalar.copy((osum if softmax else onorm)[s][:, :], bank["D"][:, 0:256]
                               ).then_inc(empty["D"], 1)

            def rounds(t, s):
                for half in range(2):
                    wait(act, probs_ready[half], t.pairs(0, 2, s))
                    act.wait_ge(scores_full[half], t.pairs(0, 2, s + 1))
                    nc.scalar.activation(rnd[half][:, :], scores[half][:, :], ACT.Copy, bias=MAGIC
                                         ).then_inc(rounded[half], 1)

            def sines(t, s):
                for half in range(2):
                    act.wait_ge(frac_ready[half], t.pairs(0, 2, s + 1))
                    nc.scalar.activation(probs[s][:, half * 1024:(half + 1) * 1024], rnd[half][:, :], ACT.Sin,
                                         scale=float(-2 * np.pi)).then_inc(probs_ready[half], 1)

            def turn(t):
                p, m, v, o1, o0 = has(t.n + 2), has(t.n + 1) and softmax, has(t.n + 1), has(t.n - 1), has(t.n)
                if o0:
                    if softmax:
                        exps(t, 0, 0)
                        exps(t, 0, 1)
                    else:
                        rounds(t, 0)
                        sines(t, 0)
                if o1:
                    take_out(t, 1)
                if p:
                    take_xT(t)
                if o0:
                    exps(t, 1, 0) if softmax else rounds(t, 1)
                if m:
                    take_maxima(t, 0)
                if o0:
                    exps(t, 1, 1) if softmax else sines(t, 1)
                if m:
                    take_maxima(t, 1)
                if p and not softmax:
                    take_k(t)
                if o0:
                    take_out(t, 0)
                if v and kind == "causal":
                    take_v(t)
                if p and softmax:
                    take_k(t)

            def name_table(i):
                act.wait_ge(warmed, i + 1)
                nc.scalar.activation(warm[:, 1:2], cst("ident", 0, 1), ACT.Exp if softmax else ACT.Sin
                                     ).then_inc(warmed, 1)

            act.wait_ge(kg_zero, 3 if softmax else 2)
            if softmax:
                act.wait_ge(shift_zero, 2)
            act.wait_ge(vb_set, 4)
            nc.scalar.copy(warm[:, 0:1], cst("ident", 0, 1)).then_inc(warmed, 1)
            all_turns(act, turn, name_table)

        @block.gpsimd
        def _(pool):
            def residual(t, ahead, s):
                wait(pool, x_ready, t.pairs(ahead, 2, s - 1))
                nc.gpsimd.tensor_tensor(xres[s][:, :], state(t, ahead, s), k.bias_row[:, b_out, :], ALU.add
                                        ).then_inc(xres_ready, 1)

            def inverse_deviation(t, ahead, s):
                pool.wait_ge(vare_ready, t.pairs(ahead, 2, s + 1))
                nc.gpsimd.tensor_tensor(rstd[s][:, :], vare[s][:, :], mhalf[:, :], ALU.pow).then_inc(rstd_ready, 1)

            unit = cst("ones", 0, 1).unsqueeze(2).to_broadcast([P, J, 256])

            def round_queries(t):
                if kind == "rope":
                    pool.wait_ge(q_ready, t.pairs(3))
                else:
                    pool.wait_ge(empty["A"], nth("A", "q", t) + 1)
                nc.gpsimd.tensor_tensor(q4_r[:, :, :], q4[t.n % 2][:, :, :], unit, ALU.mult
                                        ).then_inc(qr_ready, 1)

            def turn(t):
                p, o1 = has(t.n + 2), has(t.n - 1)
                if o1:
                    residual(t, -1, 0)
                    residual(t, -1, 1)
                    inverse_deviation(t, -1, 0)
                    inverse_deviation(t, -1, 1)
                if p and softmax:
                    round_queries(t)

            for i in range(2):
                nc.gpsimd.memset(kg[i][:, :, :], 0.0).then_inc(kg_zero, 1)
            if softmax:
                nc.gpsimd.memset(kg_r[:, :, :].bitcast(F32), 0.0).then_inc(kg_zero, 1)
                for s in range(2):
                    nc.gpsimd.memset(shift[s][:, :].bitcast(F32), 0.0).then_inc(shift_zero, 1)
            nc.gpsimd.memset(mhalf[:, :], -0.5).then_inc(half_set, 1)
            pool.wait_ge(half_set, 1)
            all_turns(pool, turn)

        @block.vector
        def _(dve):
            def maxima(t, s):
                for j in range(J):
                    b = "AB"[j % 2]
                    dve.wait_ge(full[b], nth(b, f"m{s}{j}", t) + 1)
                    nc.vector.tensor_reduce(negmax[s][:, j::4], bank[b][:, :].rearrange("p (g t) -> p g t", g=G),
                                            AX.X, ALU.max, negate=True).then_inc(empty[b], 1)

            def take_lat(t):
                dve.wait_ge(full["A"], nth("A", "lat", t) + 1)
                nc.vector.tensor_copy(latT[t.n % 2][0:3 * LAT, :], bank["A"][0:3 * LAT, 0:256]
                                      ).then_inc(empty["A"], 1)

            def take_q(t):
                p = t.n % 2
                if kind == "rope":
                    wait(dve, q_ready, t.pairs(2))
                    wait(dve, k_ready, t.pairs(2))
                    dve.wait_ge(full["A"], nth("A", "q", t) + 1)
                    nc.vector.scalar_tensor_tensor(rot[0][:, :], bank["A"][:, 0:256], k.bias_col[:, BQ1:BQ1 + 1],
                                                   cst("cos"), ALU.add, ALU.mult)
                    nc.vector.scalar_tensor_tensor(rot[1][:, :], bank["A"][:, 256:512], k.bias_col[:, BQ1R:BQ1R + 1],
                                                   cst("sin"), ALU.add, ALU.mult).then_inc(empty["A"], 1)
                    dve.wait_ge(full["B"], nth("B", "k", t) + 1)
                    nc.vector.scalar_tensor_tensor(rot[3][:, :], bank["B"][:, 0:256], k.bias_col[:, BK1:BK1 + 1],
                                                   cst("cos"), ALU.add, ALU.mult)
                    nc.vector.scalar_tensor_tensor(rot[4][:, :], bank["B"][:, 256:512], k.bias_col[:, BK1R:BK1R + 1],
                                                   cst("sin"), ALU.add, ALU.mult).then_inc(empty["B"], 1)
                    dve.wait_ge(empty["B"], nth("B", "k", t) + 1)
                    nc.vector.tensor_tensor(rot[2][:, :], rot[0][:, :], rot[1][:, :], ALU.add).then_inc(rotated, 1)
                    nc.vector.tensor_tensor(rot[5][:, :], rot[3][:, :], rot[4][:, :], ALU.add).then_inc(rotated, 1)
                    dve.wait_ge(rotated, t.pairs(3, 2))
                else:
                    dve.wait_ge(full["A"], nth("A", "q", t) + 1)
                for j in range(J):
                    if kind == "sine":
                        ins = nc.vector.tensor_scalar(q4[p][:, j, :], bank["A"][:, 0:256], k.bias_col[:, BQ0:BQ0 + 1],
                                                      cst("maskc", j, j + 1), ALU.add, ALU.mult)
                    else:
                        ins = nc.vector.tensor_scalar(q4[p][:, j, :], rot[2][:, :] if kind == "rope" else bank["A"][:, 0:256],
                                                      cst("mask", j, j + 1), None, ALU.mult)
                ins.then_inc(q_ready if kind == "rope" else empty["A"], 1)

            def take_v(t):
                dve.wait_ge(full["C"], nth("C", "v", t) + 1)
                bias = k.bias_row[:, BV0 if kind == "sine" else BV1, :].rearrange("p (g j d) -> p g j d", g=G, j=J)
                for s in range(2):
                    ins = nc.vector.tensor_tensor(value_blocks((t.n + 1) % 2, s), bank["C"][:, s * P:(s + 1) * P]
                                                  .rearrange("p (g j d) -> p g j d", g=G, j=J), bias, ALU.add)
                ins.then_inc(empty["C"], 1)

            def fractions(t, s):
                for half in range(2):
                    dve.wait_ge(rounded[half], t.pairs(0, 2, s + 1))
                    nc.vector.scalar_tensor_tensor(rnd[half][:, :], rnd[half][:, :], -MAGIC, scores[half][:, :],
                                                   ALU.add, ALU.subtract).then_inc(frac_ready[half], 1)

            def normalise(t, s):
                dve.wait_ge(full["D"], nth("D", f"sum{s}", t) + 1)
                nc.vector.reciprocal(recip[s][:, :], bank["D"][:, 256:512]).then_inc(empty["D"], 1)
                dve.wait_ge(empty["D"], nth("D", f"sum{s}", t) + 1)
                nc.vector.tensor_tensor(onorm[s][:, :], osum[s][:, :], recip[s][:, :], ALU.mult).then_inc(onorm_ready, 1)

            def add_residual(t, ahead, s):
                wait(dve, x_ready, t.pairs(ahead, 2, s - 1))
                dve.wait_ge(full["C"], nth("C", f"y{s}", t) + 1)
                dve.wait_ge(xres_ready, t.pairs(ahead, 2, s + 1))
                nc.vector.tensor_tensor(z[s][:, :], bank["C"][:, 0:P], xres[s][:, :], ALU.add).then_inc(empty["C"], 1)
                dve.wait_ge(empty["C"], nth("C", f"y{s}", t) + 1)
                nc.vector.bn_stats(stats[s][:, :], z[s][:, :]).then_inc(stats_ready, 1)
                dve.wait_ge(stats_ready, t.pairs(ahead, 2, s + 1))
                nc.vector.tensor_copy(spare[s][:, :], cst("ident", 0, 1))
                nc.vector.bn_aggr(mv[s][:, :], stats[s][:, :]).then_inc(var_ready, 1)
                dve.wait_ge(var_ready, t.pairs(ahead, 2, s + 1))
                nc.vector.tensor_scalar(vare[s][:, :], mv[s][:, 1:2], EPS, None, ALU.add).then_inc(vare_ready, 1)

            def layer_norm(t, ahead, s):
                dve.wait_ge(rstd_ready, t.pairs(ahead, 2, s + 1))
                nc.vector.tensor_scalar(state(t, ahead, s), z[s][:, :], mv[s][:, 0:1], rstd[s][:, :],
                                        ALU.subtract, ALU.mult).then_inc(x_ready, 1)

            def turn(t):
                p, m, v, o1, o0 = has(t.n + 2), has(t.n + 1) and softmax, has(t.n + 1), has(t.n - 1), has(t.n)
                if o0 and not softmax:
                    fractions(t, 0)
                if o1:
                    add_residual(t, -1, 0)
                if m:
                    maxima(t, 0)
                if o1 and softmax:
                    normalise(t, 1)
                if p and kind == "causal":
                    take_lat(t)
                if o1:
                    layer_norm(t, -1, 0)
                if m:
                    maxima(t, 1)
                if o0 and not softmax:
                    fractions(t, 1)
                if o1:
                    add_residual(t, -1, 1)
                if p:
                    take_q(t)
                if o1:
                    layer_norm(t, -1, 1)
                if v and kind != "causal":
                    take_v(t)
                if o0 and softmax:
                    normalise(t, 0)

            for i in range(2):
                for s in range(2):
                    nc.vector.memset(vb[i][s][:, :, :, :], 0.0).then_inc(vb_zero, 1)
            dve.wait_ge(vb_zero, 4)
            for i in range(2):
                for s in range(2):
                    nc.vector.memset(sum_columns(i, s), 1.0).then_inc(vb_set, 1)
            dve.wait_ge(vb_set, 4)
            all_turns(dve, turn)


def channel_attention(k, ctx_in):
    nc = k.nc
    with ExitStack() as ctx:
        sb = lambda n, s, dt=F32: ctx.enter_context(nc.sbuf_tensor(f"channel_{n}", s, dt))
        ps = lambda n: ctx.enter_context(nc.psum_tensor(f"channel_{n}", [P, 512], F32))
        sem = lambda n: k.sem(f"channel_{n}")
        scores, turned_ctx, turned_attn, attended = ps("scores"), ps("turned_ctx"), ps("turned_attn"), ps("attended")
        cin = sb("cin", [P, 2, P])
        qp = sb("qp", [P, 2, 2, P])
        q = sb("q", [P, 2, 2, P])
        kp = sb("kp", [P, 2, 2, P])
        key = sb("key", [P, 2, 2, P])
        vT = sb("vT", [P, 2, 2, P])
        xres = sb("xres", [P, 2, P])
        negmax = sb("negmax", [P, 4])
        shift = sb("shift", [P, 4])
        ex = sb("ex", [P, 4, P])
        sums = sb("sums", [P, 4])
        recip = sb("recip", [P, 4])
        factor = sb("factor", [P, 4])
        attn = sb("attn", [P, 4, P])
        attnT = sb("attnT", [P, 4, P])
        z = sb("z", [P, 2, P])
        stats = sb("stats", [P, 2, 6])
        mv = sb("mv", [P, 2, 2])
        vare = sb("vare", [P, 2])
        rstd = sb("rstd", [P, 2])
        mhalf = sb("mhalf", [P, 2])

        c_loaded = sem("c_loaded")
        qp_ready = sem("qp_ready")
        q_ready = sem("q_ready")
        kp_ready = sem("kp_ready")
        key_ready = sem("key_ready")
        v_ready = sem("v_ready")
        xres_ready = sem("xres_ready")
        ctx_turned = sem("ctx_turned")
        scores_full = sem("scores_full")
        attn_turned = sem("attn_turned")
        out_full = sem("out_full")
        max_ready = sem("max_ready")
        shift_ready = sem("shift_ready")
        ex_ready = sem("ex_ready")
        sums_ready = sem("sums_ready")
        recip_ready = sem("recip_ready")
        factor_ready = sem("factor_ready")
        attn_ready = sem("attn_ready")
        attnT_ready = sem("attnT_ready")
        z_ready = sem("z_ready")
        stats_ready = sem("stats_ready")
        var_ready = sem("var_ready")
        vare_ready = sem("vare_ready")
        rstd_ready = sem("rstd_ready")
        x_ready = sem("x_ready")
        init = sem("init")
        LAST = NPAIR - 1
        scale = P ** -0.5
        rows = lambda m: k.ch_row[:, m:m + 2, :].unsqueeze(1).to_broadcast([P, 2, 2, P])
        block = ctx.enter_context(nc.Block())


        @block.sync
        def _(sp):
            def load(n):
                sp.dma_start(cin[:, :, :], ctx_in[bass.ds(n * 2, 2), :, :].rearrange("b t d -> t b d")
                             ).then_inc(c_loaded, 16)

            load(0)
            for e in range(E1):
                sp.dma_start(k.dn1[:, e, :, :], k.dram["L1_ffn_w2"][e, :, :].rearrange("(c p) h -> p c h", p=P)
                             ).then_inc(k.loaded_ffn1, 16)
            with sp.Fori(0, LAST) as i:
                sp.wait_ge(key_ready, i + 1)
                load(i + 1)

        @block.tensor
        def _(pe):
            def turn_ctx(n):
                pe.wait_ge(c_loaded, n * 16 + 16)
                for s in range(2):
                    ins = nc.tensor.transpose(turned_ctx[:, s * P:(s + 1) * P], cin[:, s, :], k.c("ident"))
                ins.then_inc(ctx_turned, 1)

            def turn(i, last):
                pe.wait_ge(q_ready, i + 1)
                pe.wait_ge(key_ready, i + 1)
                nc.tensor.matmul(scores[:, :], k.ident_bf[:, :],
                                 k.blocks_bf[:, :].unsqueeze(1).to_broadcast([P, 4, P]), start=True, stop=False)
                for s in range(2):
                    for m in range(2):
                        ins = nc.tensor.matmul(scores[:, (2 * s + m) * P:(2 * s + m + 1) * P], q[:, s, m, :],
                                               key[:, s, m, :], start=False, stop=s + m == 2)
                ins.then_inc(scores_full, 1)
                pe.wait_ge(v_ready, i + 1)
                if not last:
                    turn_ctx(i + 1)
                pe.wait_ge(attn_ready, i + 1)
                for n in range(4):
                    ins = nc.tensor.transpose(turned_attn[:, n * P:(n + 1) * P], attn[:, n, :], k.c("ident"))
                ins.then_inc(attn_turned, 1)
                pe.wait_ge(attnT_ready, i + 1)
                for s in range(2):
                    for m in range(2):
                        ins = nc.tensor.matmul(attended[:, s * P:(s + 1) * P], vT[:, m, s, :], attnT[:, 2 * s + m, :],
                                               start=(m == 0), stop=(m == 1))
                ins.then_inc(out_full, 1)

            turn_ctx(0)
            with pe.Fori(0, LAST) as i:
                turn(i, False)
            turn(LAST, True)

        @block.scalar
        def _(act):
            def take_values(n):
                act.wait_ge(ctx_turned, n + 1)
                for m in range(2):
                    ins = nc.scalar.activation(vT[:, m, :, :].rearrange("p s t -> p (s t)"), turned_ctx[:, 0:256],
                                               ACT.Identity, bias=k.ch_col[:, BV + m:BV + m + 1],
                                               scale=k.ch_col[:, WV + m:WV + m + 1])
                ins.then_inc(v_ready, 1)

            def turn(i, last):
                act.wait_ge(shift_ready, i + 1)
                for n in range(4):
                    ins = nc.scalar.activation(ex[:, n, :], scores[:, n * P:(n + 1) * P], ACT.Exp,
                                               bias=shift[:, n:n + 1], scale=scale)
                ins.then_inc(ex_ready, 1)
                act.wait_ge(attn_turned, i + 1)
                nc.scalar.copy(attnT[:, :, :].rearrange("p n d -> p (n d)"), turned_attn[:, :]).then_inc(attnT_ready, 1)
                if not last:
                    act.wait_ge(out_full, i + 1)
                    take_values(i + 1)

            act.wait_ge(k.loaded_channel, N_CHANNEL)
            take_values(0)
            with act.Fori(0, LAST) as i:
                turn(i, False)
            turn(LAST, True)

        @block.gpsimd
        def _(pool):
            def take_keys(n):
                pool.wait_ge(c_loaded, n * 16 + 16)
                pool.wait_ge(ctx_turned, n + 1)
                nc.gpsimd.tensor_tensor(kp[:, :, :, :], cin[:, :, :].unsqueeze(2).to_broadcast([P, 2, 2, P]), rows(WK),
                                        ALU.mult).then_inc(kp_ready, 1)
                pool.wait_ge(kp_ready, n + 1)
                nc.gpsimd.tensor_tensor(key[:, :, :, :], kp[:, :, :, :], rows(BK), ALU.add).then_inc(key_ready, 1)

            def turn(i, last):
                pool.wait_ge(max_ready, i + 1)
                nc.gpsimd.tensor_tensor(xres[:, :, :], k.x[:, bass.ds(i * 2, 2), :],
                                        k.ch_row[:, BP:BP + 1, :].to_broadcast([P, 2, P]), ALU.add
                                        ).then_inc(xres_ready, 1)
                if not last:
                    take_keys(i + 1)
                pool.wait_ge(vare_ready, i + 1)
                nc.gpsimd.tensor_tensor(rstd[:, :], vare[:, :], mhalf[:, :], ALU.pow).then_inc(rstd_ready, 1)

            nc.gpsimd.memset(mhalf[:, :], -0.5).then_inc(init, 1)
            pool.wait_ge(k.loaded_channel, N_CHANNEL)
            take_keys(0)
            pool.wait_ge(init, 1)
            with pool.Fori(0, LAST) as i:
                turn(i, False)
            turn(LAST, True)

        @block.vector
        def _(dve):
            def scale_queries(n):
                nc.vector.tensor_tensor(qp[:, :, :, :], k.x[:, bass.ds(n * 2, 2), :].unsqueeze(2)
                                        .to_broadcast([P, 2, 2, P]), rows(WQ), ALU.mult).then_inc(qp_ready, 1)

            def finish_queries(n):
                dve.wait_ge(qp_ready, n + 1)
                nc.vector.tensor_tensor(q[:, :, :, :], qp[:, :, :, :], rows(BQ), ALU.add).then_inc(q_ready, 1)

            def turn(i, last):
                dve.wait_ge(scores_full, i + 1)
                nc.vector.tensor_reduce(negmax[:, :], scores[:, :].rearrange("p (n e) -> p n e", n=4), AX.X, ALU.max,
                                        negate=True).then_inc(max_ready, 1)
                dve.wait_ge(max_ready, i + 1)
                nc.vector.tensor_scalar(shift[:, :], negmax[:, :], scale, None, ALU.mult).then_inc(shift_ready, 1)
                if not last:
                    dve.wait_ge(q_ready, i + 1)
                    scale_queries(i + 1)
                dve.wait_ge(ex_ready, i + 1)
                nc.vector.tensor_reduce(sums[:, :], ex[:, :, :], AX.X, ALU.add).then_inc(sums_ready, 1)
                dve.wait_ge(sums_ready, i + 1)
                nc.vector.reciprocal(recip[:, :], sums[:, :]).then_inc(recip_ready, 1)
                dve.wait_ge(recip_ready, i + 1)
                nc.vector.scalar_tensor_tensor(factor[:, :], recip[:, :], 2.0, k.ch_col[:, WP:WP + 1].to_broadcast([P, 4]),
                                               ALU.mult, ALU.mult).then_inc(factor_ready, 1)
                dve.wait_ge(factor_ready, i + 1)
                nc.vector.tensor_tensor(attn[:, :, :], ex[:, :, :], factor[:, :].unsqueeze(2).to_broadcast([P, 4, P]),
                                        ALU.mult).then_inc(attn_ready, 1)
                dve.wait_ge(out_full, i + 1)
                dve.wait_ge(xres_ready, i + 1)
                nc.vector.tensor_tensor(z[:, :, :], attended[:, 0:256].rearrange("p (s d) -> p s d", s=2), xres[:, :, :],
                                        ALU.add).then_inc(z_ready, 1)
                dve.wait_ge(z_ready, i + 1)
                for s in range(2):
                    ins = nc.vector.bn_stats(stats[:, s, :], z[:, s, :])
                ins.then_inc(stats_ready, 1)
                dve.wait_ge(stats_ready, i + 1)
                if not last:
                    finish_queries(i + 1)
                for s in range(2):
                    ins = nc.vector.bn_aggr(mv[:, s, :], stats[:, s, :])
                ins.then_inc(var_ready, 1)
                dve.wait_ge(var_ready, i + 1)
                nc.vector.tensor_scalar(vare[:, :], mv[:, :, 1], EPS, None, ALU.add).then_inc(vare_ready, 1)
                dve.wait_ge(rstd_ready, i + 1)
                for s in range(2):
                    ins = nc.vector.tensor_scalar(k.x[:, bass.ds(i * 2 + s, 1), :].rearrange("p o d -> p (o d)"),
                                                  z[:, s, :], mv[:, s, 0:1], rstd[:, s:s + 1], ALU.subtract, ALU.mult)
                ins.then_inc(x_ready, 1)

            dve.wait_ge(k.loaded_channel, N_CHANNEL)
            scale_queries(0)
            finish_queries(0)
            with dve.Fori(0, LAST) as i:
                turn(i, False)
            turn(LAST, True)


def experts(k, layer):
    nc = k.nc
    tag = f"moe{layer}"
    NE, NX = (E0, E0 + 1) if layer == 0 else (E1, E1)
    router, bias = (k.wr0, k.rb0) if layer == 0 else (k.gate_w, k.gate_b)
    dn, W = (k.dn0, W0) if layer == 0 else (k.dn1, I1)
    NC = W // P
    NG = NB // 4
    with ExitStack() as outer:
        sb = lambda n, s, dt=F32: outer.enter_context(nc.sbuf_tensor(f"{tag}_{n}", s, dt))
        sem = lambda n: k.sem(f"{tag}_{n}")
        x_high = sb("x_high", [P, NB * P], F32R)
        x_low = sb("x_low", [P, NB * P], F32R)
        gu_high = sb("gu_high", [P, NX, 2 * W], F32R)
        gu_low = sb("gu_low", [P, NX, 2 * W], F32R)
        weight = sb("weight", [P, NB, NX])
        credit = sb("credit", [P, 4])

        with ExitStack() as ctx:
            rows = ctx.enter_context(nc.sbuf_tensor(f"{tag}_rows", [P, 2, 4, P], F32))
            xT = [ctx.enter_context(nc.sbuf_tensor(f"{tag}_xT{b}", [P, 512], F32)) for b in range(2)]
            if layer == 1:
                whole = [ctx.enter_context(nc.sbuf_tensor(f"{tag}_whole{b}", [P, 2 * W], F32)) for b in range(2)]
            else:
                whole = None
            part = lambda n: ctx.enter_context(nc.sbuf_tensor(f"{tag}_{n}", [P, NB, NE], F32))
            line = lambda n: ctx.enter_context(nc.sbuf_tensor(f"{tag}_{n}", [P, NB], F32))
            logits, equal1, place1, first, rest, equal2, place2, second, w_first, w_second = (
                part(n) for n in ("logits", "equal1", "place1", "first", "rest", "equal2", "place2", "second",
                                  "w_first", "w_second"))
            max1, at1, max2, at2, gap, ratio, total, w1, w2 = (
                line(n) for n in ("max1", "at1", "max2", "at2", "gap", "ratio", "total", "w1", "w2"))
            turned = [ctx.enter_context(nc.psum_tensor(f"{tag}_turned{b}", [P, 512], F32)) for b in range(2)]
            scored = [ctx.enter_context(nc.psum_tensor(f"{tag}_scored{b}", [P, 4, NE], F32)) for b in range(2)]
            rows_loaded = [sem(f"rows_loaded{b}") for b in range(2)]
            turned_full = [sem(f"turned_full{b}") for b in range(2)]
            xT_ready = [sem(f"xT_ready{b}") for b in range(2)]
            high_ready = [sem(f"high_ready{b}") for b in range(2)]
            low_ready = sem("low_ready")
            whole_loaded = [sem(f"whole_loaded{b}") for b in range(2)]
            gu_low_ready = sem("gu_low_ready")
            source = lambda e: k.gu0[:, e, :] if layer == 0 else whole[e % 2][:, :]
            gu_high_ready = sem("gu_high_ready")
            scored_full = [sem(f"scored_full{b}") for b in range(2)]
            logits_ready = sem("logits_ready")
            gap_ready = sem("gap_ready")
            ratio_ready = sem("ratio_ready")
            step = sem("step")
            block = ctx.enter_context(nc.Block())

            @block.sync
            def _(sp):
                for g in range(NG):
                    if g >= 2:
                        sp.wait_ge(turned_full[g % 2], g // 2)
                    sp.dma_start(rows[:, g % 2, :, :], k.x[:, 4 * g:4 * g + 4, :]).then_inc(rows_loaded[g % 2], 16)
                    if layer == 1:
                        b = g % 2
                        if g >= 2:
                            sp.wait_ge(gu_low_ready, g - 1)
                        sp.dma_start(whole[b][:, 0:W], k.dram["L1_ffn_w1"][g, :, :]).then_inc(whole_loaded[b], 16)
                        sp.dma_start(whole[b][:, W:], k.dram["L1_ffn_w3"][g, :, :]).then_inc(whole_loaded[b], 16)

            @block.tensor
            def _(pe):
                for g in range(NG):
                    b = g % 2
                    pe.wait_ge(rows_loaded[b], 16 * (g // 2 + 1))
                    if g >= 2:
                        pe.wait_ge(high_ready[b], g // 2)
                    for t in range(4):
                        ins = nc.tensor.transpose(turned[b][:, t * P:(t + 1) * P], rows[:, b, t, :], k.c("ident"))
                    ins.then_inc(turned_full[b], 1)
                    pe.wait_ge(xT_ready[b], g // 2 + 1)
                    if g >= 2:
                        pe.wait_ge(logits_ready, g - 1)
                    for t in range(4):
                        ins = nc.tensor.matmul(scored[b][:, t, :], xT[b][:, t * P:(t + 1) * P], router[:, :],
                                               start=True, stop=True)
                    ins.then_inc(scored_full[b], 1)

            @block.gpsimd
            def _(pool):
                unit = k.c("ones", 0, 1).to_broadcast([P, 2 * W])
                for e in range(NX):
                    if layer == 1:
                        pool.wait_ge(whole_loaded[e % 2], 32 * (e // 2 + 1))
                    nc.gpsimd.tensor_tensor(gu_high[:, e, :], source(e), unit, ALU.mult).then_inc(gu_high_ready, 1)

            @block.scalar
            def _(act):
                for g in range(NG):
                    b = g % 2
                    act.wait_ge(turned_full[b], g // 2 + 1)
                    if g >= 2:
                        act.wait_ge(scored_full[b], g // 2)
                        act.wait_ge(low_ready, g - 1)
                    nc.scalar.copy(xT[b][:, :], turned[b][:, :]).then_inc(xT_ready[b], 1)
                    nc.scalar.copy(x_high[:, g * 512:(g + 1) * 512], turned[b][:, :]).then_inc(high_ready[b], 1)
                act.wait_ge(gap_ready, 1)
                nc.scalar.activation(ratio[:, :], gap[:, :], ACT.Exp).then_inc(ratio_ready, 1)

            @block.vector
            def _(dve):
                for g in range(NG):
                    dve.wait_ge(scored_full[g % 2], g // 2 + 1)
                    nc.vector.tensor_tensor(logits[:, 4 * g:4 * g + 4, :], scored[g % 2][:, :, :],
                                            bias[:, :].unsqueeze(1).to_broadcast([P, 4, NE]), ALU.add
                                            ).then_inc(logits_ready, 1)
                    at = slice(g * 512, (g + 1) * 512)
                    dve.wait_ge(high_ready[g % 2], g // 2 + 1)
                    nc.vector.tensor_tensor(x_low[:, at], xT[g % 2][:, :], x_high[:, at].bitcast(F32), ALU.subtract
                                            ).then_inc(low_ready, 1)
                    if g < NX:
                        dve.wait_ge(gu_high_ready, g + 1)
                        nc.vector.tensor_tensor(gu_low[:, g, :], source(g), gu_high[:, g, :].bitcast(F32),
                                                ALU.subtract).then_inc(gu_low_ready, 1)
                over = lambda a: a[:, :].unsqueeze(2).to_broadcast([P, NB, NE])
                index = k.c("eidx", 0, NE).unsqueeze(1).to_broadcast([P, NB, NE])
                dve.wait_ge(logits_ready, NG)
                nc.vector.tensor_reduce(max1[:, :], logits[:, :, :], AX.X, ALU.max).then_inc(step, 1)
                dve.wait_ge(step, 1)
                nc.vector.tensor_tensor(equal1[:, :, :], logits[:, :, :], over(max1), ALU.is_equal).then_inc(step, 1)
                dve.wait_ge(step, 2)
                nc.vector.scalar_tensor_tensor(place1[:, :, :], equal1[:, :, :], -64.0, index, ALU.mult, ALU.add
                                               ).then_inc(step, 1)
                dve.wait_ge(step, 3)
                nc.vector.tensor_reduce(at1[:, :], place1[:, :, :], AX.X, ALU.min).then_inc(step, 1)
                dve.wait_ge(step, 4)
                nc.vector.tensor_tensor(first[:, :, :], place1[:, :, :], over(at1), ALU.is_equal).then_inc(step, 1)
                dve.wait_ge(step, 5)
                nc.vector.scalar_tensor_tensor(rest[:, :, :], first[:, :, :], NEG, logits[:, :, :], ALU.mult, ALU.add
                                               ).then_inc(step, 1)
                dve.wait_ge(step, 6)
                nc.vector.tensor_reduce(max2[:, :], rest[:, :, :], AX.X, ALU.max).then_inc(step, 1)
                dve.wait_ge(step, 7)
                nc.vector.tensor_tensor(gap[:, :], max2[:, :], max1[:, :], ALU.subtract).then_inc(gap_ready, 1)
                nc.vector.tensor_tensor(equal2[:, :, :], rest[:, :, :], over(max2), ALU.is_equal).then_inc(step, 1)
                dve.wait_ge(step, 8)
                nc.vector.scalar_tensor_tensor(place2[:, :, :], equal2[:, :, :], -64.0, index, ALU.mult, ALU.add
                                               ).then_inc(step, 1)
                dve.wait_ge(step, 9)
                nc.vector.tensor_reduce(at2[:, :], place2[:, :, :], AX.X, ALU.min).then_inc(step, 1)
                dve.wait_ge(step, 10)
                nc.vector.tensor_tensor(second[:, :, :], place2[:, :, :], over(at2), ALU.is_equal).then_inc(step, 1)
                dve.wait_ge(ratio_ready, 1)
                nc.vector.tensor_scalar(total[:, :], ratio[:, :], 1.0, None, ALU.add).then_inc(step, 1)
                dve.wait_ge(step, 12)
                nc.vector.reciprocal(w1[:, :], total[:, :]).then_inc(step, 1)
                dve.wait_ge(step, 13)
                nc.vector.tensor_tensor(w2[:, :], ratio[:, :], w1[:, :], ALU.mult).then_inc(step, 1)
                nc.vector.tensor_tensor(w_first[:, :, :], first[:, :, :], over(w1), ALU.mult).then_inc(step, 1)
                dve.wait_ge(step, 14)
                nc.vector.tensor_tensor(w_second[:, :, :], second[:, :, :], over(w2), ALU.mult).then_inc(step, 1)
                dve.wait_ge(step, 16)
                if NX > NE:
                    nc.vector.memset(weight[:, :, NE:], 1.0)
                nc.vector.tensor_tensor(weight[:, :, 0:NE], w_first[:, :, :], w_second[:, :, :], ALU.add
                                        ).then_inc(step, 1)

        with ExitStack() as ctx:
            buf = lambda n, s: ctx.enter_context(nc.sbuf_tensor(f"{tag}_{n}", s, F32))
            ps = lambda n: ctx.enter_context(nc.psum_tensor(f"{tag}_{n}", [P, 512], F32))
            gate, up, down = ([ps(f"{n}{b}") for b in range(2)] for n in ("gate", "up", "down"))
            silu = [buf(f"silu{b}", [P, 512]) for b in range(2)]
            hidden = [buf(f"hidden{b}", [P, NC, 512]) for b in range(2)]
            w_group = buf("w_group", [P, 4, NX])
            acc = buf("acc", [P, 4, P])
            stats = buf("stats", [P, 4, 6])
            mv = buf("mv", [P, 4, 2])
            vare = buf("vare", [P, 4])
            rstd = buf("rstd", [P, 4])
            mhalf = buf("mhalf", [P, 4])
            up_full = [sem(f"up_full{b}") for b in range(2)]
            silu_ready = [sem(f"silu_ready{b}") for b in range(2)]
            hidden_ready = sem("hidden_ready")
            down_full = sem("down_full")
            acc_ready = sem("acc_ready")
            w_ready = sem("w_ready")
            stats_ready = sem("stats_ready")
            wait_done = sem("wait_done")
            var_ready = sem("var_ready")
            vare_ready = sem("vare_ready")
            rstd_ready = sem("rstd_ready")
            x_ready = sem("x_ready")
            init = sem("init")
            N = NX * NC
            block = ctx.enter_context(nc.Block())


            @block.tensor
            def _(pe):
                def go_up(g, e):
                    for c in range(NC):
                        n = e * NC + c
                        b = n % 2
                        pe.wait_ge(hidden_ready, g * N + (n + 1))
                        high, low = x_high[:, bass.ds(g * 512, 512)], x_low[:, bass.ds(g * 512, 512)]
                        for dst, at in ((gate[b], c * P), (up[b], W + c * P)):
                            nc.tensor.matmul(dst[:, :], gu_high[:, e, at:at + P], high, start=True, stop=False)
                            nc.tensor.matmul(dst[:, :], gu_high[:, e, at:at + P], low, start=False, stop=False)
                            ins = nc.tensor.matmul(dst[:, :], gu_low[:, e, at:at + P], high, start=False, stop=True)
                        ins.then_inc(up_full[b], 1)

                def go_down(g, e):
                    pe.wait_ge(hidden_ready, g * N + ((e + 1) * NC + 2))
                    for t in range(4):
                        for c in range(NC):
                            ins = nc.tensor.matmul(down[e % 2][:, t * P:(t + 1) * P],
                                                   hidden[e % 2][:, c, t * P:(t + 1) * P], dn[:, e, c, :],
                                                   start=(c == 0), stop=(c == NC - 1))
                    ins.then_inc(down_full, 1)

                if layer == 1:
                    pe.wait_ge(k.loaded_ffn1, N_FFN1)
                with pe.Fori(0, NG) as g:
                    go_up(g, 0)
                    for e in range(1, NX):
                        go_up(g, e)
                        go_down(g, e - 1)
                    go_down(g, NX - 1)

            @block.scalar
            def _(act):
                with act.Fori(0, NG) as g:
                    for n in range(N):
                        b = n % 2
                        act.wait_ge(up_full[b], g * (N // 2) + (n // 2 + 1))
                        nc.scalar.activation(silu[b][:, :], gate[b][:, :], ACT.Silu).then_inc(silu_ready[b], 1)

            @block.gpsimd
            def _(pool):
                nc.gpsimd.memset(mhalf[:, :], -0.5).then_inc(init, 1)
                pool.wait_ge(init, 1)
                with pool.Fori(0, NG) as g:
                    pool.wait_ge(vare_ready, g + 1)
                    nc.gpsimd.tensor_tensor(rstd[:, :], vare[:, :], mhalf[:, :], ALU.pow).then_inc(rstd_ready, 1)

            @block.vector
            def _(dve):
                def join(g, e):
                    for c in range(NC):
                        n = e * NC + c
                        dve.wait_ge(silu_ready[n % 2], g * (N // 2) + (n // 2 + 1))
                        nc.vector.tensor_tensor(hidden[e % 2][:, c, :], silu[n % 2][:, :], up[n % 2][:, :], ALU.mult
                                                ).then_inc(hidden_ready, 1)

                def add_up(g, e):
                    dve.wait_ge(down_full, g * NX + (e + 1))
                    dve.wait_ge(w_ready, g + 1) if e == 0 else dve.wait_ge(acc_ready, g * NX + e)
                    for t in range(4):
                        below = (k.x[:, bass.ds(g * 4 + t, 1), :].rearrange("p o d -> p (o d)") if e == 0
                                 else acc[:, t, :])
                        ins = nc.vector.scalar_tensor_tensor(acc[:, t, :], down[e % 2][:, t * P:(t + 1) * P],
                                                             w_group[:, t, e:e + 1], below, ALU.mult, ALU.add)
                    ins.then_inc(acc_ready, 1)

                for n, (sem_one, by) in enumerate(((hidden_ready, 2), (x_ready, 1), (wait_done, 1))):
                    nc.vector.tensor_copy(credit[:, n:n + 1], k.c("ident", 0, 1)).then_inc(sem_one, by)
                with dve.Fori(0, NG) as g:
                    join(g, 0)
                    dve.wait_ge(x_ready, g + 1)
                    nc.vector.tensor_copy(w_group[:, :, :], weight[:, bass.ds(g * 4, 4), :]).then_inc(w_ready, 1)
                    for e in range(1, NX):
                        join(g, e)
                        add_up(g, e - 1)
                    add_up(g, NX - 1)
                    dve.wait_ge(acc_ready, g * NX + NX)
                    for t in range(4):
                        ins = nc.vector.bn_stats(stats[:, t, :], acc[:, t, :])
                    ins.then_inc(stats_ready, 1)
                    dve.wait_ge(wait_done, g + 1)
                    dve.wait_ge(stats_ready, g + 1)
                    nc.vector.tensor_copy(credit[:, 3:4], k.c("ident", 0, 1)).then_inc(wait_done, 1)
                    for t in range(4):
                        ins = nc.vector.bn_aggr(mv[:, t, :], stats[:, t, :])
                    ins.then_inc(var_ready, 1)
                    dve.wait_ge(var_ready, g + 1)
                    nc.vector.tensor_scalar(vare[:, :], mv[:, :, 1], EPS, None, ALU.add).then_inc(vare_ready, 1)
                    dve.wait_ge(rstd_ready, g + 1)
                    for t in range(4):
                        ins = nc.vector.tensor_scalar(k.x[:, bass.ds(g * 4 + t, 1), :].rearrange("p o d -> p (o d)"),
                                                      acc[:, t, :], mv[:, t, 0:1], rstd[:, t:t + 1],
                                                      ALU.subtract, ALU.mult)
                    ins.then_inc(x_ready, 1)


def write_state(k, out):
    nc = k.nc
    with ExitStack() as ctx:
        stored = k.sem("stored")
        block = ctx.enter_context(nc.Block())

        @block.sync
        def _(sp):
            for n in range(4):
                sp.dma_start(out[8 * n:8 * n + 8, :, :].rearrange("b t d -> t b d"), k.x[:, 8 * n:8 * n + 8, :]
                             ).then_inc(stored, 16)
            sp.wait_ge(stored, 64)


def program(nc, d, out):
    with ExitStack() as ctx:
        k = Core(nc, ctx, d)
        with ExitStack() as layer0:
            k.place_experts0(layer0)
            setup(k, d)
            with nc.cleanup_on_exit():
                head_attention(k, "sine", None)
            with nc.cleanup_on_exit():
                head_attention(k, "rope", d["ctx_1024"])
            with nc.cleanup_on_exit():
                experts(k, 0)
        with nc.cleanup_on_exit():
            head_attention(k, "causal", None)
        k.place_experts1()
        with nc.cleanup_on_exit():
            channel_attention(k, d["ctx_1024"])
        with nc.cleanup_on_exit():
            experts(k, 1)
        write_state(k, out)


NAMES = ["x", "ctx_1024",
         "L0_attn_Wq", "L0_attn_bq", "L0_attn_Wk", "L0_attn_bk", "L0_attn_Wv", "L0_attn_bv", "L0_attn_Wo", "L0_attn_bo",
         "L0_xattn_Wq", "L0_xattn_bq", "L0_xattn_Wk", "L0_xattn_bk", "L0_xattn_Wv", "L0_xattn_bv", "L0_xattn_Wo",
         "L0_xattn_bo", "L0_ffn_sg", "L0_ffn_su", "L0_ffn_sd", "L0_ffn_rg", "L0_ffn_ru", "L0_ffn_rd", "L0_ffn_wr",
         "L0_ffn_rb", "L1_attn_wq_lat", "L1_attn_wk_lat", "L1_attn_wv_lat", "L1_attn_wq_heads", "L1_attn_wk_heads",
         "L1_attn_wv_heads", "L1_attn_w_proj", "L1_attn_b_proj",
         "L1_xattn_wqg", "L1_xattn_bqg", "L1_xattn_wkg", "L1_xattn_bkg", "L1_xattn_wvg", "L1_xattn_bvg",
         "L1_xattn_wql", "L1_xattn_bql", "L1_xattn_wkl", "L1_xattn_bkl", "L1_xattn_wvl", "L1_xattn_bvl",
         "L1_xattn_wp", "L1_xattn_bp", "L1_ffn_gate_w", "L1_ffn_gate_b", "L1_ffn_w1", "L1_ffn_w3", "L1_ffn_w2"]


def kernel(**inputs):
    import concourse.bacc as bacc
    from concourse.bass_utils import run_bass_kernel_spmd

    nc = bacc.Bacc("TRN2", target_bir_lowering=False, num_devices=1)
    arrays = {n: np.ascontiguousarray(inputs[n]) for n in NAMES}
    arrays["const"] = constants()
    drams = {n: nc.dram_tensor("in_" + n, a.shape, mybir.dt.from_np(a.dtype), kind="ExternalInput").ap()
             for n, a in arrays.items()}
    out = nc.dram_tensor("out", (NB, P, P), F32, kind="ExternalOutput").ap()
    program(nc, drams, out)
    r = run_bass_kernel_spmd(nc, [{"in_" + n: a for n, a in arrays.items()}], core_ids=[0])
    return r.results[0]["out"]
```

```python
from contextlib import ExitStack

import numpy as np

import concourse.bass as bass
from concourse import mybir

F32 = mybir.dt.float32
F32R = mybir.dt.float32r
BF16 = mybir.dt.bfloat16
ALU = mybir.AluOpType
ACT = mybir.ActivationFunctionType
AX = mybir.AxisListType

P = 128
NB = 32
NPAIR = NB // 2
H, HD = 16, 8
G, J = 4, 4
VW = 64
EPS = 1e-5
NEG = -1e30
MAGIC = 12582912.0
E0, I0 = 7, 352
E1, I1 = 8, 512
CH0 = [(0, 128), (128, 128), (256, 96)]
W0 = 384
LAT = 32
CONST = {}
_at = 0
for _n, _w in (("ident", 128), ("rot", 128), ("cos", 256), ("sin", 256), ("sumrep", 128),
               ("ones", 128), ("under", 128), ("causal_qk", 128), ("causal_kq", 128),
               ("blocks", 128), ("mask", 4), ("maskc", 4), ("eidx", 8)):
    CONST[_n] = (_at, _w)
    _at += _w
NCONST = _at


def constants():
    c = {n: np.zeros((P, w), np.float32) for n, (_, w) in CONST.items()}
    p = np.arange(P)
    c["ident"][p, p] = 1
    for e in range(P):
        lo = e % HD < HD // 2
        c["rot"][e + 4 if lo else e - 4, e] = -1 if lo else 1
    inv = (1.0 / np.float32(10000.0) ** (np.arange(0, HD, 2, dtype=np.float32) / HD)).astype(np.float32)
    ang = np.arange(P, dtype=np.float32)[None, :] * inv[p % (HD // 2)][:, None]
    c["cos"][:] = np.tile(np.cos(ang), (1, 2))
    c["sin"][:] = np.tile(np.sin(ang), (1, 2))
    for a in range(2):
        for j in range(J):
            c["sumrep"][64 * a + 32 + j, 64 * a + 8 * j:64 * a + 8 * j + 8] = 1
        c["sumrep"][64 * a + 32, 64 * a + 32:64 * a + 64] = 1
    c["under"][p, p] = 1
    c["under"][0] = 1
    c["ones"][:] = 1
    c["causal_qk"][:] = np.where(p[None, :] > p[:, None], NEG, 0)
    c["causal_kq"][:] = c["causal_qk"].T
    c["blocks"][:] = np.where(p[None, :] // 32 != p[:, None] // 32, NEG, 0)
    c["mask"][:] = (p[:, None] % 32) // HD == np.arange(J)
    c["maskc"][:] = c["mask"] * np.float32(30.0 / (np.sqrt(8.0) * 2 * np.pi))
    c["eidx"][:] = np.arange(8)
    return np.concatenate([c[n] for n in CONST], axis=1)


class Core:

    def __init__(self, nc, ctx, dram):
        self.nc, self.ctx, self.dram = nc, ctx, dram
        sb = self.sb
        self.const = sb("const", [P, NCONST])
        self.ident_bf = sb("ident_bf", [P, P], BF16)
        self.causal_qk_bf = sb("causal_qk_bf", [P, P], BF16)
        self.blocks_bf = sb("blocks_bf", [P, P], BF16)
        self.ones_r = sb("ones_r", [P, P], F32R)
        self.under_r = sb("under_r", [P, P], F32R)
        self.x = sb("x_state", [P, NB, P])
        self.w_sin = sb("w_sin", [P, 5, P])
        self.w_rope = sb("w_rope", [P, 7, P])
        self.w_lat = sb("w_lat", [P, 3 * LAT])
        self.w_heads = sb("w_heads", [P, 3, P])
        self.w_proj = sb("w_proj", [P, 2, P])
        self.bias_col = sb("bias_col", [P, 8])
        self.bias_row = sb("bias_row", [P, 5, P])
        self.wr0 = sb("wr0", [P, E0])
        self.rb0 = sb("rb0", [P, E0])
        self.gate_w = sb("gate_w", [P, E1])
        self.gate_b = sb("gate_b", [P, E1])
        self.ch_row = sb("ch_row", [P, 9, P])
        self.ch_col = sb("ch_col", [P, 5])
        self.loaded_channel = self.sem("loaded_channel")
        self.loaded_ffn1 = self.sem("loaded_ffn1")

    def place_experts0(self, ctx):
        self.gu0 = ctx.enter_context(self.nc.sbuf_tensor("gu0", [P, E0 + 1, 2 * W0], F32))
        self.dn0 = ctx.enter_context(self.nc.sbuf_tensor("dn0", [P, E0 + 1, 3, P], F32))

    def place_experts1(self):
        self.dn1 = self.sb("dn1", [P, E1, 4, P])

    def sb(self, name, shape, dt=F32):
        return self.ctx.enter_context(self.nc.sbuf_tensor(name, shape, dt))

    def sem(self, name):
        return self.nc.alloc_semaphore(name)

    def c(self, name, a=0, b=None):
        at, w = CONST[name]
        return self.const[:, at + a:at + (w if b is None else b)]


BQ0, BK0, BQ1, BK1, BQ1R, BK1R = range(6)
BV0, BO0, BV1, BO1, BPROJ = range(5)
CH_ROWS = ["wqg", "wql", "bqg", "bql", "wkg", "wkl", "bkg", "bkl", "bp"]
WQ, BQ, WK, BK, BP = 0, 2, 4, 6, 8
CH_COLS = ["wvg", "wvl", "bvg", "bvl", "wp"]
WV, BV, WP = 0, 2, 4
N_CHANNEL = 16 * (len(CH_ROWS) + len(CH_COLS))
N_FFN1 = 16 * E1


def setup(k, d):
    nc = k.nc
    with ExitStack() as ctx:
        sb = lambda n, s, dt=F32: ctx.enter_context(nc.sbuf_tensor(n, s, dt))
        raw = sb("raw_attn", [P, 8, P])
        raw_gu = sb("raw_gu", [P, 2 * (E0 + 1), 3, P])
        raw_dn = sb("raw_dn", [P, E0 + 1, I0])
        raw_wr = sb("raw_wr", [E0, P])
        bank = [ctx.enter_context(nc.psum_tensor(f"turn{i}", [P, 512], F32)) for i in range(4)]
        loaded_x = k.sem("loaded_x")
        loaded_attn = k.sem("loaded_attn")
        loaded_later = k.sem("loaded_later")
        loaded_ffn = k.sem("loaded_ffn")
        cleared = k.sem("cleared")
        cast = k.sem("cast")
        turned = [k.sem(f"turned{i}") for i in range(4)]
        taken = [k.sem(f"taken{i}") for i in range(4)]
        attn_names = ["L0_attn_Wq", "L0_attn_Wk", "L0_attn_Wv", "L0_attn_Wo",
                      "L0_xattn_Wq", "L0_xattn_Wk", "L0_xattn_Wv", "L0_xattn_Wo"]
        cols = ["L0_attn_bq", "L0_attn_bk", "L0_xattn_bq", "L0_xattn_bk"]
        rows = ["L0_attn_bv", "L0_attn_bo", "L0_xattn_bv", "L0_xattn_bo", "L1_attn_b_proj"]
        n_attn = 1 + len(attn_names) + 1 + len(cols)
        n_ffn = 4 * len(CH0) + 2

        ident, rot = k.c("ident"), k.c("rot")

        def jobs():
            for base, dst, plan in ((0, k.w_sin, ((0, ident), (1, ident), (2, ident))),
                                    (4, k.w_rope, ((0, ident), (0, rot), (1, ident), (1, rot), (2, ident)))):
                for n0 in range(0, len(plan), 4):
                    part = plan[n0:n0 + 4]
                    yield ([(raw[:, base + m, :], by, (slice(0, P), slice(i * P, i * P + P)))
                            for i, (m, by) in enumerate(part)],
                           [((slice(0, P), slice(0, len(part) * P)),
                             dst[:, n0:n0 + len(part), :].rearrange("p a b -> p (a b)"))])
            for m, dst in ((3, k.w_sin[:, 3:5, :]), (7, k.w_rope[:, 5:7, :])):
                yield ([(raw[:, m, :], ident, (slice(0, P), slice(0, P)))],
                       [((slice(32 * g, 32 * g + 32), slice(0, P)), dst[64 * (g % 2):64 * (g % 2) + 32, g // 2, :])
                        for g in range(G)])
            yield ([(rot, k.bias_col[:, BQ1:BQ1 + 2], (slice(0, P), slice(0, 2))),
                    (raw_wr[:, :], ident[0:E0, 0:E0], (slice(0, P), slice(128, 128 + E0)))],
                   [((slice(0, P), slice(0, 2)), k.bias_col[:, BQ1R:BQ1R + 2]),
                    ((slice(0, P), slice(128, 128 + E0)), k.wr0[:, :])])
            for e in range(E0 + 1):
                for m in range(2):
                    yield ([(raw_gu[0:n, 2 * e + m, c, :], ident[0:n, 0:n], (slice(0, P), slice(a, a + n)))
                            for c, (a, n) in enumerate(CH0)],
                           [((slice(0, P), slice(0, I0)), k.gu0[:, e, m * W0:m * W0 + I0])])
                yield ([(raw_dn[:, e, a:a + n], ident, (slice(0, n), slice(c * P, c * P + P)))
                        for c, (a, n) in enumerate(CH0)],
                       [((slice(0, P), slice(0, 2 * P)), k.dn0[:, e, 0:2, :].rearrange("p a b -> p (a b)")),
                        ((slice(0, 96), slice(2 * P, 3 * P)), k.dn0[0:96, e, 2, :])])

        work = list(jobs())
        first_ffn = len(work) - 3 * (E0 + 1)
        block = ctx.enter_context(nc.Block())

        @block.sync
        def _(sp):
            sp.dma_start(k.const[:, :], d["const"]).then_inc(loaded_attn, 16)
            for m in range(4, 8):
                sp.dma_start(raw[:, m, :], d[attn_names[m]]).then_inc(loaded_attn, 16)
            sp.dma_start(raw_wr[:, :], d["L0_ffn_wr"]).then_inc(loaded_attn, 16)
            for m, n in enumerate(cols):
                sp.dma_start(k.bias_col[:, m:m + 1], d[n].rearrange("(p o) -> p o", o=1)).then_inc(loaded_attn, 16)
            later = 0
            for m, n in enumerate(rows):
                sp.dma_start(k.bias_row[:, m, :], d[n].rearrange("(o n) -> o n", o=1).partition_broadcast(P)
                             ).then_inc(loaded_later, 16)
                later += 16
            for dst, n in ((k.rb0, "L0_ffn_rb"), (k.gate_b, "L1_ffn_gate_b")):
                sp.dma_start(dst[:, :], d[n].rearrange("(o n) -> o n", o=1).partition_broadcast(P)
                             ).then_inc(loaded_later, 16)
                later += 16
            sp.dma_start(k.gate_w[:, :], d["L1_ffn_gate_w"]).then_inc(loaded_later, 16)
            later += 16
            for m, n in enumerate(("L1_attn_wq_lat", "L1_attn_wk_lat", "L1_attn_wv_lat")):
                sp.dma_start(k.w_lat[:, m * LAT:(m + 1) * LAT], d[n]).then_inc(loaded_later, 16)
                later += 16
            sp.wait_ge(cleared, 2)
            for m, n in enumerate(("L1_attn_wq_heads", "L1_attn_wk_heads", "L1_attn_wv_heads")):
                sp.dma_start(k.w_heads[m * LAT:(m + 1) * LAT, m, :], d[n]).then_inc(loaded_later, 16)
                later += 16
            for g in range(G):
                sp.dma_start(k.w_proj[64 * (g % 2):64 * (g % 2) + 32, g // 2, :],
                             d["L1_attn_w_proj"][32 * g:32 * g + 32, :]).then_inc(loaded_later, 16)
                later += 16
            for m, n in enumerate(CH_ROWS):
                sp.dma_start(k.ch_row[:, m, :], d["L1_xattn_" + n].rearrange("(o n) -> o n", o=1).partition_broadcast(P)
                             ).then_inc(k.loaded_channel, 16)
            for m, n in enumerate(CH_COLS):
                sp.dma_start(k.ch_col[:, m:m + 1], d["L1_xattn_" + n].rearrange("(p o) -> p o", o=1)
                             ).then_inc(k.loaded_channel, 16)
            sp.wait_ge(loaded_later, later)
            sp.wait_ge(loaded_x, 64)

        @block.scalar
        def _(act):
            for m in range(4):
                act.dma_start(raw[:, m, :], d[attn_names[m]]).then_inc(loaded_attn, 16)
            for s, n in enumerate(("g", "u")):
                for c, (a, w) in enumerate(CH0):
                    act.dma_start(raw_gu[0:w, s:2 * E0:2, c, :],
                                  d["L0_ffn_r" + n][:, a:a + w, :].rearrange("e p h -> p e h")).then_inc(loaded_ffn, 16)
                    act.dma_start(raw_gu[0:w, 2 * E0 + s, c, :], d["L0_ffn_s" + n][a:a + w, :]).then_inc(loaded_ffn, 16)
            act.dma_start(raw_dn[:, 0:E0, :], d["L0_ffn_rd"].rearrange("e h i -> h e i")).then_inc(loaded_ffn, 16)
            act.dma_start(raw_dn[:, E0, :], d["L0_ffn_sd"]).then_inc(loaded_ffn, 16)
            act.wait_ge(cleared, 4)
            for n in range(1, len(work), 2):
                b = n % 4
                act.wait_ge(turned[b], n // 4 + 1)
                for i, (s, dst) in enumerate(work[n][1]):
                    ins = nc.scalar.copy(dst, bank[b][s[0], s[1]])
                ins.then_inc(taken[b], 1)

        @block.gpsimd
        def _(pool):
            for n in range(4):
                pool.dma_start(k.x[:, 8 * n:8 * n + 8, :], d["x"][8 * n:8 * n + 8, :, :].rearrange("b t d -> t b d")
                               ).then_inc(loaded_x, 16)
            nc.gpsimd.memset(k.w_heads[:, :, :], 0.0).then_inc(cleared, 1)
            nc.gpsimd.memset(k.w_proj[:, :, :], 0.0).then_inc(cleared, 1)
            nc.gpsimd.memset(k.w_sin[:, :, :], 0.0).then_inc(cleared, 1)
            nc.gpsimd.memset(k.w_rope[:, :, :], 0.0).then_inc(cleared, 1)
            nc.gpsimd.memset(k.gu0[:, :, I0:W0], 0.0).then_inc(cleared, 1)
            nc.gpsimd.memset(k.gu0[:, :, W0 + I0:], 0.0).then_inc(cleared, 1)
            pool.wait_ge(cleared, 6)
            nc.gpsimd.memset(k.dn0[96:P, :, 2, :], 0.0).then_inc(cleared, 1)

        @block.tensor
        def _(pe):
            pe.wait_ge(loaded_attn, 16 * n_attn)
            for n, (turns, _) in enumerate(work):
                b = n % 4
                if n == first_ffn:
                    pe.wait_ge(loaded_ffn, 16 * n_ffn)
                if n >= 4:
                    pe.wait_ge(taken[b], n // 4)
                for w, by, (r, c) in turns:
                    ins = nc.tensor.matmul(bank[b][r, c], w, by, start=True, stop=True)
                ins.then_inc(turned[b], 1)

        @block.vector
        def _(dve):
            dve.wait_ge(loaded_attn, 16 * n_attn)
            for dst, n in ((k.ident_bf, "ident"), (k.causal_qk_bf, "causal_qk"), (k.blocks_bf, "blocks"),
                           (k.ones_r, "ones"), (k.under_r, "under")):
                nc.vector.tensor_copy(dst[:, :], k.c(n)).then_inc(cast, 1)
            dve.wait_ge(cleared, 4)
            for n in range(0, len(work), 2):
                b = n % 4
                dve.wait_ge(turned[b], n // 4 + 1)
                for s, dst in work[n][1]:
                    ins = nc.vector.tensor_copy(dst, bank[b][s[0], s[1]])
                ins.then_inc(taken[b], 1)


class Turn:

    def __init__(self, n, loop=None):
        self.n, self.loop = n, loop

    def count(self, first, per):
        return first if self.loop is None else self.loop * (2 * per) + first

    def pairs(self, ahead, per=1, plus=0):
        return self.count((self.n + ahead) * per + plus, per)


def head_attention(k, kind, ctx_in):
    nc = k.nc
    softmax = kind != "sine"
    with ExitStack() as ctx:
        sb = lambda n, s, dt=F32: ctx.enter_context(nc.sbuf_tensor(f"{kind}_{n}", s, dt))
        ps = lambda n, s: ctx.enter_context(nc.psum_tensor(f"{kind}_{n}", s, F32))
        sem = lambda n: k.sem(f"{kind}_{n}")
        two = lambda n, s, dt=F32: [sb(f"{n}{i}", s, dt) for i in range(2)]
        scores = [ps("scores0", [P, 1024]), ps("scores1", [P, 1024])]
        bank = {n: ps("bank" + n, [P, 512]) for n in "ABCD"}
        xT = two("xT", [P, 512])
        latT = two("latT", [P, 256]) if kind == "causal" else None
        q4_high, q4_low = two("q4_high", [P, J, 256], F32R), two("q4_low", [P, J, 256], F32R)
        kg_high, kg_low = two("kg_high", [P, G, 256], F32R), two("kg_low", [P, G, 256], F32R)
        vb = [[sb(f"vb{i}{s}", [P, G, J, VW]) for s in range(2)] for i in range(2)]
        q4 = sb("q4", [P, J, 256])
        kg = sb("kg", [P, G, 256])
        xin = sb("xin", [P, 2, P])
        cin = sb("cin", [P, 2, P]) if ctx_in is not None else None
        rot = [sb(f"rot{i}", [P, 256]) for i in range(6)] if kind == "rope" else None
        rnd = two("rnd", [P, 1024]) if kind == "sine" else None
        probs = two("probs", [P, H * P])
        if softmax:
            negmax = two("negmax", [P, H])
            negmaxT = two("negmaxT", [H, P], F32R)
            shift = two("shift", [P, H * P], F32R)
            osum = two("osum", [P, 256])
            recip = two("recip", [P, 256])
        onorm = two("onorm", [P, 256])
        xres = two("xres", [P, P])
        z = two("z", [P, P])
        stats = two("stats", [P, 6])
        mv = two("mv", [P, 2])
        vare = two("vare", [P, 1])
        rstd = two("rstd", [P, 1])
        spare = two("spare", [P, 1])
        mhalf = sb("mhalf", [P, 1])
        warm = sb("warm", [P, 2])

        has = lambda pair: 0 <= pair < NPAIR

        def uses(b, n):
            p, m, v = has(n + 2), has(n + 1) and softmax, has(n + 1)
            o1, o0 = has(n - 1), has(n)
            return {"A": ["m00", "m02"] * m + ["lat"] * (p and kind == "causal") + ["m10", "m12"] * m + ["q"] * p,
                    "B": ["m01", "m03", "m11", "m13"] * m + ["k"] * p,
                    "C": ["y0"] * o1 + ["xT"] * p + ["nm0"] * m + ["y1"] * o1 + ["nm1"] * m + ["v"] * v,
                    "D": (["pv1"] + ["sum1"] * softmax) * o1 + (["pv0"] + ["sum0"] * softmax) * o0}[b]

        full = {n: sem("full" + n) for n in "ABCD"}
        empty = {n: sem("empty" + n) for n in "ABCD"}

        def nth(b, use, t):
            first = sum(len(uses(b, n)) for n in range(-2, t.n)) + uses(b, t.n).index(use)
            return t.count(first, len(uses(b, 2)))

        x_loaded = sem("x_loaded")
        rotated = sem("rotated")
        q_ready = sem("q_ready")
        k_ready = sem("k_ready")
        q_high_ready = sem("q_high_ready")
        q_low_ready = sem("q_low_ready")
        k_high_ready = sem("k_high_ready")
        k_low_ready = sem("k_low_ready")
        shift_loaded = [sem(f"shift_loaded{i}") for i in range(2)]
        scores_full = [sem(f"scores_full{i}") for i in range(2)]
        rounded = [sem(f"rounded{i}") for i in range(2)]
        frac_ready = [sem(f"frac_ready{i}") for i in range(2)]
        probs_ready = [sem(f"probs_ready{i}") for i in range(2)]
        onorm_ready = sem("onorm_ready")
        xres_ready = sem("xres_ready")
        z_ready = sem("z_ready")
        stats_ready = sem("stats_ready")
        var_ready = sem("var_ready")
        vare_ready = sem("vare_ready")
        rstd_ready = sem("rstd_ready")
        x_ready = sem("x_ready")
        warmed = sem("warmed")
        kg_zero = sem("kg_zero")
        shift_zero = sem("shift_zero")
        vb_zero = sem("vb_zero")
        vb_set = sem("vb_set")
        half_set = sem("half_set")
        scores_empty = probs_ready if softmax else frac_ready

        def wait(engine, semaphore, value):
            if not isinstance(value, int) or value > 0:
                engine.wait_ge(semaphore, value)

        def value_blocks(i, s):
            return bass.AP(vb[i][s], 0, [[G * J * VW, P], [J * VW, G], [VW + HD, J], [1, HD]])

        def sum_columns(i, s):
            return bass.AP(vb[i][s], 32, [[G * J * VW, P], [J * VW, G], [VW + 1, J]])

        def state(t, ahead, s):
            at = t.pairs(ahead, 2, s)
            rows = k.x[:, at:at + 1, :] if isinstance(at, int) else k.x[:, bass.ds(at, 1), :]
            return rows.rearrange("p o d -> p (o d)")

        n_in = 2 if ctx_in is not None else 1
        w, cst = (k.w_sin if kind == "sine" else k.w_rope), k.c
        w_out = {"sine": k.w_sin[:, 3:5, :], "rope": k.w_rope[:, 5:7, :], "causal": k.w_proj[:, :, :]}[kind]
        b_out = {"sine": BO0, "rope": BO1, "causal": BPROJ}[kind]
        LOOP0, LOOP1 = 2, NPAIR - 2
        block = ctx.enter_context(nc.Block())

        def all_turns(engine, turn, start_loop=None):
            for n in range(-2, LOOP0):
                turn(Turn(n))
            with engine.Fori(0, (LOOP1 - LOOP0) // 2) as i:
                if start_loop is not None:
                    start_loop(i)
                turn(Turn(LOOP0, i))
                turn(Turn(LOOP0 + 1, i))
            for n in range(LOOP1, NPAIR + 1):
                turn(Turn(n))

        @block.sync
        def _(sp):
            def turn(t):
                if not has(t.n + 2):
                    return
                if has(t.n + 1):
                    sp.wait_ge(full["C"], nth("C", "xT", Turn(t.n - 1, t.loop)) + 1)
                pair = bass.ds(t.pairs(2, 2), 2)
                sp.dma_start(xin[:, :, :], k.x[:, pair, :]).then_inc(x_loaded, 16)
                if ctx_in is not None:
                    sp.dma_start(cin[:, :, :], ctx_in[pair, :, :].rearrange("b t d -> t b d")).then_inc(x_loaded, 16)

            all_turns(sp, turn)
            sp.wait_ge(x_loaded, 16 * n_in * NPAIR)

        @block.tensor
        def _(pe):
            def transposes(t):
                pe.wait_ge(x_loaded, t.pairs(3, 16 * n_in))
                wait(pe, empty["C"], nth("C", "xT", t))
                for m, src in enumerate((xin, cin)[:n_in]):
                    for s in range(2):
                        ins = nc.tensor.transpose(bank["C"][:, (2 * m + s) * P:(2 * m + s + 1) * P],
                                                  src[:, s, :], cst("ident"))
                ins.then_inc(full["C"], 1)

            def project_lat(t):
                pe.wait_ge(empty["C"], nth("C", "xT", t) + 1)
                wait(pe, empty["A"], nth("A", "lat", t))
                nc.tensor.matmul(bank["A"][0:3 * LAT, 0:256], k.w_lat[:, :], xT[t.n % 2][:, 0:256],
                                 start=True, stop=True).then_inc(full["A"], 1)

            def project_qk(t):
                p = t.n % 2
                if kind != "causal":
                    pe.wait_ge(empty["C"], nth("C", "xT", t) + 1)
                wait(pe, empty["A"], nth("A", "q", t))
                src_q, src_k = xT[p][:, 0:256], xT[p][:, 256 * (n_in - 1):256 * n_in]
                if kind == "causal":
                    latent = latT[p][0:3 * LAT, :]
                    nc.tensor.matmul(bank["A"][:, 0:256], k.w_heads[0:3 * LAT, 0, :], latent, start=True, stop=True
                                     ).then_inc(full["A"], 1)
                    wait(pe, empty["B"], nth("B", "k", t))
                    nc.tensor.matmul(bank["B"][:, 0:256], k.w_heads[0:3 * LAT, 1, :], latent, start=True, stop=True
                                     ).then_inc(full["B"], 1)
                elif kind == "rope":
                    nc.tensor.matmul(bank["A"][:, 0:256], w[:, 0, :], src_q, start=True, stop=True)
                    nc.tensor.matmul(bank["A"][:, 256:512], w[:, 1, :], src_q, start=True, stop=True
                                     ).then_inc(full["A"], 1)
                    wait(pe, empty["B"], nth("B", "k", t))
                    nc.tensor.matmul(bank["B"][:, 0:256], w[:, 2, :], src_k, start=True, stop=True)
                    nc.tensor.matmul(bank["B"][:, 256:512], w[:, 3, :], src_k, start=True, stop=True
                                     ).then_inc(full["B"], 1)
                else:
                    nc.tensor.matmul(bank["A"][:, 0:256], w[:, 0, :], src_q, start=True, stop=True
                                     ).then_inc(full["A"], 1)
                    wait(pe, empty["B"], nth("B", "k", t))
                    nc.tensor.matmul(bank["B"][:, 0:256], w[:, 1, :], src_k, start=True, stop=True
                                     ).then_inc(full["B"], 1)

            def project_v(t):
                p = (t.n + 1) % 2
                pe.wait_ge(empty["C"], nth("C", "v", t))
                for s in range(2):
                    if kind == "causal":
                        src, wv = latT[p][0:3 * LAT, s * P:(s + 1) * P], k.w_heads[0:3 * LAT, 2, :]
                    else:
                        at = 256 * (n_in - 1) + s * P
                        src, wv = xT[p][:, at:at + P], w[:, 4 if kind == "rope" else 2, :]
                    ins = nc.tensor.matmul(bank["C"][:, s * P:(s + 1) * P], src, wv, start=True, stop=True)
                ins.then_inc(full["C"], 1)

            def row_scores(t, s, j0):
                if s == 0 and j0 == 0:
                    pe.wait_ge(q_high_ready, t.pairs(2))
                    pe.wait_ge(k_high_ready, t.pairs(2))
                for j in (j0, j0 + 1):
                    b = "AB"[j % 2]
                    pe.wait_ge(empty[b], nth(b, f"m{s}{j}", t))
                    p = (t.n + 1) % 2
                    ins = nc.tensor.matmul(bank[b][:, :], q4_high[p][:, j, s * P:(s + 1) * P],
                                           kg_high[p][:, :, s * P:(s + 1) * P],
                                           start=True, stop=kind != "causal")
                    if kind == "causal":
                        ins = nc.tensor.matmul(bank[b][:, :], k.ident_bf[:, :],
                                               k.causal_qk_bf[:, :].unsqueeze(1).to_broadcast([P, 4, P]),
                                               start=False, stop=True)
                    ins.then_inc(full[b], 1)

            def turn_maxima(t, s):
                pe.wait_ge(empty["B"], nth("B", f"m{s}3", t) + 1)
                pe.wait_ge(empty["C"], nth("C", f"nm{s}", t))
                nc.tensor.transpose(bank["C"][0:H, 0:P], negmax[s][:, :], cst("ident")).then_inc(full["C"], 1)

            def key_scores(t, s, half):
                p = t.n % 2
                if softmax and half == 0:
                    pe.wait_ge(shift_loaded[s], t.pairs(1, 16))
                if s == 0 and half == 0:
                    pe.wait_ge(q_low_ready, t.pairs(1))
                    pe.wait_ge(k_low_ready, t.pairs(1))
                wait(pe, scores_empty[half], t.pairs(0, 2, s))
                for g in (2 * half, 2 * half + 1):
                    out = scores[half][:, (g % 2) * 512:(g % 2 + 1) * 512]
                    key_high, key_low = kg_high[p][:, g, s * P:(s + 1) * P], kg_low[p][:, g, s * P:(s + 1) * P]
                    high, low = q4_high[p][:, :, s * P:(s + 1) * P], q4_low[p][:, :, s * P:(s + 1) * P]
                    nc.tensor.matmul(out, key_high, high, start=True, stop=False)
                    nc.tensor.matmul(out, key_high, low, start=False, stop=False)
                    ins = nc.tensor.matmul(out, key_low, high, start=False, stop=not softmax)
                    if softmax:
                        ins = nc.tensor.matmul(out, (k.under_r if kind == "causal" else k.ones_r)[:, :],
                                               shift[s][:, g * 512:(g + 1) * 512],
                                               start=False, stop=True)
                ins.then_inc(scores_full[half], 1)

            def values(t, ahead, s):
                p = (t.n + ahead) % 2
                wait(pe, empty["D"], nth("D", f"pv{s}", t))
                for r in range(2):
                    pe.wait_ge(probs_ready[r], t.pairs(ahead, 2, s + 1))
                    for j in range(J):
                        for a in range(2):
                            h = 4 * (2 * r + a) + j
                            ins = nc.tensor.matmul(bank["D"][64 * a:64 * a + 64, r * P:(r + 1) * P],
                                                   vb[p][s][:, 2 * r + a, j, :], probs[s][:, h * P:(h + 1) * P],
                                                   start=(j == 0), stop=(j == J - 1))
                ins.then_inc(full["D"], 1)

            def repeat_sums(t, s):
                pe.wait_ge(empty["D"], nth("D", f"sum{s}", t))
                nc.tensor.matmul(bank["D"][:, 256:512], cst("sumrep"), osum[s][:, :], start=True, stop=True
                                 ).then_inc(full["D"], 1)

            def project_out(t, ahead, s):
                if softmax:
                    pe.wait_ge(onorm_ready, t.pairs(ahead, 2, s + 1))
                else:
                    pe.wait_ge(empty["D"], nth("D", f"pv{s}", t if s == 1 else Turn(t.n - 1, t.loop)) + 1)
                wait(pe, empty["C"], nth("C", f"y{s}", t))
                for r in range(2):
                    ins = nc.tensor.matmul(bank["C"][:, 0:P], onorm[s][:, r * P:(r + 1) * P], w_out[:, r, :],
                                           start=(r == 0), stop=(r == 1))
                ins.then_inc(full["C"], 1)

            def turn(t):
                p, m, v, o1, o0 = has(t.n + 2), has(t.n + 1) and softmax, has(t.n + 1), has(t.n - 1), has(t.n)
                if o0:
                    key_scores(t, 0, 0)
                    key_scores(t, 0, 1)
                if o1:
                    project_out(t, -1, 0)
                if m:
                    row_scores(t, 0, 0)
                if o1:
                    values(t, -1, 1)
                if m:
                    row_scores(t, 0, 2)
                if p and softmax:
                    transposes(t)
                if o1 and softmax:
                    repeat_sums(t, 1)
                if o0:
                    key_scores(t, 1, 0)
                if p and not softmax:
                    transposes(t)
                if p and kind == "causal":
                    project_lat(t)
                if m:
                    turn_maxima(t, 0)
                    row_scores(t, 1, 0)
                if o0:
                    key_scores(t, 1, 1)
                if m:
                    row_scores(t, 1, 2)
                if o1:
                    project_out(t, -1, 1)
                if p:
                    project_qk(t)
                if m:
                    turn_maxima(t, 1)
                if o0:
                    values(t, 0, 0)
                if v:
                    project_v(t)
                if o0 and softmax:
                    repeat_sums(t, 0)

            all_turns(pe, turn)

        @block.scalar
        def _(act):
            def take_xT(t):
                act.wait_ge(full["C"], nth("C", "xT", t) + 1)
                nc.scalar.copy(xT[t.n % 2][:, 0:256 * n_in], bank["C"][:, 0:256 * n_in]).then_inc(empty["C"], 1)

            def take_k(t):
                if kind == "rope":
                    act.wait_ge(rotated, t.pairs(3, 2))
                else:
                    act.wait_ge(full["B"], nth("B", "k", t) + 1)
                wait(act, k_low_ready, t.pairs(2))
                wait(act, k_high_ready, t.pairs(2))
                src = rot[5] if kind == "rope" else bank["B"]
                for g in range(G):
                    rows = slice(32 * g, 32 * g + 32)
                    if kind == "sine":
                        ins = nc.scalar.activation(kg[rows, g, :], src[rows, 0:256], ACT.Identity,
                                                   bias=k.bias_col[rows, BK0:BK0 + 1])
                    else:
                        ins = nc.scalar.copy(kg[rows, g, :], src[rows, 0:256])
                ins.then_inc(k_ready if kind == "rope" else empty["B"], 1)
                if kind == "rope":
                    act.wait_ge(k_ready, t.pairs(3))
                else:
                    act.wait_ge(empty["B"], nth("B", "k", t) + 1)
                nc.scalar.copy(kg_high[t.n % 2][:, :, :], kg[:, :, :]).then_inc(k_high_ready, 1)

            def take_v(t):
                act.wait_ge(full["C"], nth("C", "v", t) + 1)
                for s in range(2):
                    ins = nc.scalar.copy(value_blocks((t.n + 1) % 2, s), bank["C"][:, s * P:(s + 1) * P]
                                         .rearrange("p (g j d) -> p g j d", g=G, j=J))
                ins.then_inc(empty["C"], 1)

            def take_maxima(t, s):
                act.wait_ge(full["C"], nth("C", f"nm{s}", t) + 1)
                nc.scalar.copy(negmaxT[s][:, :], bank["C"][0:H, 0:P]).then_inc(empty["C"], 1)
                act.wait_ge(empty["C"], nth("C", f"nm{s}", t) + 1)
                act.dma_start(shift[s][0:1, :].bitcast(F32).rearrange("o (h q) -> o h q", q=P),
                              negmaxT[s][:, :].bitcast(F32)).then_inc(shift_loaded[s], 16)

            def exps(t, s, half):
                act.wait_ge(scores_full[half], t.pairs(0, 2, s + 1))
                nc.scalar.activation(probs[s][:, half * 1024:(half + 1) * 1024], scores[half][:, :], ACT.Exp,
                                     scale=HD ** -0.5).then_inc(probs_ready[half], 1)

            def take_out(t, s):
                act.wait_ge(full["D"], nth("D", f"pv{s}", t) + 1)
                nc.scalar.copy((osum if softmax else onorm)[s][:, :], bank["D"][:, 0:256]
                               ).then_inc(empty["D"], 1)

            def rounds(t, s, half):
                wait(act, probs_ready[half], t.pairs(0, 2, s))
                act.wait_ge(scores_full[half], t.pairs(0, 2, s + 1))
                nc.scalar.activation(rnd[half][:, :], scores[half][:, :], ACT.Copy, bias=MAGIC
                                     ).then_inc(rounded[half], 1)

            def sines(t, s):
                for half in range(2):
                    act.wait_ge(frac_ready[half], t.pairs(0, 2, s + 1))
                    nc.scalar.activation(probs[s][:, half * 1024:(half + 1) * 1024], rnd[half][:, :], ACT.Sin,
                                         scale=float(-2 * np.pi)).then_inc(probs_ready[half], 1)

            def turn(t):
                p, m, v, o1, o0 = has(t.n + 2), has(t.n + 1) and softmax, has(t.n + 1), has(t.n - 1), has(t.n)
                if o0:
                    if softmax:
                        exps(t, 0, 0)
                        exps(t, 0, 1)
                    else:
                        rounds(t, 0, 0)
                        rounds(t, 0, 1)
                        sines(t, 0)
                if o1:
                    take_out(t, 1)
                if p and softmax:
                    take_xT(t)
                if o0:
                    exps(t, 1, 0) if softmax else rounds(t, 1, 0)
                if p and not softmax:
                    take_xT(t)
                if o0 and not softmax:
                    rounds(t, 1, 1)
                if m:
                    take_maxima(t, 0)
                if o0:
                    exps(t, 1, 1) if softmax else sines(t, 1)
                if m:
                    take_maxima(t, 1)
                if p and not softmax:
                    take_k(t)
                if o0:
                    take_out(t, 0)
                if v and kind == "causal":
                    take_v(t)
                if p and softmax:
                    take_k(t)

            def name_table(i):
                act.wait_ge(warmed, i + 1)
                nc.scalar.activation(warm[:, 1:2], cst("ident", 0, 1), ACT.Exp if softmax else ACT.Sin
                                     ).then_inc(warmed, 1)

            act.wait_ge(kg_zero, 1)
            if softmax:
                act.wait_ge(shift_zero, 2)
            act.wait_ge(vb_set, 4)
            nc.scalar.copy(warm[:, 0:1], cst("ident", 0, 1)).then_inc(warmed, 1)
            all_turns(act, turn, name_table)

        @block.gpsimd
        def _(pool):
            def residual(t, ahead, s):
                wait(pool, x_ready, t.pairs(ahead, 2, s - 1))
                nc.gpsimd.tensor_tensor(xres[s][:, :], state(t, ahead, s), k.bias_row[:, b_out, :], ALU.add
                                        ).then_inc(xres_ready, 1)

            def inverse_deviation(t, ahead, s):
                pool.wait_ge(vare_ready, t.pairs(ahead, 2, s + 1))
                nc.gpsimd.tensor_tensor(rstd[s][:, :], vare[s][:, :], mhalf[:, :], ALU.pow).then_inc(rstd_ready, 1)

            def round_queries(t):
                if kind == "rope":
                    pool.wait_ge(q_ready, t.pairs(3))
                else:
                    pool.wait_ge(empty["A"], nth("A", "q", t) + 1)
                nc.gpsimd.tensor_tensor(q4_high[t.n % 2][:, :, :], q4[:, :, :],
                                        cst("ones", 0, 1).unsqueeze(2).to_broadcast([P, J, 256]), ALU.mult
                                        ).then_inc(q_high_ready, 1)

            def lower_keys(t):
                p = t.n % 2
                pool.wait_ge(k_high_ready, t.pairs(3))
                nc.gpsimd.tensor_tensor(kg_low[p][:, :, :], kg[:, :, :], kg_high[p][:, :, :].bitcast(F32), ALU.subtract
                                        ).then_inc(k_low_ready, 1)

            def turn(t):
                p, o1 = has(t.n + 2), has(t.n - 1)
                if o1:
                    residual(t, -1, 0)
                    residual(t, -1, 1)
                    inverse_deviation(t, -1, 0)
                    inverse_deviation(t, -1, 1)
                if p:
                    round_queries(t)
                    lower_keys(t)

            nc.gpsimd.memset(kg[:, :, :], 0.0).then_inc(kg_zero, 1)
            if softmax:
                for s in range(2):
                    if kind == "causal":
                        nc.gpsimd.tensor_tensor(shift[s][:, :].rearrange("p (h q) -> p h q", q=P),
                                                cst("causal_kq").unsqueeze(1).to_broadcast([P, H, P]),
                                                cst("ones").unsqueeze(1).to_broadcast([P, H, P]), ALU.mult
                                                ).then_inc(shift_zero, 1)
                    else:
                        nc.gpsimd.memset(shift[s][:, :].bitcast(F32), 0.0).then_inc(shift_zero, 1)
            nc.gpsimd.memset(mhalf[:, :], -0.5).then_inc(half_set, 1)
            pool.wait_ge(half_set, 1)
            all_turns(pool, turn)

        @block.vector
        def _(dve):
            def maxima(t, s):
                for j in range(J):
                    b = "AB"[j % 2]
                    dve.wait_ge(full[b], nth(b, f"m{s}{j}", t) + 1)
                    nc.vector.tensor_reduce(negmax[s][:, j::4], bank[b][:, :].rearrange("p (g t) -> p g t", g=G),
                                            AX.X, ALU.max, negate=True).then_inc(empty[b], 1)

            def take_lat(t):
                dve.wait_ge(full["A"], nth("A", "lat", t) + 1)
                nc.vector.tensor_copy(latT[t.n % 2][0:3 * LAT, :], bank["A"][0:3 * LAT, 0:256]
                                      ).then_inc(empty["A"], 1)

            def lower_queries(t):
                p = (t.n + 1) % 2
                dve.wait_ge(q_high_ready, t.pairs(2))
                nc.vector.tensor_tensor(q4_low[p][:, :, :], q4[:, :, :], q4_high[p][:, :, :].bitcast(F32), ALU.subtract
                                        ).then_inc(q_low_ready, 1)

            def take_q(t):
                wait(dve, q_low_ready, t.pairs(2))
                if kind == "rope":
                    wait(dve, q_ready, t.pairs(2))
                    wait(dve, k_ready, t.pairs(2))
                    dve.wait_ge(full["A"], nth("A", "q", t) + 1)
                    nc.vector.scalar_tensor_tensor(rot[0][:, :], bank["A"][:, 0:256], k.bias_col[:, BQ1:BQ1 + 1],
                                                   cst("cos"), ALU.add, ALU.mult)
                    nc.vector.scalar_tensor_tensor(rot[1][:, :], bank["A"][:, 256:512], k.bias_col[:, BQ1R:BQ1R + 1],
                                                   cst("sin"), ALU.add, ALU.mult).then_inc(empty["A"], 1)
                    dve.wait_ge(full["B"], nth("B", "k", t) + 1)
                    nc.vector.scalar_tensor_tensor(rot[3][:, :], bank["B"][:, 0:256], k.bias_col[:, BK1:BK1 + 1],
                                                   cst("cos"), ALU.add, ALU.mult)
                    nc.vector.scalar_tensor_tensor(rot[4][:, :], bank["B"][:, 256:512], k.bias_col[:, BK1R:BK1R + 1],
                                                   cst("sin"), ALU.add, ALU.mult).then_inc(empty["B"], 1)
                    dve.wait_ge(empty["B"], nth("B", "k", t) + 1)
                    nc.vector.tensor_tensor(rot[2][:, :], rot[0][:, :], rot[1][:, :], ALU.add).then_inc(rotated, 1)
                    nc.vector.tensor_tensor(rot[5][:, :], rot[3][:, :], rot[4][:, :], ALU.add).then_inc(rotated, 1)
                    dve.wait_ge(rotated, t.pairs(3, 2))
                else:
                    dve.wait_ge(full["A"], nth("A", "q", t) + 1)
                for j in range(J):
                    if kind == "sine":
                        ins = nc.vector.tensor_scalar(q4[:, j, :], bank["A"][:, 0:256], k.bias_col[:, BQ0:BQ0 + 1],
                                                      cst("maskc", j, j + 1), ALU.add, ALU.mult)
                    else:
                        ins = nc.vector.tensor_scalar(q4[:, j, :], rot[2][:, :] if kind == "rope" else bank["A"][:, 0:256],
                                                      cst("mask", j, j + 1), None, ALU.mult)
                ins.then_inc(q_ready if kind == "rope" else empty["A"], 1)

            def take_v(t):
                dve.wait_ge(full["C"], nth("C", "v", t) + 1)
                bias = k.bias_row[:, BV0 if kind == "sine" else BV1, :].rearrange("p (g j d) -> p g j d", g=G, j=J)
                for s in range(2):
                    ins = nc.vector.tensor_tensor(value_blocks((t.n + 1) % 2, s), bank["C"][:, s * P:(s + 1) * P]
                                                  .rearrange("p (g j d) -> p g j d", g=G, j=J), bias, ALU.add)
                ins.then_inc(empty["C"], 1)

            def fractions(t, s):
                for half in range(2):
                    dve.wait_ge(rounded[half], t.pairs(0, 2, s + 1))
                    nc.vector.scalar_tensor_tensor(rnd[half][:, :], rnd[half][:, :], -MAGIC, scores[half][:, :],
                                                   ALU.add, ALU.subtract).then_inc(frac_ready[half], 1)

            def normalise(t, s):
                dve.wait_ge(full["D"], nth("D", f"sum{s}", t) + 1)
                nc.vector.reciprocal(recip[s][:, :], bank["D"][:, 256:512]).then_inc(empty["D"], 1)
                dve.wait_ge(empty["D"], nth("D", f"sum{s}", t) + 1)
                nc.vector.tensor_tensor(onorm[s][:, :], osum[s][:, :], recip[s][:, :], ALU.mult).then_inc(onorm_ready, 1)

            def add_residual(t, ahead, s):
                wait(dve, x_ready, t.pairs(ahead, 2, s - 1))
                dve.wait_ge(full["C"], nth("C", f"y{s}", t) + 1)
                dve.wait_ge(xres_ready, t.pairs(ahead, 2, s + 1))
                nc.vector.tensor_tensor(z[s][:, :], bank["C"][:, 0:P], xres[s][:, :], ALU.add).then_inc(empty["C"], 1)
                dve.wait_ge(empty["C"], nth("C", f"y{s}", t) + 1)
                nc.vector.bn_stats(stats[s][:, :], z[s][:, :]).then_inc(stats_ready, 1)
                dve.wait_ge(stats_ready, t.pairs(ahead, 2, s + 1))
                nc.vector.tensor_copy(spare[s][:, :], cst("ident", 0, 1))
                nc.vector.bn_aggr(mv[s][:, :], stats[s][:, :]).then_inc(var_ready, 1)
                dve.wait_ge(var_ready, t.pairs(ahead, 2, s + 1))
                nc.vector.tensor_scalar(vare[s][:, :], mv[s][:, 1:2], EPS, None, ALU.add).then_inc(vare_ready, 1)

            def layer_norm(t, ahead, s):
                dve.wait_ge(rstd_ready, t.pairs(ahead, 2, s + 1))
                nc.vector.tensor_scalar(state(t, ahead, s), z[s][:, :], mv[s][:, 0:1], rstd[s][:, :],
                                        ALU.subtract, ALU.mult).then_inc(x_ready, 1)

            def turn(t):
                p, m, v, o1, o0 = has(t.n + 2), has(t.n + 1) and softmax, has(t.n + 1), has(t.n - 1), has(t.n)
                if v and softmax:
                    lower_queries(t)
                if o0 and not softmax:
                    fractions(t, 0)
                if o1:
                    add_residual(t, -1, 0)
                if v and not softmax:
                    lower_queries(t)
                if m:
                    maxima(t, 0)
                if o1 and softmax:
                    normalise(t, 1)
                if p and kind == "causal":
                    take_lat(t)
                if o1:
                    layer_norm(t, -1, 0)
                if m:
                    maxima(t, 1)
                if o0 and not softmax:
                    fractions(t, 1)
                if o1:
                    add_residual(t, -1, 1)
                if p:
                    take_q(t)
                if o1:
                    layer_norm(t, -1, 1)
                if v and kind != "causal":
                    take_v(t)
                if o0 and softmax:
                    normalise(t, 0)

            for i in range(2):
                for s in range(2):
                    nc.vector.memset(vb[i][s][:, :, :, :], 0.0).then_inc(vb_zero, 1)
            dve.wait_ge(vb_zero, 4)
            for i in range(2):
                for s in range(2):
                    nc.vector.memset(sum_columns(i, s), 1.0).then_inc(vb_set, 1)
            dve.wait_ge(vb_set, 4)
            all_turns(dve, turn)


def channel_attention(k, ctx_in):
    nc = k.nc
    with ExitStack() as ctx:
        sb = lambda n, s, dt=F32: ctx.enter_context(nc.sbuf_tensor(f"channel_{n}", s, dt))
        ps = lambda n: ctx.enter_context(nc.psum_tensor(f"channel_{n}", [P, 512], F32))
        sem = lambda n: k.sem(f"channel_{n}")
        scores, turned_ctx, turned_attn, attended = ps("scores"), ps("turned_ctx"), ps("turned_attn"), ps("attended")
        cin = sb("cin", [P, 2, P])
        qp = sb("qp", [P, 2, 2, P])
        q = sb("q", [P, 2, 2, P])
        kp = sb("kp", [P, 2, 2, P])
        key = sb("key", [P, 2, 2, P])
        vT = sb("vT", [P, 2, 2, P])
        xres = sb("xres", [P, 2, P])
        negmax = sb("negmax", [P, 4])
        shift = sb("shift", [P, 4])
        ex = sb("ex", [P, 4, P])
        sums = sb("sums", [P, 4])
        recip = sb("recip", [P, 4])
        factor = sb("factor", [P, 4])
        attn = sb("attn", [P, 4, P])
        attnT = sb("attnT", [P, 4, P])
        z = sb("z", [P, 2, P])
        stats = sb("stats", [P, 2, 6])
        mv = sb("mv", [P, 2, 2])
        vare = sb("vare", [P, 2])
        rstd = sb("rstd", [P, 2])
        mhalf = sb("mhalf", [P, 2])

        c_loaded = sem("c_loaded")
        qp_ready = sem("qp_ready")
        q_ready = sem("q_ready")
        kp_ready = sem("kp_ready")
        key_ready = sem("key_ready")
        v_ready = sem("v_ready")
        xres_ready = sem("xres_ready")
        ctx_turned = sem("ctx_turned")
        scores_full = sem("scores_full")
        attn_turned = sem("attn_turned")
        out_full = sem("out_full")
        max_ready = sem("max_ready")
        shift_ready = sem("shift_ready")
        ex_ready = sem("ex_ready")
        sums_ready = sem("sums_ready")
        recip_ready = sem("recip_ready")
        factor_ready = sem("factor_ready")
        attn_ready = sem("attn_ready")
        attnT_ready = sem("attnT_ready")
        z_ready = sem("z_ready")
        stats_ready = sem("stats_ready")
        var_ready = sem("var_ready")
        vare_ready = sem("vare_ready")
        rstd_ready = sem("rstd_ready")
        x_ready = sem("x_ready")
        init = sem("init")
        scale = P ** -0.5
        rows = lambda m: k.ch_row[:, m:m + 2, :].unsqueeze(1).to_broadcast([P, 2, 2, P])
        has = lambda pair: not isinstance(pair, int) or 0 <= pair < NPAIR
        seqs = lambda n: slice(n * 2, n * 2 + 2) if isinstance(n, int) else bass.ds(n * 2, 2)
        block = ctx.enter_context(nc.Block())


        def all_turns(engine, turn):
            for n in range(-1, 2):
                turn(n)
            with engine.Fori(2, NPAIR - 1) as n:
                turn(n)
            for n in range(NPAIR - 1, NPAIR + 1):
                turn(n)

        def wait(engine, semaphore, value):
            if not isinstance(value, int) or value > 0:
                engine.wait_ge(semaphore, value)

        @block.sync
        def _(sp):
            def turn(n):
                if has(n + 1):
                    wait(sp, ctx_turned, n + 1)
                    sp.dma_start(cin[:, :, :], ctx_in[seqs(n + 1), :, :].rearrange("b t d -> t b d")
                                 ).then_inc(c_loaded, 16)

            for e in range(E1):
                sp.dma_start(k.dn1[:, e, :, :], k.dram["L1_ffn_w2"][e, :, :].rearrange("(c p) h -> p c h", p=P)
                             ).then_inc(k.loaded_ffn1, 16)
            all_turns(sp, turn)

        @block.tensor
        def _(pe):
            def turn(n):
                if has(n - 1):
                    pe.wait_ge(attn_ready, n)
                    for m in range(4):
                        ins = nc.tensor.transpose(turned_attn[:, m * P:(m + 1) * P], attn[:, m, :], k.c("ident"))
                    ins.then_inc(attn_turned, 1)
                if has(n):
                    pe.wait_ge(q_ready, n + 1)
                    pe.wait_ge(key_ready, n + 1)
                    nc.tensor.matmul(scores[:, :], k.ident_bf[:, :],
                                     k.blocks_bf[:, :].unsqueeze(1).to_broadcast([P, 4, P]), start=True, stop=False)
                    for s in range(2):
                        for m in range(2):
                            ins = nc.tensor.matmul(scores[:, (2 * s + m) * P:(2 * s + m + 1) * P], q[:, s, m, :],
                                                   key[:, s, m, :], start=False, stop=s + m == 2)
                    ins.then_inc(scores_full, 1)
                if has(n - 1):
                    pe.wait_ge(attnT_ready, n)
                    wait(pe, v_ready, n)
                    for s in range(2):
                        for m in range(2):
                            ins = nc.tensor.matmul(attended[:, s * P:(s + 1) * P], vT[:, m, s, :],
                                                   attnT[:, 2 * s + m, :], start=(m == 0), stop=(m == 1))
                    ins.then_inc(out_full, 1)
                if has(n + 1):
                    wait(pe, v_ready, n + 1)
                    pe.wait_ge(key_ready, n + 2)
                    pe.wait_ge(c_loaded, n * 16 + 32)
                    for s in range(2):
                        ins = nc.tensor.transpose(turned_ctx[:, s * P:(s + 1) * P], cin[:, s, :], k.c("ident"))
                    ins.then_inc(ctx_turned, 1)

            all_turns(pe, turn)

        @block.scalar
        def _(act):
            def turn(n):
                if has(n - 1):
                    act.wait_ge(attn_turned, n)
                    nc.scalar.copy(attnT[:, :, :].rearrange("p n d -> p (n d)"), turned_attn[:, :]
                                   ).then_inc(attnT_ready, 1)
                if has(n):
                    act.wait_ge(shift_ready, n + 1)
                    for m in range(4):
                        ins = nc.scalar.activation(ex[:, m, :], scores[:, m * P:(m + 1) * P], ACT.Exp,
                                                   bias=shift[:, m:m + 1], scale=scale)
                    ins.then_inc(ex_ready, 1)
                    act.wait_ge(ctx_turned, n + 1)
                    wait(act, out_full, n)
                    for m in range(2):
                        ins = nc.scalar.activation(vT[:, m, :, :].rearrange("p s t -> p (s t)"), turned_ctx[:, 0:256],
                                                   ACT.Identity, bias=k.ch_col[:, BV + m:BV + m + 1],
                                                   scale=k.ch_col[:, WV + m:WV + m + 1])
                    ins.then_inc(v_ready, 1)

            act.wait_ge(k.loaded_channel, N_CHANNEL)
            all_turns(act, turn)

        @block.gpsimd
        def _(pool):
            def turn(n):
                if has(n - 1):
                    wait(pool, z_ready, n - 1)
                    nc.gpsimd.tensor_tensor(xres[:, :, :], k.x[:, seqs(n - 1), :],
                                            k.ch_row[:, BP:BP + 1, :].to_broadcast([P, 2, P]), ALU.add
                                            ).then_inc(xres_ready, 1)
                if has(n + 1):
                    pool.wait_ge(c_loaded, n * 16 + 32)
                    nc.gpsimd.tensor_tensor(kp[:, :, :, :], cin[:, :, :].unsqueeze(2).to_broadcast([P, 2, 2, P]),
                                            rows(WK), ALU.mult).then_inc(kp_ready, 1)
                    pool.wait_ge(kp_ready, n + 2)
                    wait(pool, scores_full, n + 1)
                    nc.gpsimd.tensor_tensor(key[:, :, :, :], kp[:, :, :, :], rows(BK), ALU.add).then_inc(key_ready, 1)
                if has(n - 1):
                    pool.wait_ge(vare_ready, n)
                    nc.gpsimd.tensor_tensor(rstd[:, :], vare[:, :], mhalf[:, :], ALU.pow).then_inc(rstd_ready, 1)

            nc.gpsimd.memset(mhalf[:, :], -0.5).then_inc(init, 1)
            pool.wait_ge(init, 1)
            pool.wait_ge(k.loaded_channel, N_CHANNEL)
            all_turns(pool, turn)

        @block.vector
        def _(dve):
            def turn(n):
                if has(n):
                    dve.wait_ge(scores_full, n + 1)
                    nc.vector.tensor_reduce(negmax[:, :], scores[:, :].rearrange("p (n e) -> p n e", n=4), AX.X,
                                            ALU.max, negate=True).then_inc(max_ready, 1)
                    dve.wait_ge(max_ready, n + 1)
                    nc.vector.tensor_scalar(shift[:, :], negmax[:, :], scale, None, ALU.mult).then_inc(shift_ready, 1)
                if has(n + 1):
                    nc.vector.tensor_tensor(qp[:, :, :, :], k.x[:, seqs(n + 1), :].unsqueeze(2)
                                            .to_broadcast([P, 2, 2, P]), rows(WQ), ALU.mult).then_inc(qp_ready, 1)
                if has(n - 1):
                    dve.wait_ge(out_full, n)
                    dve.wait_ge(xres_ready, n)
                    wait(dve, x_ready, n - 1)
                    nc.vector.tensor_tensor(z[:, :, :], attended[:, 0:256].rearrange("p (s d) -> p s d", s=2),
                                            xres[:, :, :], ALU.add).then_inc(z_ready, 1)
                    dve.wait_ge(z_ready, n)
                    for s in range(2):
                        ins = nc.vector.bn_stats(stats[:, s, :], z[:, s, :])
                    ins.then_inc(stats_ready, 1)
                if has(n):
                    dve.wait_ge(ex_ready, n + 1)
                    nc.vector.tensor_reduce(sums[:, :], ex[:, :, :], AX.X, ALU.add).then_inc(sums_ready, 1)
                    dve.wait_ge(sums_ready, n + 1)
                    nc.vector.reciprocal(recip[:, :], sums[:, :]).then_inc(recip_ready, 1)
                    dve.wait_ge(recip_ready, n + 1)
                    nc.vector.scalar_tensor_tensor(factor[:, :], recip[:, :], 2.0,
                                                   k.ch_col[:, WP:WP + 1].to_broadcast([P, 4]),
                                                   ALU.mult, ALU.mult).then_inc(factor_ready, 1)
                    dve.wait_ge(factor_ready, n + 1)
                    nc.vector.tensor_tensor(attn[:, :, :], ex[:, :, :],
                                            factor[:, :].unsqueeze(2).to_broadcast([P, 4, P]), ALU.mult
                                            ).then_inc(attn_ready, 1)
                if has(n - 1):
                    dve.wait_ge(stats_ready, n)
                if has(n + 1):
                    dve.wait_ge(qp_ready, n + 2)
                    nc.vector.tensor_tensor(q[:, :, :, :], qp[:, :, :, :], rows(BQ), ALU.add).then_inc(q_ready, 1)
                if has(n - 1):
                    for s in range(2):
                        ins = nc.vector.bn_aggr(mv[:, s, :], stats[:, s, :])
                    ins.then_inc(var_ready, 1)
                    dve.wait_ge(var_ready, n)
                    nc.vector.tensor_scalar(vare[:, :], mv[:, :, 1], EPS, None, ALU.add).then_inc(vare_ready, 1)
                    dve.wait_ge(rstd_ready, n)
                    for s in range(2):
                        at = (n - 1) * 2 + s
                        dst = k.x[:, at:at + 1, :] if isinstance(at, int) else k.x[:, bass.ds(at, 1), :]
                        ins = nc.vector.tensor_scalar(dst.rearrange("p o d -> p (o d)"), z[:, s, :], mv[:, s, 0:1],
                                                      rstd[:, s:s + 1], ALU.subtract, ALU.mult)
                    ins.then_inc(x_ready, 1)

            dve.wait_ge(k.loaded_channel, N_CHANNEL)
            all_turns(dve, turn)


def experts(k, layer):
    nc = k.nc
    tag = f"moe{layer}"
    NE, NX = (E0, E0 + 1) if layer == 0 else (E1, E1)
    router, bias = (k.wr0, k.rb0) if layer == 0 else (k.gate_w, k.gate_b)
    dn, W = (k.dn0, W0) if layer == 0 else (k.dn1, I1)
    NC = W // P
    NG = NB // 4
    with ExitStack() as outer:
        sb = lambda n, s, dt=F32: outer.enter_context(nc.sbuf_tensor(f"{tag}_{n}", s, dt))
        sem = lambda n: k.sem(f"{tag}_{n}")
        x_high = sb("x_high", [P, NB * P], F32R)
        x_low = sb("x_low", [P, NB * P], F32R)
        gu_high = sb("gu_high", [P, NX, 2 * W], F32R)
        gu_low = sb("gu_low", [P, NX, 2 * W], F32R)
        weight = sb("weight", [P, NB, NX])
        credit = sb("credit", [P, 1])

        with ExitStack() as ctx:
            xT = [ctx.enter_context(nc.sbuf_tensor(f"{tag}_xT{b}", [P, 512], F32)) for b in range(2)]
            if layer == 1:
                whole = [ctx.enter_context(nc.sbuf_tensor(f"{tag}_whole{b}", [P, 2 * W], F32)) for b in range(2)]
            else:
                whole = None
            part = lambda n: ctx.enter_context(nc.sbuf_tensor(f"{tag}_{n}", [P, NB, NE], F32))
            line = lambda n: ctx.enter_context(nc.sbuf_tensor(f"{tag}_{n}", [P, NB], F32))
            logits, equal1, place1, first, rest, equal2, place2, second, w_first, w_second = (
                part(n) for n in ("logits", "equal1", "place1", "first", "rest", "equal2", "place2", "second",
                                  "w_first", "w_second"))
            max1, at1, max2, at2, gap, ratio, total, w1, w2 = (
                line(n) for n in ("max1", "at1", "max2", "at2", "gap", "ratio", "total", "w1", "w2"))
            turned = [ctx.enter_context(nc.psum_tensor(f"{tag}_turned{b}", [P, 512], F32)) for b in range(2)]
            scored = [ctx.enter_context(nc.psum_tensor(f"{tag}_scored{b}", [P, 4, NE], F32)) for b in range(2)]
            turned_full = [sem(f"turned_full{b}") for b in range(2)]
            xT_ready = [sem(f"xT_ready{b}") for b in range(2)]
            high_ready = [sem(f"high_ready{b}") for b in range(2)]
            low_ready = sem("low_ready")
            whole_loaded = [sem(f"whole_loaded{b}") for b in range(2)]
            gu_low_ready = sem("gu_low_ready")
            source = lambda e: k.gu0[:, e, :] if layer == 0 else whole[e % 2][:, :]
            gu_high_ready = sem("gu_high_ready")
            scored_full = [sem(f"scored_full{b}") for b in range(2)]
            logits_ready = sem("logits_ready")
            gap_ready = sem("gap_ready")
            ratio_ready = sem("ratio_ready")
            step = sem("step")
            block = ctx.enter_context(nc.Block())

            @block.sync
            def _(sp):
                if layer == 1:
                    for g in range(NX):
                        b = g % 2
                        if g >= 2:
                            sp.wait_ge(gu_low_ready, g - 1)
                        sp.dma_start(whole[b][:, 0:W], k.dram["L1_ffn_w1"][g, :, :]).then_inc(whole_loaded[b], 16)
                        sp.dma_start(whole[b][:, W:], k.dram["L1_ffn_w3"][g, :, :]).then_inc(whole_loaded[b], 16)

            @block.tensor
            def _(pe):
                def transposes(g):
                    b = g % 2
                    if g >= 2:
                        pe.wait_ge(high_ready[b], g // 2)
                    for t in range(4):
                        ins = nc.tensor.transpose(turned[b][:, t * P:(t + 1) * P], k.x[:, 4 * g + t, :], k.c("ident"))
                    ins.then_inc(turned_full[b], 1)

                transposes(0)
                for g in range(NG):
                    b = g % 2
                    if g + 1 < NG:
                        transposes(g + 1)
                    pe.wait_ge(xT_ready[b], g // 2 + 1)
                    if g >= 2:
                        pe.wait_ge(logits_ready, g - 1)
                    for t in range(4):
                        ins = nc.tensor.matmul(scored[b][:, t, :], xT[b][:, t * P:(t + 1) * P], router[:, :],
                                               start=True, stop=True)
                    ins.then_inc(scored_full[b], 1)

            @block.gpsimd
            def _(pool):
                unit = k.c("ones", 0, 1).to_broadcast([P, 2 * W])
                for e in range(NX):
                    if layer == 1:
                        pool.wait_ge(whole_loaded[e % 2], 32 * (e // 2 + 1))
                    nc.gpsimd.tensor_tensor(gu_high[:, e, :], source(e), unit, ALU.mult).then_inc(gu_high_ready, 1)

            @block.scalar
            def _(act):
                for g in range(NG):
                    b = g % 2
                    act.wait_ge(turned_full[b], g // 2 + 1)
                    if g >= 2:
                        act.wait_ge(scored_full[b], g // 2)
                        act.wait_ge(low_ready, g - 1)
                    nc.scalar.copy(xT[b][:, :], turned[b][:, :]).then_inc(xT_ready[b], 1)
                    nc.scalar.copy(x_high[:, g * 512:(g + 1) * 512], turned[b][:, :]).then_inc(high_ready[b], 1)
                act.wait_ge(gap_ready, 1)
                nc.scalar.activation(ratio[:, :], gap[:, :], ACT.Exp).then_inc(ratio_ready, 1)

            @block.vector
            def _(dve):
                for g in range(NG):
                    dve.wait_ge(scored_full[g % 2], g // 2 + 1)
                    nc.vector.tensor_tensor(logits[:, 4 * g:4 * g + 4, :], scored[g % 2][:, :, :],
                                            bias[:, :].unsqueeze(1).to_broadcast([P, 4, NE]), ALU.add
                                            ).then_inc(logits_ready, 1)
                    at = slice(g * 512, (g + 1) * 512)
                    dve.wait_ge(high_ready[g % 2], g // 2 + 1)
                    nc.vector.tensor_tensor(x_low[:, at], xT[g % 2][:, :], x_high[:, at].bitcast(F32), ALU.subtract
                                            ).then_inc(low_ready, 1)
                    if g < NX:
                        dve.wait_ge(gu_high_ready, g + 1)
                        nc.vector.tensor_tensor(gu_low[:, g, :], source(g), gu_high[:, g, :].bitcast(F32),
                                                ALU.subtract).then_inc(gu_low_ready, 1)
                over = lambda a: a[:, :].unsqueeze(2).to_broadcast([P, NB, NE])
                index = k.c("eidx", 0, NE).unsqueeze(1).to_broadcast([P, NB, NE])
                dve.wait_ge(logits_ready, NG)
                nc.vector.tensor_reduce(max1[:, :], logits[:, :, :], AX.X, ALU.max).then_inc(step, 1)
                dve.wait_ge(step, 1)
                nc.vector.tensor_tensor(equal1[:, :, :], logits[:, :, :], over(max1), ALU.is_equal).then_inc(step, 1)
                dve.wait_ge(step, 2)
                nc.vector.scalar_tensor_tensor(place1[:, :, :], equal1[:, :, :], -64.0, index, ALU.mult, ALU.add
                                               ).then_inc(step, 1)
                dve.wait_ge(step, 3)
                nc.vector.tensor_reduce(at1[:, :], place1[:, :, :], AX.X, ALU.min).then_inc(step, 1)
                dve.wait_ge(step, 4)
                nc.vector.tensor_tensor(first[:, :, :], place1[:, :, :], over(at1), ALU.is_equal).then_inc(step, 1)
                dve.wait_ge(step, 5)
                nc.vector.scalar_tensor_tensor(rest[:, :, :], first[:, :, :], NEG, logits[:, :, :], ALU.mult, ALU.add
                                               ).then_inc(step, 1)
                dve.wait_ge(step, 6)
                nc.vector.tensor_reduce(max2[:, :], rest[:, :, :], AX.X, ALU.max).then_inc(step, 1)
                dve.wait_ge(step, 7)
                nc.vector.tensor_tensor(gap[:, :], max2[:, :], max1[:, :], ALU.subtract).then_inc(gap_ready, 1)
                nc.vector.tensor_tensor(equal2[:, :, :], rest[:, :, :], over(max2), ALU.is_equal).then_inc(step, 1)
                dve.wait_ge(step, 8)
                nc.vector.scalar_tensor_tensor(place2[:, :, :], equal2[:, :, :], -64.0, index, ALU.mult, ALU.add
                                               ).then_inc(step, 1)
                dve.wait_ge(step, 9)
                nc.vector.tensor_reduce(at2[:, :], place2[:, :, :], AX.X, ALU.min).then_inc(step, 1)
                dve.wait_ge(step, 10)
                nc.vector.tensor_tensor(second[:, :, :], place2[:, :, :], over(at2), ALU.is_equal).then_inc(step, 1)
                dve.wait_ge(ratio_ready, 1)
                nc.vector.tensor_scalar(total[:, :], ratio[:, :], 1.0, None, ALU.add).then_inc(step, 1)
                dve.wait_ge(step, 12)
                nc.vector.reciprocal(w1[:, :], total[:, :]).then_inc(step, 1)
                dve.wait_ge(step, 13)
                nc.vector.tensor_tensor(w2[:, :], ratio[:, :], w1[:, :], ALU.mult).then_inc(step, 1)
                nc.vector.tensor_tensor(w_first[:, :, :], first[:, :, :], over(w1), ALU.mult).then_inc(step, 1)
                dve.wait_ge(step, 14)
                nc.vector.tensor_tensor(w_second[:, :, :], second[:, :, :], over(w2), ALU.mult).then_inc(step, 1)
                dve.wait_ge(step, 16)
                if NX > NE:
                    nc.vector.memset(weight[:, :, NE:], 1.0)
                nc.vector.tensor_tensor(weight[:, :, 0:NE], w_first[:, :, :], w_second[:, :, :], ALU.add
                                        ).then_inc(step, 1)

        with ExitStack() as ctx:
            buf = lambda n, s: ctx.enter_context(nc.sbuf_tensor(f"{tag}_{n}", s, F32))
            ps = lambda n: ctx.enter_context(nc.psum_tensor(f"{tag}_{n}", [P, 512], F32))
            gate, up, down = ([ps(f"{n}{b}") for b in range(2)] for n in ("gate", "up", "down"))
            silu = [buf(f"silu{b}", [P, 512]) for b in range(2)]
            hidden = [buf(f"hidden{b}", [P, NC, 512]) for b in range(2)]
            w_group = buf("w_group", [P, 4, NX])
            acc = buf("acc", [P, 4, P])
            stats = buf("stats", [P, 4, 6])
            mv = buf("mv", [P, 4, 2])
            vare = buf("vare", [P, 4])
            rstd = buf("rstd", [P, 4])
            mhalf = buf("mhalf", [P, 4])
            up_full = [sem(f"up_full{b}") for b in range(2)]
            silu_ready = [sem(f"silu_ready{b}") for b in range(2)]
            hidden_ready = sem("hidden_ready")
            down_full = sem("down_full")
            acc_ready = sem("acc_ready")
            w_ready = sem("w_ready")
            stats_ready = sem("stats_ready")
            var_ready = sem("var_ready")
            vare_ready = sem("vare_ready")
            rstd_ready = sem("rstd_ready")
            x_ready = sem("x_ready")
            init = sem("init")
            N = NX * NC
            block = ctx.enter_context(nc.Block())

            tiles_after = [(0, 1), (2,), (3,)] if NC == 3 else [(0,), (1,), (2,), (3,)]

            @block.tensor
            def _(pe):
                def go_up(g, e, c):
                    n = e * NC + c
                    b = n % 2
                    pe.wait_ge(hidden_ready, g * N + (n + 1))
                    cols = slice(g * 512, g * 512 + 512) if isinstance(g, int) else bass.ds(g * 512, 512)
                    high, low = x_high[:, cols], x_low[:, cols]
                    for dst, at in ((gate[b], c * P), (up[b], W + c * P)):
                        nc.tensor.matmul(dst[:, :], gu_high[:, e, at:at + P], high, start=True, stop=False)
                        nc.tensor.matmul(dst[:, :], gu_high[:, e, at:at + P], low, start=False, stop=False)
                        ins = nc.tensor.matmul(dst[:, :], gu_low[:, e, at:at + P], high, start=False, stop=True)
                    ins.then_inc(up_full[b], 1)

                def go_down(g, e, t):
                    if t == 0:
                        pe.wait_ge(hidden_ready, g * N + ((e + 1) * NC + 2))
                    for c in range(NC):
                        ins = nc.tensor.matmul(down[e % 2][:, t * P:(t + 1) * P],
                                               hidden[e % 2][:, c, t * P:(t + 1) * P], dn[:, e, c, :],
                                               start=(c == 0), stop=(c == NC - 1))
                    if t == 3:
                        ins.then_inc(down_full, 1)

                def turn(g, last):
                    for e in range(1, NX):
                        for c in range(NC):
                            go_up(g, e, c)
                            for t in tiles_after[c]:
                                go_down(g, e - 1, t)
                    if not last:
                        go_up(g + 1, 0, 0)
                    for t in range(4):
                        go_down(g, NX - 1, t)
                    if not last:
                        for c in range(1, NC):
                            go_up(g + 1, 0, c)

                if layer == 1:
                    pe.wait_ge(k.loaded_ffn1, N_FFN1)
                for c in range(NC):
                    go_up(0, 0, c)
                with pe.Fori(0, NG - 1) as g:
                    turn(g, False)
                turn(NG - 1, True)

            @block.scalar
            def _(act):
                def gates(g, e):
                    for c in range(NC):
                        n = e * NC + c
                        b = n % 2
                        act.wait_ge(up_full[b], g * (N // 2) + (n // 2 + 1))
                        nc.scalar.activation(silu[b][:, :], gate[b][:, :], ACT.Silu).then_inc(silu_ready[b], 1)

                gates(0, 0)
                with act.Fori(0, NG - 1) as g:
                    for e in range(1, NX):
                        gates(g, e)
                    gates(g + 1, 0)
                for e in range(1, NX):
                    gates(NG - 1, e)

            @block.gpsimd
            def _(pool):
                nc.gpsimd.memset(mhalf[:, :], -0.5).then_inc(init, 1)
                pool.wait_ge(init, 1)
                with pool.Fori(0, NG) as g:
                    pool.wait_ge(vare_ready, g + 1)
                    nc.gpsimd.tensor_tensor(rstd[:, :], vare[:, :], mhalf[:, :], ALU.pow).then_inc(rstd_ready, 1)

            @block.vector
            def _(dve):
                def join(g, e, c):
                    n = e * NC + c
                    dve.wait_ge(silu_ready[n % 2], g * (N // 2) + (n // 2 + 1))
                    nc.vector.tensor_tensor(hidden[e % 2][:, c, :], silu[n % 2][:, :], up[n % 2][:, :], ALU.mult
                                            ).then_inc(hidden_ready, 1)

                def add_up(g, e):
                    dve.wait_ge(down_full, g * NX + (e + 1))
                    dve.wait_ge(w_ready, g + 1) if e == 0 else dve.wait_ge(acc_ready, g * NX + e)
                    for t in range(4):
                        ins = nc.vector.scalar_tensor_tensor(acc[:, t, :], down[e % 2][:, t * P:(t + 1) * P],
                                                             w_group[:, t, e:e + 1],
                                                             state(g, t) if e == 0 else acc[:, t, :], ALU.mult, ALU.add)
                    ins.then_inc(acc_ready, 1)

                def state(g, t):
                    at = g * 4 + t
                    rows = k.x[:, at:at + 1, :] if isinstance(at, int) else k.x[:, bass.ds(at, 1), :]
                    return rows.rearrange("p o d -> p (o d)")

                def take_weights(g):
                    tiles = slice(0, 4) if isinstance(g, int) else bass.ds(g * 4, 4)
                    nc.vector.tensor_copy(w_group[:, :, :], weight[:, tiles, :]).then_inc(w_ready, 1)

                def turn(g, last):
                    for e in range(1, NX):
                        for c in range(NC):
                            join(g, e, c)
                        add_up(g, e - 1)
                    if not last:
                        join(g + 1, 0, 0)
                    add_up(g, NX - 1)
                    dve.wait_ge(acc_ready, g * NX + NX)
                    for t in range(4):
                        ins = nc.vector.bn_stats(stats[:, t, :], acc[:, t, :])
                    ins.then_inc(stats_ready, 1)
                    dve.wait_ge(stats_ready, g + 1)
                    if not last:
                        join(g + 1, 0, 1)
                    for t in range(4):
                        ins = nc.vector.bn_aggr(mv[:, t, :], stats[:, t, :])
                    ins.then_inc(var_ready, 1)
                    dve.wait_ge(var_ready, g + 1)
                    nc.vector.tensor_scalar(vare[:, :], mv[:, :, 1], EPS, None, ALU.add).then_inc(vare_ready, 1)
                    if not last:
                        for c in range(2, NC):
                            join(g + 1, 0, c)
                    dve.wait_ge(rstd_ready, g + 1)
                    for t in range(4):
                        ins = nc.vector.tensor_scalar(state(g, t), acc[:, t, :], mv[:, t, 0:1], rstd[:, t:t + 1],
                                                      ALU.subtract, ALU.mult)
                    ins.then_inc(x_ready, 1)
                    if not last:
                        dve.wait_ge(x_ready, g + 1)
                        take_weights(g + 1)

                nc.vector.tensor_copy(credit[:, 0:1], k.c("ident", 0, 1)).then_inc(hidden_ready, 2)
                take_weights(0)
                for c in range(NC):
                    join(0, 0, c)
                with dve.Fori(0, NG - 1) as g:
                    turn(g, False)
                turn(NG - 1, True)


def write_state(k, out):
    nc = k.nc
    with ExitStack() as ctx:
        stored = k.sem("stored")
        block = ctx.enter_context(nc.Block())

        @block.sync
        def _(sp):
            for n in range(4):
                sp.dma_start(out[8 * n:8 * n + 8, :, :].rearrange("b t d -> t b d"), k.x[:, 8 * n:8 * n + 8, :]
                             ).then_inc(stored, 16)
            sp.wait_ge(stored, 64)


def program(nc, d, out):
    with ExitStack() as ctx:
        k = Core(nc, ctx, d)
        with ExitStack() as layer0:
            k.place_experts0(layer0)
            setup(k, d)
            with nc.cleanup_on_exit():
                head_attention(k, "sine", None)
            with nc.cleanup_on_exit():
                head_attention(k, "rope", d["ctx_1024"])
            with nc.cleanup_on_exit():
                experts(k, 0)
        with nc.cleanup_on_exit():
            head_attention(k, "causal", None)
        k.place_experts1()
        with nc.cleanup_on_exit():
            channel_attention(k, d["ctx_1024"])
        with nc.cleanup_on_exit():
            experts(k, 1)
        write_state(k, out)


NAMES = ["x", "ctx_1024",
         "L0_attn_Wq", "L0_attn_bq", "L0_attn_Wk", "L0_attn_bk", "L0_attn_Wv", "L0_attn_bv", "L0_attn_Wo", "L0_attn_bo",
         "L0_xattn_Wq", "L0_xattn_bq", "L0_xattn_Wk", "L0_xattn_bk", "L0_xattn_Wv", "L0_xattn_bv", "L0_xattn_Wo",
         "L0_xattn_bo", "L0_ffn_sg", "L0_ffn_su", "L0_ffn_sd", "L0_ffn_rg", "L0_ffn_ru", "L0_ffn_rd", "L0_ffn_wr",
         "L0_ffn_rb", "L1_attn_wq_lat", "L1_attn_wk_lat", "L1_attn_wv_lat", "L1_attn_wq_heads", "L1_attn_wk_heads",
         "L1_attn_wv_heads", "L1_attn_w_proj", "L1_attn_b_proj",
         "L1_xattn_wqg", "L1_xattn_bqg", "L1_xattn_wkg", "L1_xattn_bkg", "L1_xattn_wvg", "L1_xattn_bvg",
         "L1_xattn_wql", "L1_xattn_bql", "L1_xattn_wkl", "L1_xattn_bkl", "L1_xattn_wvl", "L1_xattn_bvl",
         "L1_xattn_wp", "L1_xattn_bp", "L1_ffn_gate_w", "L1_ffn_gate_b", "L1_ffn_w1", "L1_ffn_w3", "L1_ffn_w2"]


def kernel(**inputs):
    import concourse.bacc as bacc
    from concourse.bass_utils import run_bass_kernel_spmd

    nc = bacc.Bacc("TRN2", target_bir_lowering=False, num_devices=1)
    arrays = {n: np.ascontiguousarray(inputs[n]) for n in NAMES}
    arrays["const"] = constants()
    drams = {n: nc.dram_tensor("in_" + n, a.shape, mybir.dt.from_np(a.dtype), kind="ExternalInput").ap()
             for n, a in arrays.items()}
    out = nc.dram_tensor("out", (NB, P, P), F32, kind="ExternalOutput").ap()
    program(nc, drams, out)
    r = run_bass_kernel_spmd(nc, [{"in_" + n: a for n, a in arrays.items()}], core_ids=[0])
    return r.results[0]["out"]
```
